# Optimizing a Trainium2 kernel written in Bass

```python
import numpy as np
import jax
import jax.numpy as jnp

def _softmax(x, axis=-1):
    return jax.nn.softmax(x, axis=axis)

def _gelu(x):
    return jax.nn.gelu(x, approximate=True)

def _silu(x):
    return jax.nn.silu(x)

def _sigmoid(x):
    return jax.nn.sigmoid(x)

def _layernorm(x, axis=-1, eps=1e-05):
    m = jnp.mean(x, axis=axis, keepdims=True)
    v = jnp.var(x, axis=axis, keepdims=True)
    return (x - m) / jnp.sqrt(v + eps)

def _scatter_add(tgt, idx, src, axis=0):
    return tgt.at[idx].add(src)

def _segment_sum(src, seg, n):
    return jax.ops.segment_sum(src, seg, n)
kernel_name = 'mk_gnn_preln_d2_gnn_r8_3670ba'

def setup_inputs(seed: int=0):
    np.random.seed(seed)
    _w = jnp.asarray

    def _rec_inputs():
        import jax
        import jax.numpy as jnp
        _gk = jax.random.key(seed)
        x = -0.000202 + 1 * jax.random.normal(jax.random.fold_in(_gk, 1), (6250, 128), jnp.float32)
        src = jax.random.randint(jax.random.fold_in(_gk, 2), (200000,), 0, 6250, jnp.int32)
        dst = jnp.minimum((6250 * jax.random.uniform(jax.random.fold_in(_gk, 3), (200000,)) ** 2.0).astype(jnp.int32), 49999)
        _o = jnp.argsort(dst, stable=True)
        src = src[_o]
        dst = dst[_o]
        edge_type_8 = jax.random.randint(jax.random.fold_in(_gk, 13), (200000,), 0, 8, jnp.int32)
        return (x, src, dst, edge_type_8)
    x, src, dst, edge_type_8 = _rec_inputs()

    def _L0_gnn_setup():
        import jax, jax.numpy as jnp
        import numpy as np
        N, E, F, H, L = (6250, 75000, 128, 128, 5)
        key = jax.random.key(seed)
        ks = jax.random.split(key, 16)
        s = 1.0 / np.sqrt(H)
        u = lambda k, shape: jax.random.uniform(k, shape, jnp.float32, -s, s)
        return {'x': jax.random.normal(ks[0], (N, F), jnp.float32), 'edge_index': jax.random.randint(ks[1], (2, E), 0, N, jnp.int64), 'enc_w1': u(ks[2], (H, F)), 'enc_b1': u(ks[3], (H,)), 'enc_w2': u(ks[4], (H, H)), 'enc_b2': u(ks[5], (H,)), 'conv_w': u(ks[6], (L, H, H)), 'gru_wih': u(ks[7], (3 * H, H)), 'gru_whh': u(ks[8], (3 * H, H)), 'gru_bih': u(ks[9], (3 * H,)), 'gru_bhh': u(ks[10], (3 * H,)), 'dec_w1': u(ks[11], (H, H)), 'dec_b1': u(ks[12], (H,)), 'dec_w2': u(ks[13], (F, H)), 'dec_b2': u(ks[14], (F,))}
    _L0_gnn_all = _L0_gnn_setup()
    _L0_gnn_in = {k: v for k, v in _L0_gnn_all.items() if k in ('enc_w1', 'enc_b1', 'enc_w2', 'enc_b2', 'conv_w', 'gru_wih', 'gru_whh', 'gru_bih', 'gru_bhh', 'dec_w1', 'dec_b1', 'dec_w2', 'dec_b2')}
    del _L0_gnn_all

    def _L1_gnn_setup():
        import jax, jax.numpy as jnp
        import numpy as np
        N_NODES = 6250
        N_EDGES = 100000
        IN_FEAT = 128
        OUT_FEAT = 128
        NUM_RELS = 8
        key = jax.random.key(seed)
        k_h, k_w, k_b, k_s, k_d, k_r = jax.random.split(key, 6)
        return {'h': jax.random.normal(k_h, (N_NODES, IN_FEAT), dtype=jnp.float32), 'weight': jax.random.normal(k_w, (NUM_RELS + 1, IN_FEAT, OUT_FEAT), dtype=jnp.float32) * (1.0 / np.sqrt(IN_FEAT)), 'bias': jax.random.normal(k_b, (NUM_RELS + 1, OUT_FEAT), dtype=jnp.float32) * 0.02, 'src': jax.random.randint(k_s, (N_EDGES,), 0, N_NODES, dtype=jnp.int32), 'dst': jax.random.randint(k_d, (N_EDGES,), 0, N_NODES, dtype=jnp.int32), 'rel': jax.random.randint(k_r, (N_EDGES,), 0, NUM_RELS, dtype=jnp.int32)}
    _L1_gnn_all = _L1_gnn_setup()
    _L1_gnn_in = {k: v for k, v in _L1_gnn_all.items() if k in ('weight', 'bias')}
    del _L1_gnn_all
    return {'x': x, 'src': src, 'dst': dst, 'edge_type_8': edge_type_8, 'L0_gnn_enc_w1': _L0_gnn_in['enc_w1'], 'L0_gnn_enc_b1': _L0_gnn_in['enc_b1'], 'L0_gnn_enc_w2': _L0_gnn_in['enc_w2'], 'L0_gnn_enc_b2': _L0_gnn_in['enc_b2'], 'L0_gnn_conv_w': _L0_gnn_in['conv_w'], 'L0_gnn_gru_wih': _L0_gnn_in['gru_wih'], 'L0_gnn_gru_whh': _L0_gnn_in['gru_whh'], 'L0_gnn_gru_bih': _L0_gnn_in['gru_bih'], 'L0_gnn_gru_bhh': _L0_gnn_in['gru_bhh'], 'L0_gnn_dec_w1': _L0_gnn_in['dec_w1'], 'L0_gnn_dec_b1': _L0_gnn_in['dec_b1'], 'L0_gnn_dec_w2': _L0_gnn_in['dec_w2'], 'L0_gnn_dec_b2': _L0_gnn_in['dec_b2'], 'L1_gnn_weight': _L1_gnn_in['weight'], 'L1_gnn_bias': _L1_gnn_in['bias']}

def reference(x, src, dst, edge_type_8, L0_gnn_enc_w1, L0_gnn_enc_b1, L0_gnn_enc_w2, L0_gnn_enc_b2, L0_gnn_conv_w, L0_gnn_gru_wih, L0_gnn_gru_whh, L0_gnn_gru_bih, L0_gnn_gru_bhh, L0_gnn_dec_w1, L0_gnn_dec_b1, L0_gnn_dec_w2, L0_gnn_dec_b2, L1_gnn_weight, L1_gnn_bias):
    import jax
    import jax.numpy as jnp

    def _L0_gnn_ref(x, edge_index, enc_w1, enc_b1, enc_w2, enc_b2, conv_w, gru_wih, gru_whh, gru_bih, gru_bhh, dec_w1, dec_b1, dec_w2, dec_b2):
        import jax, jax.numpy as jnp
        import numpy as np
        N, E, F, H, L = (6250, 75000, 128, 128, 5)
        src, dst = (edge_index[0], edge_index[1])
        n_nodes = x.shape[0]
        h = jnp.maximum(x @ enc_w1.T + enc_b1, 0.0) @ enc_w2.T + enc_b2

        def step(h, w):
            m = h @ w
            agg = jax.ops.segment_sum(m[src], dst, num_segments=n_nodes)
            gi = agg @ gru_wih.T + gru_bih
            gh = h @ gru_whh.T + gru_bhh
            ir, iz, i_n = jnp.split(gi, 3, axis=1)
            hr, hz, h_n = jnp.split(gh, 3, axis=1)
            r = jax.nn.sigmoid(ir + hr)
            z = jax.nn.sigmoid(iz + hz)
            n = jnp.tanh(i_n + r * h_n)
            return ((1.0 - z) * n + z * h, None)
        h, _ = jax.lax.scan(step, h, conv_w)
        h = jnp.maximum(h, 0.0)
        out = jnp.maximum(h @ dec_w1.T + dec_b1, 0.0) @ dec_w2.T + dec_b2
        return jax.nn.sigmoid(out)

    def _L1_gnn_ref(h, weight, bias, src, dst, rel):
        import jax, jax.numpy as jnp
        import numpy as np
        N_NODES = 6250
        N_EDGES = 100000
        IN_FEAT = 128
        OUT_FEAT = 128
        NUM_RELS = 8
        n = h.shape[0]
        hw = jnp.einsum('ni,rio->rno', h, weight)
        msg = hw[rel, src] + bias[rel]
        agg = jax.ops.segment_max(msg, dst, num_segments=n)
        in_deg = jax.ops.segment_sum(jnp.ones((msg.shape[0],), dtype=jnp.int32), dst, num_segments=n)
        agg = jnp.where((in_deg > 0)[:, None], agg, 0.0)
        out = hw[-1] + agg + bias[-1]
        return jax.nn.relu(out)
    edge_index = jnp.stack([src, dst])
    h = jnp.maximum(_layernorm(x, axis=-1), 0.0)
    x = x + _L0_gnn_ref(h, edge_index, L0_gnn_enc_w1, L0_gnn_enc_b1, L0_gnn_enc_w2, L0_gnn_enc_b2, L0_gnn_conv_w, L0_gnn_gru_wih, L0_gnn_gru_whh, L0_gnn_gru_bih, L0_gnn_gru_bhh, L0_gnn_dec_w1, L0_gnn_dec_b1, L0_gnn_dec_w2, L0_gnn_dec_b2)
    h = jnp.maximum(_layernorm(x, axis=-1), 0.0)
    x = x + _L1_gnn_ref(h, L1_gnn_weight, L1_gnn_bias, src, dst, edge_type_8)
    return x

_drawn_inputs = setup_inputs


def setup_inputs(seed=0):
    import zlib

    import numpy as np

    out = dict(_drawn_inputs(seed))
    spreads = {}
    factors = {'L0_gnn_enc_w1': 4.067,
     'L0_gnn_enc_b1': 5.229,
     'L0_gnn_enc_w2': 3.499,
     'L0_gnn_enc_b2': 3.948,
     'L0_gnn_conv_w': 4.136,
     'L0_gnn_gru_wih': 4.097,
     'L0_gnn_gru_whh': 21.19,
     'L0_gnn_gru_bih': 183.662,
     'L0_gnn_gru_bhh': 200.0,
     'L0_gnn_dec_w1': 2.838,
     'L0_gnn_dec_b1': 21.942,
     'L0_gnn_dec_b2': 7.079,
     'L1_gnn_bias': 4.896}
    for name, (base, spread) in spreads.items():
        noise = np.random.default_rng([zlib.crc32(name.encode()), seed]).standard_normal(out[name].shape)
        drawn = base * np.exp(spread * noise) if base else spread * noise
        out[name] = jnp.asarray(drawn.astype(out[name].dtype))
    for name, factor in factors.items():
        out[name] = (out[name] * factor).astype(out[name].dtype)
    return out
```

```python
from contextlib import ExitStack

import concourse.bass as bass
from concourse import mybir

ALU = mybir.AluOpType
ACT = mybir.ActivationFunctionType
F32 = mybir.dt.float32
BF16 = mybir.dt.bfloat16
I32 = mybir.dt.int32

P = 128
NODES, FEAT, EDGES, RELS, STEPS = 6250, 128, 200000, 8, 5
TILES = -(-NODES // P)
ROWS = TILES * P
WIN = 512
FULL_WINDOWS = ROWS // WIN
WINDOWS = FULL_WINDOWS + 1
LAST = ROWS - FULL_WINDOWS * WIN

COLS = 2048
SORTED = P * COLS
COL_BITS, PART_BITS = 11, 7
SLAB = 16
SLABS = -(-EDGES // (P * SLAB))
PER = SLABS * SLAB
PAD_NODE = 8191
FLOAT_BIT = 0x20000000
SRC_SHIFT, DST_SHIFT, NODE_MASK = 3, 16, 0x1FFF
OUT_OF_BOUNDS = 27

COUNT_CELLS = WINDOWS * ROWS * WIN
NO_EDGE_ROW = P * PER
NO_CARRY = P
LOWEST = -3.4028234663852886e38

PACK = {}
_at = 0
for _name, _width in [("enc_w1", FEAT), ("enc_w2", FEAT), ("wih", 3 * FEAT), ("whh", 3 * FEAT),
                      ("dec_w1", FEAT), ("dec_w2", FEAT), ("conv", STEPS * FEAT),
                      ("rel", (RELS + 1) * FEAT), ("enc_b1", 1), ("enc_b2", 1), ("bih", 3),
                      ("bhh", 3), ("dec_b1", 1), ("dec_b2", 1)]:
    PACK[_name] = (_at, _width)
    _at += _width
PACKED = _at


NORM_STEPS = 6


class Count:

    def __init__(self, sem):
        self.sem, self.value = sem, 0

    def add(self, by=1):
        self.value += by
        return self.sem, by


def whole_rows(keys):
    return keys.rearrange("p (g t e) -> p g t e", t=2, e=1)


class WaitHolder:

    def __init__(self, nc, ctx, engine, name):
        self.engine, self.turns = engine, ctx.enter_context(nc.semaphore(name))

    def take(self):
        self.engine.sem_inc(self.turns, 1)


def sort_edges(nc, mem, dram):
    with ExitStack() as ctx:
        def sb(name, shape, dt):
            return ctx.enter_context(nc.sbuf_tensor(name, shape, dt))

        def sem(name):
            return ctx.enter_context(nc.semaphore(name))

        raw = sb("raw_edges", [P, 3, COLS], I32)
        keys_a = sb("keys_a", [P, COLS], F32)
        keys_b = sb("keys_b", [P, COLS], F32)
        turned = sb("keys_turned", [P, COLS], F32)
        turned_b = sb("keys_turned_b", [P, COLS], F32)
        zeros = sb("zeros", [P, TILES * WIN // 2], F32)
        part = sb("partition_number", [P, 1], I32)
        bits = sb("partition_bits", [P, PART_BITS + 1], I32)
        signs = sb("partition_signs", [P, PART_BITS + 1], F32)
        flips = sb("sign_changes", [P, PART_BITS], F32)

        edges_in, packed_in = sem("edges_in"), sem("packed_in")
        zeros_set, iota_done, ident_zero, ident_done = sem("zeros_set"), sem("iota_done"), sem("ident_zero"), sem("ident_done")
        zero_filled = sem("zero_filled")
        keys_step = Count(sem("keys_step"))
        turned_psum, turned_sbuf = Count(sem("turned_psum")), Count(sem("turned_sbuf"))
        keys_out = sem("keys_out")

        psum = mem["psum"]
        ident = mem["ident"]
        psum_keys = psum[:, 0:4, :].rearrange("p b c -> p (b c)")

        handoffs = []

        block = ctx.enter_context(nc.Block())

        @block.vector
        def _(dve):
            v = nc.vector

            def done(ins):
                ins.then_inc(*keys_step.add())

            def settled():
                dve.wait_ge(keys_step.sem, keys_step.value)

            def exchange(src, dst, bit, mirrored=False):
                s = src.rearrange("p (g t e) -> p g t e", t=2, e=1 << bit)
                d = dst.rearrange("p (g t e) -> p g t e", t=2, e=1 << bit)
                turn = slice(None, None, -1) if mirrored else slice(None)
                settled()
                done(v.tensor_tensor(d[:, :, 0, :], s[:, :, 0, :], s[:, :, 1, turn], ALU.min))
                done(v.tensor_tensor(d[:, :, 1, turn], s[:, :, 0, :], s[:, :, 1, turn], ALU.max))

            dve.wait_ge(iota_done, 1)
            for b in range(PART_BITS):
                done(v.tensor_scalar(bits[:, b:b + 1], part[:], b, 1, ALU.logical_shift_right, ALU.bitwise_and))
            done(v.memset(bits[:, PART_BITS:], 0))
            settled()
            done(v.tensor_scalar(signs[:], bits[:], -2.0, 1.0, ALU.mult, ALU.add))
            settled()
            done(v.tensor_tensor(flips[:], signs[:, :PART_BITS], signs[:, 1:], ALU.mult))

            dve.wait_ge(edges_in, 48)
            key = keys_a[:].bitcast(I32)
            tmp = keys_b[:].bitcast(I32)
            done(v.scalar_tensor_tensor(out=tmp, in0=raw[:, 1, :], scalar=SRC_SHIFT, in1=raw[:, 2, :],
                                        op0=ALU.logical_shift_left, op1=ALU.bitwise_or))
            settled()
            done(v.scalar_tensor_tensor(out=key, in0=raw[:, 0, :], scalar=DST_SHIFT, in1=tmp,
                                        op0=ALU.logical_shift_left, op1=ALU.bitwise_or))
            settled()
            done(v.tensor_scalar(tmp, key, FLOAT_BIT, None, ALU.bitwise_or))
            settled()
            done(v.tensor_scalar(keys_a[:], keys_b[:], signs[:, 0:1], None, ALU.mult))

            cur, other = keys_a[:], keys_b[:]
            for phase in range(1, COL_BITS + 1):
                exchange(cur, other, phase - 1, mirrored=phase > 1)
                cur, other = other, cur
                for bit in range(phase - 2, -1, -1):
                    exchange(cur, other, bit)
                    cur, other = other, cur
            for phase in range(1, PART_BITS + 1):
                settled()
                done(v.tensor_scalar(other, cur, flips[:, phase - 1:phase], None, ALU.mult))
                cur, other = other, cur
                handoffs.append(keys_step.value)
                dve.wait_ge(turned_sbuf.sem, 4 * (2 * phase - 1))
                t_cur, t_other = turned[:], turned_b[:]
                for bit in range(phase - 1, -1, -1):
                    exchange(t_cur, t_other, bit)
                    t_cur, t_other = t_other, t_cur
                handoffs.append(keys_step.value)
                dve.wait_ge(turned_sbuf.sem, 4 * 2 * phase)
                cur, other = keys_a[:], keys_b[:]
                for bit in range(COL_BITS - 1, -1, -1):
                    exchange(cur, other, bit)
                    cur, other = other, cur
            mem["sorted_keys"] = cur
            handoffs.append(keys_step.value)

        local = COL_BITS * (COL_BITS + 1) // 2
        first = [keys_a[:], keys_b[:]]

        def keys_to_turn(phase):
            steps = local + 1 if phase == 1 else COL_BITS + 1
            return first[steps % 2]

        def turned_back(phase):
            return [turned[:], turned_b[:]][phase % 2]

        @block.tensor
        def _(pe):
            pe.wait_ge(ident_done, 1)
            for turn in range(2 * PART_BITS):
                phase = turn // 2 + 1
                src = keys_to_turn(phase) if turn % 2 == 0 else turned_back(phase)
                pe.wait_ge(keys_step.sem, handoffs[turn])
                for bank in range(4):
                    if turn:
                        pe.wait_ge(turned_sbuf.sem, 4 * (turn - 1) + bank + 1)
                    for c in range(4 * bank, 4 * bank + 4):
                        mm = nc.tensor.transpose(psum_keys[:, c * P:(c + 1) * P], src[:, c * P:(c + 1) * P], ident[:])
                    mm.then_inc(*turned_psum.add())

        @block.scalar
        def _(act):
            act.wait_ge(zeros_set, 1)
            cells = dram["counts"].rearrange("(w p c) one -> w p (c one)", w=WINDOWS, p=P)
            for w in range(WINDOWS):
                act.dma_start(cells[w], zeros[:].bitcast(BF16)).then_inc(zero_filled, 16)
            for turn in range(2 * PART_BITS):
                dst = turned if turn % 2 == 0 else keys_a
                for bank in range(4):
                    act.wait_ge(turned_psum.sem, 4 * turn + bank + 1)
                    nc.scalar.activation(dst[:, bank * 512:(bank + 1) * 512], psum_keys[:, bank * 512:(bank + 1) * 512],
                                         ACT.Copy).then_inc(*turned_sbuf.add())
            act.wait_ge(zero_filled, 16 * WINDOWS)

        @block.gpsimd
        def _(pool):
            nc.gpsimd.iota(part[:], [[0, 1]], base=0, channel_multiplier=1).then_inc(iota_done, 1)
            nc.gpsimd.memset(ident[:], 0.0).then_inc(ident_zero, 1)
            pool.wait_ge(ident_zero, 1)
            nc.gpsimd.affine_select(out=ident[:], in_=ident[:], compare_op=ALU.not_equal, fill=1.0, base=0,
                                    pattern=[[-1, P]], channel_multiplier=1).then_inc(ident_done, 1)
            nc.gpsimd.memset(zeros[:], 0.0).then_inc(zeros_set, 1)

        @block.sync
        def _(sp):
            for n, name in enumerate(("dst", "src", "edge_type")):
                sp.dma_start(raw[:, n, :], dram[name]).then_inc(edges_in, 16)
            sp.dma_start(mem["packed"][:], dram["packed"]).then_inc(packed_in, 16)
            sp.wait_ge(keys_step.sem, handoffs[-1])
            sp.dma_start(dram["keys"][1:1 + SORTED].rearrange("(p c) -> p c", p=P), mem["sorted_keys"].bitcast(I32)).then_inc(keys_out, 16)
            sp.dma_start(dram["keys"][0:1].rearrange("(a c) -> a c", a=1), zeros[0:1, 0:1].bitcast(I32)).then_inc(keys_out, 16)
            sp.wait_ge(keys_out, 32)
            sp.wait_ge(packed_in, 16)


def work_out_indices(nc, mem, dram):
    with ExitStack() as ctx:
        def sb(name, shape, dt):
            return ctx.enter_context(nc.sbuf_tensor(name, shape, dt))

        def sem(name):
            return ctx.enter_context(nc.semaphore(name))

        around = sb("keys_before_at_after", [P, 3, PER], I32)
        scratch = [sb(f"scratch_{n}", [P, PER], I32) for n in range(3)]
        before_cell = sb("before_in_cell", [P, PER], F32)
        before_dst = sb("before_in_dst", [P, PER], F32)
        ones = sb("ones", [P, PER], F32)
        rank = sb("rank_in_cell", [P, PER], F32)
        through = sb("cell_through", [P, PER], F32)
        dst_through = sb("dst_through", [P, PER], F32)
        place = sb("place", [P, PER], I32)
        part = sb("partition_less_none", [P, 1], F32)
        ends_start = sb("ends_start", [P, TILES, 2], I32)
        rows = sb("carry_rows", [1, 3, P + 1], F32)
        carry = sb("carry_column", [P, 1], F32)

        keys_in, ends_init = sem("keys_in"), sem("ends_init")
        iotas, iota_part = sem("iotas"), sem("iota_part")
        step = Count(sem("index_step"))
        rows_turned, carry_turned = sem("rows_turned"), sem("carry_turned")
        psum, ident = mem["psum"], mem["ident"]
        marks = {}

        block = ctx.enter_context(nc.Block())

        @block.vector
        def _(dve):
            v = nc.vector
            prev, key, nxt = (around[:, n, :] for n in range(3))
            a, b, c = (s[:] for s in scratch)

            def done(ins):
                ins.then_inc(*step.add())

            def settled():
                dve.wait_ge(step.sem, step.value)

            done(v.memset(ones[:], 1.0))
            done(v.memset(ends_start[:, :, 0], NO_EDGE_ROW))
            done(v.memset(ends_start[:, :, 1], NO_CARRY))
            done(v.memset(rows[:], 0.0))
            marks["ends_start"] = step.value
            dve.wait_ge(keys_in, 48)
            done(v.tensor_tensor(a, prev, key, ALU.bitwise_xor))
            done(v.tensor_tensor(b, nxt, key, ALU.bitwise_xor))
            settled()
            done(v.tensor_scalar(c, a, SRC_SHIFT, None, ALU.logical_shift_right))
            done(v.tensor_scalar(prev, a, DST_SHIFT, None, ALU.logical_shift_right))
            settled()
            done(v.tensor_scalar(before_cell[:], c, 0.0, None, ALU.is_equal))
            done(v.tensor_scalar(before_dst[:], prev, 0.0, None, ALU.is_equal))
            settled()
            done(v.tensor_tensor_scan(rank[:], before_cell[:], ones[:], 0.0, ALU.mult, ALU.add))
            done(v.tensor_tensor_scan(through[:], before_cell[:], ones[:], 1.0, ALU.mult, ALU.mult))
            done(v.tensor_tensor_scan(dst_through[:], before_dst[:], ones[:], 1.0, ALU.mult, ALU.mult))
            marks["scanned"] = step.value
            done(v.tensor_scalar(mem["cap"][:], before_dst[:], -2.0, 1.0, ALU.mult, ALU.add))
            settled()
            done(v.tensor_scalar(mem["cap"][:], mem["cap"][:], LOWEST, None, ALU.mult))
            done(v.tensor_copy(mem["all_through"][:], dst_through[:, PER - 1:PER]))
            done(v.tensor_scalar(a, b, SRC_SHIFT, None, ALU.logical_shift_right))
            done(v.tensor_scalar(c, b, DST_SHIFT, None, ALU.logical_shift_right))
            settled()
            done(v.tensor_scalar(nxt, a, 0.0, None, ALU.is_equal))
            done(v.tensor_scalar(prev, c, 0.0, None, ALU.is_equal))
            settled()
            done(v.tensor_scalar(a, key, DST_SHIFT, NODE_MASK, ALU.logical_shift_right, ALU.bitwise_and))
            settled()
            done(v.scalar_tensor_tensor(out=mem["end_index"][:], in0=prev, scalar=OUT_OF_BOUNDS, in1=a,
                                        op0=ALU.logical_shift_left, op1=ALU.bitwise_or))
            dve.wait_ge(iotas, 2)
            done(v.tensor_copy(mem["end_row"][:, :, 0], place[:]))
            done(v.tensor_scalar(mem["end_row"][:, :, 1], dst_through[:], part[:, 0:1], float(NO_CARRY), ALU.mult, ALU.add))
            done(v.tensor_scalar(mem["table_index"][:], key, (1 << DST_SHIFT) - 1, None, ALU.bitwise_and))
            done(v.tensor_scalar(b, key, SRC_SHIFT, NODE_MASK, ALU.logical_shift_right, ALU.bitwise_and))
            done(v.tensor_scalar(c, key, DST_SHIFT + 9, 15, ALU.logical_shift_right, ALU.bitwise_and))
            settled()
            done(v.scalar_tensor_tensor(out=prev, in0=c, scalar=float(ROWS), in1=b, op0=ALU.mult, op1=ALU.add))
            settled()
            done(v.tensor_scalar(c, a, WIN - 1, None, ALU.bitwise_and))
            settled()
            done(v.scalar_tensor_tensor(out=b, in0=prev, scalar=9, in1=c,
                                        op0=ALU.logical_shift_left, op1=ALU.bitwise_or))
            settled()
            done(v.scalar_tensor_tensor(out=mem["cell_index"][:], in0=nxt, scalar=OUT_OF_BOUNDS, in1=b,
                                        op0=ALU.logical_shift_left, op1=ALU.bitwise_or))
            dve.wait_ge(rows_turned, 2)
            done(v.tensor_copy(rows[:, 0, 0:P], psum[0:1, 0, 0:P]))
            done(v.tensor_copy(rows[:, 1, 0:P], psum[0:1, 1, 0:P]))
            settled()
            done(v.tensor_tensor_scan(rows[:, 2, 1:P + 1], rows[:, 1, 0:P], rows[:, 0, 0:P], 0.0, ALU.mult, ALU.add))
            marks["carry_row"] = step.value
            dve.wait_ge(carry_turned, 1)
            done(v.tensor_copy(carry[:], psum[:, 2, 0:1]))
            settled()
            done(v.scalar_tensor_tensor(out=mem["cell_count"][:], in0=through[:], scalar=carry[:, 0:1], in1=rank[:],
                                        op0=ALU.mult, op1=ALU.add))
            settled()

        @block.tensor
        def _(pe):
            pe.wait_ge(step.sem, marks["scanned"])
            nc.tensor.transpose(psum[0:1, 0, 0:P], rank[:, PER - 1:PER], ident[:]).then_inc(rows_turned, 1)
            nc.tensor.transpose(psum[0:1, 1, 0:P], through[:, PER - 1:PER], ident[:]).then_inc(rows_turned, 1)
            pe.wait_ge(step.sem, marks["carry_row"])
            nc.tensor.transpose(psum[:, 2, 0:1], rows[:, 2, 0:P], ident[0:1, 0:1]).then_inc(carry_turned, 1)

        @block.gpsimd
        def _(pool):
            nc.gpsimd.iota(place[:], [[1, PER]], base=0, channel_multiplier=PER).then_inc(iotas, 1)
            nc.gpsimd.iota(part[:], [[0, 1]], base=-NO_CARRY, channel_multiplier=1,
                           allow_small_or_imprecise_dtypes=True).then_inc(iotas, 1)

        @block.sync
        def _(sp):
            for n in range(3):
                sp.dma_start(around[:, n, :], dram["keys"][n:n + P * PER].rearrange("(p c) -> p c", p=P)).then_inc(keys_in, 16)
            sp.wait_ge(step.sem, marks["ends_start"])
            sp.dma_start(dram["ends"].rearrange("(k p) two -> p k two", p=P), ends_start[:]).then_inc(ends_init, 16)
            sp.wait_ge(ends_init, 16)


def scatter(nc, ctx, pool, name, index, rows, index_slots, row_slots, to, bound, copied, landed):
    held = WaitHolder(nc, ctx, pool, f"{name}_slab_turns")
    with pool.Fori(0, SLABS // 2) as pair:
        for slot in range(2):
            first = pair * (2 * SLAB) + slot * SLAB
            pool.wait_ge(landed[slot], pair * (16 * SLAB))
            nc.gpsimd.tensor_copy(index_slots[:, slot, :], index[:, bass.ds(first, SLAB)]).then_inc(copied, 1)
            nc.gpsimd.tensor_copy(row_slots[:, slot], rows[:, bass.ds(first, SLAB)]).then_inc(copied, 1)
            pool.wait_ge(copied, pair * 4 + (2 * slot + 2))
            held.take()
            for j in range(SLAB):
                nc.gpsimd.indirect_dma_start(
                    out=to, out_offset=bass.IndirectOffsetOnAxis(ap=index_slots[:, slot, j:j + 1], axis=0),
                    in_=row_slots[:, slot, j], in_offset=None,
                    bounds_check=bound, oob_is_err=False).then_inc(landed[slot], 16)
    for slot in range(2):
        pool.wait_ge(landed[slot], 16 * SLAB * (SLABS // 2))


def windows(engine, body, **kw):
    with engine.Fori(0, FULL_WINDOWS) as w:
        body(w * WIN, WIN, w)
    body(FULL_WINDOWS * WIN, LAST, FULL_WINDOWS)


def groups():
    return [list(range(g, min(g + 4, TILES))) for g in range(0, TILES, 4)]


def encode_and_scatter_counts(nc, mem, dram):
    with ExitStack() as ctx:
        def sb(name, shape, dt):
            return ctx.enter_context(nc.sbuf_tensor(name, shape, dt))

        def sem(name):
            return ctx.enter_context(nc.semaphore(name))

        index_slots = sb("cell_index_slots", [P, 2, SLAB], I32)
        count_slots = sb("cell_count_slots", [P, 2, SLAB, 1], BF16)
        copied, landed = sem("cell_copied"), [sem("cells_landed_0"), sem("cells_landed_1")]
        x = sb("x", [P, TILES, FEAT], F32)
        hidden = sb("encoder_hidden", [P, WIN], F32)
        norm = norm_buffers(nc, ctx, "encoder")
        x_in = sem("x_in")
        normed, turned, lifted = sem("x_normed"), sem("x_turned"), sem("x_lifted")
        pre1, act1, pre2, act2 = sem("enc_pre1"), sem("enc_act1"), sem("enc_pre2"), sem("enc_act2")
        psum, ident, h = mem["psum"], mem["ident"], mem["h"]
        w = mem["weight"]

        block = ctx.enter_context(nc.Block())

        @block.gpsimd
        def _(pool):
            scatter(nc, ctx, pool, "cells", mem["cell_index"], mem["cell_count"][:].rearrange("p (c one) -> p c one", one=1),
                    index_slots, count_slots, dram["counts"], COUNT_CELLS - 1, copied, landed)

        @block.sync
        def _(sp):
            sp.dma_start(x[:], dram["x"].rearrange("(k p) f -> p k f", p=P)).then_inc(x_in, 16)

        @block.vector
        def _(dve):
            dve.wait_ge(x_in, 16)
            norm_first(nc, dve, x, norm)
            norm_last(nc, dve, x, norm, normed)

        @block.tensor
        def _(pe):
            pe.wait_ge(normed, 1)
            for g, tiles in enumerate(groups()):
                if g >= 2:
                    pe.wait_ge(lifted, g - 1)
                for i, k in enumerate(tiles):
                    mm = nc.tensor.transpose(psum[:, g % 2, i * P:(i + 1) * P], x[:, k, :], ident[:])
                mm.then_inc(turned, 1)

            def window(at, width, n):
                pe.wait_ge(lifted, len(groups()))
                pe.wait_ge(act1, n)
                nc.tensor.matmul(psum[:, 2, :width], w("enc_w1"), h[:, bass.ds(at, width)],
                                 start=True, stop=True).then_inc(pre1, 1)
                pe.wait_ge(act1, n + 1)
                pe.wait_ge(act2, n)
                nc.tensor.matmul(psum[:, 3, :width], w("enc_w2"), hidden[:, :width],
                                 start=True, stop=True).then_inc(pre2, 1)
            windows(pe, window)

        @block.scalar
        def _(act):
            norm_middle(nc, act, norm)
            for g, tiles in enumerate(groups()):
                act.wait_ge(turned, g + 1)
                nc.scalar.activation(h[:, tiles[0] * P:(tiles[-1] + 1) * P], psum[:, g % 2, :len(tiles) * P],
                                     ACT.Relu).then_inc(lifted, 1)

            def window(at, width, n):
                act.wait_ge(pre1, n + 1)
                act.wait_ge(pre2, n)
                nc.scalar.activation(hidden[:, :width], psum[:, 2, :width], ACT.Relu,
                                     bias=w("enc_b1")).then_inc(act1, 1)
                act.wait_ge(pre2, n + 1)
                nc.scalar.activation(h[:, bass.ds(at, width)], psum[:, 3, :width], ACT.Identity,
                                     bias=w("enc_b2")).then_inc(act2, 1)
            windows(act, window)


def norm_buffers(nc, ctx, name):
    def sb(what, shape):
        return ctx.enter_context(nc.sbuf_tensor(f"{name}_{what}", shape, F32))

    def sem(what):
        return ctx.enter_context(nc.semaphore(f"{name}_{what}"))

    return {"squares": sb("squares", [P, TILES, FEAT]), "mean": sb("mean", [P, TILES]),
            "var": sb("var", [P, TILES]), "std": sb("std", [P, TILES]), "scale": sb("scale", [P, TILES]),
            "eps": sb("eps", [P, 1]), "step": Count(sem("norm_step")), "rooted": sem("rooted")}


def norm_first(nc, dve, x, n):
    v, step = nc.vector, n["step"]
    AX = mybir.AxisListType.X

    def done(ins):
        ins.then_inc(*step.add())
        dve.wait_ge(step.sem, step.value)

    done(v.memset(n["eps"][:], 1e-5))
    done(v.tensor_reduce(n["mean"][:], x[:], AX, ALU.add))
    done(v.tensor_scalar(n["mean"][:], n["mean"][:], 1.0 / FEAT, None, ALU.mult))
    done(v.tensor_tensor(x[:], x[:], n["mean"][:].unsqueeze(2).broadcast_to([P, TILES, FEAT]), ALU.subtract))
    done(v.tensor_tensor(n["squares"][:], x[:], x[:], ALU.mult))
    done(v.tensor_reduce(n["var"][:], n["squares"][:], AX, ALU.add))
    assert step.value == NORM_STEPS


def norm_middle(nc, act, n):
    act.wait_ge(n["step"].sem, NORM_STEPS)
    nc.scalar.activation(n["std"][:], n["var"][:], ACT.Sqrt, bias=n["eps"][:, 0:1],
                         scale=1.0 / FEAT).then_inc(n["rooted"], 1)


def norm_last(nc, dve, x, n, normed):
    v, step = nc.vector, n["step"]
    dve.wait_ge(n["rooted"], 1)
    v.reciprocal(n["scale"][:], n["std"][:]).then_inc(*step.add())
    dve.wait_ge(step.sem, step.value)
    v.tensor_tensor(x[:], x[:], n["scale"][:].unsqueeze(2).broadcast_to([P, TILES, FEAT]),
                    ALU.mult).then_inc(normed, 1)


def gated_steps(nc, mem, dram):
    HALVES = [(0, 25), (25, TILES)]
    with ExitStack() as ctx:
        def sb(name, shape, dt):
            return ctx.enter_context(nc.sbuf_tensor(name, shape, dt))

        def sem(name):
            return ctx.enter_context(nc.semaphore(name))

        index_slots = sb("end_index_slots", [P, 2, SLAB], I32)
        row_slots = sb("end_row_slots", [P, 2, SLAB, 2], I32)
        copied, landed = sem("end_copied"), [sem("ends_landed_0"), sem("ends_landed_1")]
        counts = [sb(f"counts_half_{n}", [P, b - a, WIN], BF16) for n, (a, b) in enumerate(HALVES)]
        parts = sb("m_parts", [P, TILES, 3, FEAT], BF16)
        rest = sb("m_rest", [P, WIN], F32)
        sums = sb("sums", [P, WIN], F32)
        gate_r, gate_z = sb("gate_r", [P, WIN], F32), sb("gate_z", [P, WIN], F32)
        new, diff = sb("candidate", [P, WIN], F32), sb("difference", [P, WIN], F32)
        gate_bias = sb("gate_bias", [P, 2], F32)

        bias_done = sem("gate_bias_done")
        loaded = [sem("counts_loaded_0"), sem("counts_loaded_1")]
        used = [sem("counts_used_0"), sem("counts_used_1")]
        m_done, high_done, rest1_done, mid_done, low_done = (sem(f"m_{s}") for s in ("product", "high", "rest", "mid", "low"))
        sums_done, sums_copied = sem("sums_done"), sem("sums_copied")
        gates_done, gates_acted, cand_pre, cand_done = sem("gates_done"), sem("gates_acted"), sem("candidate_pre"), sem("candidate_done")
        cand_step = sem("candidate_step")
        h_done = sem("h_done")
        psum, h, w = mem["psum"], mem["h"], mem["weight"]
        G = len(groups())
        SUMS, M = 0, (1, 2)
        R, Z, IN, HN = 3, 4, 5, 6

        block = ctx.enter_context(nc.Block())

        @block.gpsimd
        def _(pool):
            scatter(nc, ctx, pool, "ends", mem["end_index"], mem["end_row"], index_slots, row_slots, dram["ends"],
                    NODES - 1, copied, landed)

        @block.sync
        def _(sp):
            cells = dram["counts"].rearrange("(w k p c) one -> w p k (c one)", w=WINDOWS, p=P, c=WIN)
            with sp.Fori(0, STEPS) as t:
                def window(at, width, n):
                    for half, (a, b) in enumerate(HALVES):
                        sp.wait_ge(used[half], t * WINDOWS + n)
                        src = cells[n] if isinstance(n, int) else cells[bass.ds(n, 1)].rearrange("w p k c -> (w p) k c")
                        sp.dma_start(counts[half][:, :, :width], src[:, a:b, :width]).then_inc(loaded[half], 16)
                windows(sp, window)

        @block.tensor
        def _(pe):
            held = WaitHolder(nc, ctx, pe, "step_turns")
            with pe.Fori(0, STEPS) as t:
                pe.wait_ge(h_done, t * WINDOWS)
                for g, tiles in enumerate(groups()):
                    if g >= 2:
                        pe.wait_ge(rest1_done, t * G + (g - 1))
                    else:
                        pe.wait_ge(rest1_done, t * G)
                    for i, k in enumerate(tiles):
                        mm = nc.tensor.matmul(psum[:, M[g % 2], i * P:(i + 1) * P], h[:, k * P:(k + 1) * P],
                                              mem["packed"][:, bass.ds(t * FEAT + PACK["conv"][0], FEAT)],
                                              start=True, stop=True)
                    mm.then_inc(m_done, 1)
                pe.wait_ge(low_done, t * G + G)
                held.take()

                def window(at, width, n):
                    at_window = t * WINDOWS + n
                    pe.wait_ge(sums_copied, at_window)
                    for half, (a, b) in enumerate(HALVES):
                        pe.wait_ge(loaded[half], (at_window + 1) * 16)
                        for k in range(a, b):
                            for part in range(3):
                                mm = nc.tensor.matmul(psum[:, SUMS, :width], parts[:, k, part, :],
                                                      counts[half][:, k - a, :width],
                                                      start=(k == 0 and part == 0), stop=(k == TILES - 1 and part == 2))
                        if half == 0:
                            mm.then_inc(used[0], 1)
                    mm.then_inc(used[1], 1)
                    pe.wait_ge(used[1], at_window + 1)
                    pe.sem_inc(sums_done, 1)
                    pe.wait_ge(sums_copied, at_window + 1)
                    pe.wait_ge(cand_pre, at_window)
                    hw = h[:, bass.ds(at, width)]
                    for bank, gate in ((R, 0), (Z, 1)):
                        nc.tensor.matmul(psum[:, bank, :width], w("wih", gate), sums[:, :width], start=True, stop=False)
                        mm = nc.tensor.matmul(psum[:, bank, :width], w("whh", gate), hw, start=False, stop=True)
                    nc.tensor.matmul(psum[:, IN, :width], w("wih", 2), sums[:, :width], start=True, stop=True)
                    nc.tensor.matmul(psum[:, HN, :width], w("whh", 2), hw, start=True, stop=True).then_inc(gates_done, 1)
                windows(pe, window)

        @block.scalar
        def _(act):
            act.wait_ge(bias_done, 1)
            with act.Fori(0, STEPS) as t:
                for g, tiles in enumerate(groups()):
                    n = len(tiles)
                    part = lambda i: parts[:, tiles[0]:tiles[0] + n, i, :]
                    act.wait_ge(m_done, t * G + (g + 1))
                    nc.scalar.activation(part(0), psum[:, M[g % 2], :n * P].rearrange("p (k f) -> p k f", f=FEAT),
                                         ACT.Copy).then_inc(high_done, 1)
                    act.wait_ge(rest1_done, t * G + (g + 1))
                    nc.scalar.activation(part(1), rest[:, :n * P].rearrange("p (k f) -> p k f", f=FEAT),
                                         ACT.Copy).then_inc(mid_done, 1)

                def window(at, width, n):
                    at_window = t * WINDOWS + n
                    act.wait_ge(sums_done, at_window + 1)
                    act.wait_ge(gates_done, at_window)
                    nc.scalar.activation(sums[:, :width], psum[:, SUMS, :width], ACT.Copy).then_inc(sums_copied, 1)
                    act.wait_ge(gates_done, at_window + 1)
                    act.wait_ge(h_done, at_window)
                    nc.scalar.activation(gate_r[:, :width], psum[:, R, :width], ACT.Sigmoid, bias=gate_bias[:, 0:1]).then_inc(gates_acted, 1)
                    nc.scalar.activation(gate_z[:, :width], psum[:, Z, :width], ACT.Sigmoid, bias=gate_bias[:, 1:2]).then_inc(gates_acted, 1)
                    act.wait_ge(cand_pre, at_window + 1)
                    nc.scalar.activation(new[:, :width], diff[:, :width], ACT.Tanh, bias=w("bih", 2)).then_inc(cand_done, 1)
                windows(act, window)

        @block.vector
        def _(dve):
            v = nc.vector
            v.tensor_tensor(gate_bias[:], mem["packed"][:, PACK["bih"][0]:PACK["bih"][0] + 2],
                            mem["packed"][:, PACK["bhh"][0]:PACK["bhh"][0] + 2], ALU.add).then_inc(bias_done, 1)
            with dve.Fori(0, STEPS) as t:
                for g, tiles in enumerate(groups()):
                    n = len(tiles)
                    part = lambda i: parts[:, tiles[0]:tiles[0] + n, i, :]
                    rest3 = rest[:, :n * P].rearrange("p (k f) -> p k f", f=FEAT)
                    dve.wait_ge(high_done, t * G + (g + 1))
                    dve.wait_ge(low_done, t * G + g)
                    v.tensor_tensor(rest3, psum[:, M[g % 2], :n * P].rearrange("p (k f) -> p k f", f=FEAT), part(0),
                                    ALU.subtract).then_inc(rest1_done, 1)
                    dve.wait_ge(mid_done, t * G + (g + 1))
                    v.tensor_tensor(part(2), rest3, part(1), ALU.subtract).then_inc(low_done, 1)

                def window(at, width, n):
                    at_window = t * WINDOWS + n
                    hw = h[:, bass.ds(at, width)]
                    dve.wait_ge(gates_acted, at_window * 2 + 2)
                    v.scalar_tensor_tensor(out=diff[:, :width], in0=psum[:, HN, :width], scalar=w("bhh", 2),
                                           in1=gate_r[:, :width], op0=ALU.add, op1=ALU.mult).then_inc(cand_step, 1)
                    dve.wait_ge(cand_step, at_window * 3 + 1)
                    v.tensor_tensor(diff[:, :width], diff[:, :width], psum[:, IN, :width], ALU.add).then_inc(cand_pre, 1)
                    dve.wait_ge(cand_done, at_window + 1)
                    v.tensor_tensor(diff[:, :width], hw, new[:, :width], ALU.subtract).then_inc(cand_step, 1)
                    dve.wait_ge(cand_step, at_window * 3 + 2)
                    v.tensor_tensor(diff[:, :width], diff[:, :width], gate_z[:, :width], ALU.mult).then_inc(cand_step, 1)
                    dve.wait_ge(cand_step, at_window * 3 + 3)
                    v.tensor_tensor(hw, diff[:, :width], new[:, :width], ALU.add).then_inc(h_done, 1)
                windows(dve, window)


def decode_and_table(nc, mem, dram):
    with ExitStack() as ctx:
        def sb(name, shape, dt):
            return ctx.enter_context(nc.sbuf_tensor(name, shape, dt))

        def sem(name):
            return ctx.enter_context(nc.semaphore(name))

        hidden = sb("decoder_hidden", [P, WIN], F32)
        decoded = sb("decoded", [P, 2, WIN], F32)
        y = sb("second_norm", [P, TILES, FEAT], F32)
        norm = norm_buffers(nc, ctx, "second")
        table = sb("table_rows", [P, 2, RELS * FEAT], F32)
        rel_bias = sb("relation_bias", [P, (RELS + 1) * FEAT], F32)
        x_in, bias_in = sem("x_again_in"), sem("relation_bias_in")
        h_relu = sem("h_relu")
        pre1, act1, pre2, act2 = sem("dec_pre1"), sem("dec_act1"), sem("dec_pre2"), sem("dec_act2")
        back, added = sem("turned_back"), sem("residual_added")
        y_copied, normed, turned, lifted = sem("y_copied"), sem("y_normed"), sem("y_turned"), sem("y_lifted")
        rows_done, rows_biased, rows_out = sem("rows_done"), sem("rows_biased"), [sem("rows_out_0"), sem("rows_out_1")]
        psum, ident, h, w = mem["psum"], mem["ident"], mem["h"], mem["weight"]
        x1, base = mem["x1"], mem["base"]
        wins = [(n * WIN, WIN) for n in range(FULL_WINDOWS)] + [(FULL_WINDOWS * WIN, LAST)]
        HALF = RELS * FEAT // 2

        block = ctx.enter_context(nc.Block())

        @block.sync
        def _(sp):
            sp.dma_start(x1[:], dram["x"].rearrange("(k p) f -> p k f", p=P)).then_inc(x_in, 16)
            sp.dma_start(rel_bias[:], dram["rel_bias"].broadcast_to([P, (RELS + 1) * FEAT])).then_inc(bias_in, 16)
            rows = dram["table"].rearrange("(k p r) f -> k p (r f)", p=P, r=RELS)
            for k in range(TILES):
                sp.wait_ge(rows_biased, 3 * k + 2)
                sp.dma_start(rows[k], table[:, k % 2, :]).then_inc(rows_out[k % 2], 16)
            sp.wait_ge(rows_out[0], 16 * (TILES - TILES // 2))
            sp.wait_ge(rows_out[1], 16 * (TILES // 2))

        @block.tensor
        def _(pe):
            for n, (at, width) in enumerate(wins):
                pe.wait_ge(h_relu, n + 1)
                if n:
                    pe.wait_ge(act1, n)
                nc.tensor.matmul(psum[:, 0, :width], w("dec_w1"), h[:, at:at + width], start=True, stop=True).then_inc(pre1, 1)
                pe.wait_ge(act1, n + 1)
                if n:
                    pe.wait_ge(act2, n)
                nc.tensor.matmul(psum[:, 1, :width], w("dec_w2"), hidden[:, :width], start=True, stop=True).then_inc(pre2, 1)
                pe.wait_ge(act2, n + 1)
                if n >= 2:
                    pe.wait_ge(added, n - 1)
                for i in range(width // P):
                    mm = nc.tensor.transpose(psum[:, 2 + n % 2, i * P:(i + 1) * P], decoded[:, n % 2, i * P:(i + 1) * P], ident[:])
                mm.then_inc(back, 1)
            pe.wait_ge(normed, 1)
            for g, tiles in enumerate(groups()):
                if g >= 2:
                    pe.wait_ge(lifted, g - 1)
                for i, k in enumerate(tiles):
                    mm = nc.tensor.transpose(psum[:, g % 2, i * P:(i + 1) * P], y[:, k, :], ident[:])
                mm.then_inc(turned, 1)
            pe.wait_ge(added, len(wins))
            for k in range(TILES):
                if k % 4 == 0:
                    pe.wait_ge(lifted, k // 4 + 1)
                banks = (2, 3, 4) if k % 2 == 0 else (5, 6, 7)
                if k >= 2:
                    pe.wait_ge(rows_biased, 3 * (k - 1))
                lhs = h[:, k * P:(k + 1) * P]
                nc.tensor.matmul(psum[:, banks[0], :], lhs, w.wide("rel", 0, HALF), start=True, stop=True)
                nc.tensor.matmul(psum[:, banks[1], :], lhs, w.wide("rel", HALF, HALF), start=True, stop=True)
                nc.tensor.matmul(psum[:, banks[2], :FEAT], lhs, w.wide("rel", 2 * HALF, FEAT), start=True, stop=True).then_inc(rows_done, 1)

        @block.scalar
        def _(act):
            for n, (at, width) in enumerate(wins):
                nc.scalar.activation(h[:, at:at + width], h[:, at:at + width], ACT.Relu).then_inc(h_relu, 1)
            for n, (at, width) in enumerate(wins):
                act.wait_ge(pre1, n + 1)
                if n:
                    act.wait_ge(pre2, n)
                nc.scalar.activation(hidden[:, :width], psum[:, 0, :width], ACT.Relu, bias=w("dec_b1")).then_inc(act1, 1)
                act.wait_ge(pre2, n + 1)
                if n >= 2:
                    act.wait_ge(back, n - 1)
                nc.scalar.activation(decoded[:, n % 2, :width], psum[:, 1, :width], ACT.Sigmoid, bias=w("dec_b2")).then_inc(act2, 1)
            norm_middle(nc, act, norm)
            for g, tiles in enumerate(groups()):
                act.wait_ge(turned, g + 1)
                nc.scalar.activation(h[:, tiles[0] * P:(tiles[-1] + 1) * P], psum[:, g % 2, :len(tiles) * P],
                                     ACT.Relu).then_inc(lifted, 1)

        @block.vector
        def _(dve):
            v = nc.vector
            dve.wait_ge(x_in, 16)
            for n, (at, width) in enumerate(wins):
                dve.wait_ge(back, n + 1)
                tiles = x1[:, 4 * n:4 * n + width // P, :]
                v.tensor_tensor(tiles, tiles, psum[:, 2 + n % 2, :width].rearrange("p (k f) -> p k f", f=FEAT), ALU.add).then_inc(added, 1)
            dve.wait_ge(added, len(wins))
            v.tensor_copy(y[:], x1[:]).then_inc(y_copied, 1)
            dve.wait_ge(y_copied, 1)
            norm_first(nc, dve, y, norm)
            norm_last(nc, dve, y, norm, normed)
            dve.wait_ge(bias_in, 16)
            for k in range(TILES):
                banks = (2, 3, 4) if k % 2 == 0 else (5, 6, 7)
                dve.wait_ge(rows_done, k + 1)
                if k >= 2:
                    dve.wait_ge(rows_out[k % 2], 16 * (k // 2))
                for half in range(2):
                    v.tensor_tensor(table[:, k % 2, half * HALF:(half + 1) * HALF], psum[:, banks[half], :],
                                    rel_bias[:, half * HALF:(half + 1) * HALF], ALU.add).then_inc(rows_biased, 1)
                v.tensor_tensor(base[:, k, :], psum[:, banks[2], :FEAT], rel_bias[:, 2 * HALF:], ALU.add).then_inc(rows_biased, 1)


def running_maximum(nc, mem, dram):
    with ExitStack() as ctx:
        def sb(name, shape, dt):
            return ctx.enter_context(nc.sbuf_tensor(name, shape, dt))

        def sem(name):
            return ctx.enter_context(nc.semaphore(name))

        index_slots = sb("table_index_slots", [P, 2, SLAB], I32)
        cap_slots = sb("cap_slots", [P, 2, SLAB], F32)
        rows = sb("gathered", [P, 2, SLAB, FEAT], F32)
        best = sb("best", [P, 2, SLAB, FEAT], F32)
        zero_row = sb("zero_row", [1, FEAT], F32)
        none_row = sb("none_row", [1, FEAT], F32)
        spread = sb("all_through_spread", [P, P], F32)
        keep = sb("keep", [P, P], F32)
        last = sb("last_turned", [P, P], F32)
        joined = sb("joined", [P, P], F32)
        carries = sb("carries", [P, FEAT], F32)
        copied = sem("table_index_copied")
        slot_read = [sem("gathered_read_0"), sem("gathered_read_1")]
        gathered = [sem("gathered_0"), sem("gathered_1")]
        consts = sem("max_constants")
        masks, step = sem("cap_copied"), sem("max_step")
        written = [sem("best_written_0"), sem("best_written_1")]
        zero_out, carry_out = sem("zero_row_out"), sem("carry_out")
        join_step, join_turned = sem("join_step"), sem("join_turned")
        psum, ident = mem["psum"], mem["ident"]
        CONSTS = 4

        block = ctx.enter_context(nc.Block())

        @block.gpsimd
        def _(pool):
            held = WaitHolder(nc, ctx, pool, "gather_turns")
            with pool.Fori(0, SLABS // 2) as pair:
                for slot in range(2):
                    pool.wait_ge(slot_read[slot], pair)
                    nc.gpsimd.tensor_copy(index_slots[:, slot, :],
                                          mem["table_index"][:, bass.ds(pair * (2 * SLAB) + slot * SLAB, SLAB)]).then_inc(copied, 1)
                    pool.wait_ge(copied, pair * 2 + (slot + 1))
                    held.take()
                    for j in range(SLAB):
                        nc.gpsimd.indirect_dma_start(
                            out=rows[:, slot, j, :], out_offset=None, in_=dram["table"],
                            in_offset=bass.IndirectOffsetOnAxis(ap=index_slots[:, slot, j:j + 1], axis=0)).then_inc(gathered[slot], 16)

        @block.vector
        def _(dve):
            v = nc.vector
            v.memset(best[:, 1, SLAB - 1, :], LOWEST).then_inc(consts, 1)
            v.memset(none_row[:], LOWEST).then_inc(consts, 1)
            v.memset(zero_row[:], 0.0).then_inc(consts, 1)
            v.memset(spread[:], 1.0).then_inc(consts, 1)
            dve.wait_ge(consts, CONSTS)
            with dve.Fori(0, SLABS // 2) as pair:
                for slot in range(2):
                    base_step = pair * (2 * SLAB) + slot * SLAB
                    v.tensor_copy(cap_slots[:, slot, :], mem["cap"][:, bass.ds(base_step, SLAB)]).then_inc(masks, 1)
                    dve.wait_ge(masks, pair * 2 + (slot + 1))
                    dve.wait_ge(gathered[slot], (pair + 1) * (16 * SLAB))
                    dve.wait_ge(written[slot], pair * 16)
                    for j in range(SLAB):
                        before = best[:, slot, j - 1, :] if j else best[:, 1 - slot, SLAB - 1, :]
                        dve.wait_ge(step, base_step + j)
                        v.scalar_tensor_tensor(out=best[:, slot, j, :], in0=before, scalar=cap_slots[:, slot, j:j + 1],
                                               in1=rows[:, slot, j, :], op0=ALU.min, op1=ALU.max).then_inc(step, 1)
                    dve.wait_ge(step, base_step + SLAB)
                    dve.sem_inc(slot_read[slot], 1)
            v.tensor_scalar(spread[:], spread[:], mem["all_through"][:, 0:1], None, ALU.mult).then_inc(join_step, 1)
            dve.wait_ge(join_turned, 2)
            v.tensor_scalar(keep[:], psum[:, 0, 0:P], -2.0, 1.0, ALU.mult, ALU.add).then_inc(join_step, 1)
            v.tensor_copy(last[:], psum[:, 1, 0:P]).then_inc(join_step, 1)
            dve.wait_ge(join_step, 3)
            v.tensor_scalar(keep[:], keep[:], LOWEST, None, ALU.mult).then_inc(join_step, 1)
            dve.wait_ge(join_step, 4)
            v.tensor_tensor_scan(joined[:], keep[:], last[:], LOWEST, ALU.min, ALU.max).then_inc(join_step, 1)
            dve.wait_ge(join_turned, 3)
            v.tensor_copy(carries[:], psum[:, 2, 0:FEAT]).then_inc(join_step, 1)

        @block.tensor
        def _(pe):
            pe.wait_ge(join_step, 1)
            pe.wait_ge(step, PER)
            nc.tensor.transpose(psum[:, 0, 0:P], spread[:], ident[:]).then_inc(join_turned, 1)
            nc.tensor.transpose(psum[:, 1, 0:P], best[:, 1, SLAB - 1, :], ident[:]).then_inc(join_turned, 1)
            pe.wait_ge(join_step, 5)
            nc.tensor.transpose(psum[:, 2, 0:FEAT], joined[:], ident[:]).then_inc(join_turned, 1)

        @block.sync
        def _(sp):
            sp.wait_ge(consts, CONSTS)
            sp.dma_start(dram["maxima"][NO_EDGE_ROW:NO_EDGE_ROW + 1, :], zero_row[:]).then_inc(zero_out, 16)
            sp.dma_start(dram["carries"][0:1, :], none_row[:]).then_inc(zero_out, 16)
            sp.dma_start(dram["carries"][NO_CARRY:NO_CARRY + 1, :], none_row[:]).then_inc(zero_out, 16)
            maxima = dram["maxima"][0:P * PER, :].rearrange("(p s c) f -> p s (c f)", p=P, s=SLABS)
            with sp.Fori(0, SLABS // 2) as pair:
                for slot in range(2):
                    sp.wait_ge(step, pair * (2 * SLAB) + (slot + 1) * SLAB)
                    sp.dma_start(maxima[:, bass.ds(pair * 2 + slot, 1), :].rearrange("p s c -> p (s c)"),
                                 best[:, slot].rearrange("p c f -> p (c f)")).then_inc(written[slot], 16)
            sp.wait_ge(join_step, 6)
            sp.dma_start(dram["carries"][1:P, :], carries[0:P - 1, :]).then_inc(carry_out, 16)
            sp.wait_ge(zero_out, 48)
            sp.wait_ge(carry_out, 16)
            for slot in range(2):
                sp.wait_ge(written[slot], 16 * (SLABS // 2))


def finish(nc, mem, dram):
    BATCH = 7
    BATCHES = TILES // BATCH
    with ExitStack() as ctx:
        def sb(name, shape, dt):
            return ctx.enter_context(nc.sbuf_tensor(name, shape, dt))

        def sem(name):
            return ctx.enter_context(nc.semaphore(name))

        ends = sb("ends", [P, TILES, 2], I32)
        end_slots = sb("end_slots", [P, BATCH, 2], I32)
        maxima = sb("node_maxima", [P, BATCH, FEAT], F32)
        carries = sb("node_carries", [P, BATCH, FEAT], F32)
        result = sb("result", [P, BATCH, FEAT], F32)
        ends_in, copied, gathered, step, out_done = (sem(s) for s in ("ends_in", "ends_copied", "maxima_gathered", "finish_step", "out_done"))
        x1, base = mem["x1"], mem["base"]

        block = ctx.enter_context(nc.Block())

        @block.sync
        def _(sp):
            sp.dma_start(ends[:], dram["ends"].rearrange("(k p) two -> p k two", p=P)).then_inc(ends_in, 16)
            out = dram["out"].rearrange("(k p) f -> p k f", p=P)
            with sp.Fori(0, BATCHES) as b:
                sp.wait_ge(step, b * 4 + 4)
                sp.dma_start(out[:, bass.ds(b * BATCH, BATCH), :], result[:]).then_inc(out_done, 16)
            sp.wait_ge(out_done, 16 * BATCHES)

        @block.gpsimd
        def _(pool):
            pool.wait_ge(ends_in, 16)
            held = WaitHolder(nc, ctx, pool, "batch_turns")
            with pool.Fori(0, BATCHES) as b:
                pool.wait_ge(step, b * 4)
                nc.gpsimd.tensor_copy(end_slots[:], ends[:, bass.ds(b * BATCH, BATCH), :]).then_inc(copied, 1)
                pool.wait_ge(copied, b + 1)
                held.take()
                for i in range(BATCH):
                    for n, (to, table) in enumerate(((maxima, "maxima"), (carries, "carries"))):
                        nc.gpsimd.indirect_dma_start(
                            out=to[:, i, :], out_offset=None, in_=dram[table],
                            in_offset=bass.IndirectOffsetOnAxis(ap=end_slots[:, i, n:n + 1], axis=0)).then_inc(gathered, 16)

        @block.vector
        def _(dve):
            v = nc.vector
            with dve.Fori(0, BATCHES) as b:
                tiles = bass.ds(b * BATCH, BATCH)
                dve.wait_ge(gathered, (b + 1) * (32 * BATCH))
                dve.wait_ge(out_done, b * 16)
                v.tensor_tensor(result[:], maxima[:], carries[:], ALU.max).then_inc(step, 1)
                dve.wait_ge(step, b * 4 + 1)
                v.tensor_tensor(result[:], result[:], base[:, tiles, :], ALU.add).then_inc(step, 1)
                dve.wait_ge(step, b * 4 + 2)
                v.tensor_scalar(result[:], result[:], 0.0, None, ALU.max).then_inc(step, 1)
                dve.wait_ge(step, b * 4 + 3)
                v.tensor_tensor(result[:], result[:], x1[:, tiles, :], ALU.add).then_inc(step, 1)


class Weights:

    def __init__(self, packed):
        self.packed = packed

    def __call__(self, name, n=0):
        at, width = PACK[name]
        one = 1 if name in ("enc_b1", "enc_b2", "bih", "bhh", "dec_b1", "dec_b2") else FEAT
        return self.packed[:, at + n * one:at + (n + 1) * one]

    def wide(self, name, first, width):
        at = PACK[name][0] + first
        return self.packed[:, at:at + width]


def build(nc, dram):
    def scratch(name, shape, dt):
        dram[name] = nc.dram_tensor(f"scratch_{name}", shape, dt, kind="Internal").ap()

    scratch("keys", (1 + SORTED,), I32)
    scratch("counts", (COUNT_CELLS, 1), BF16)
    scratch("ends", (ROWS, 2), I32)
    scratch("table", (ROWS * RELS, FEAT), F32)
    scratch("maxima", (NO_EDGE_ROW + 1, FEAT), F32)
    scratch("carries", (NO_CARRY + 1, FEAT), F32)
    with ExitStack() as ctx:
        def sb(name, shape, dt):
            return ctx.enter_context(nc.sbuf_tensor(name, shape, dt))

        mem = {"psum": ctx.enter_context(nc.psum_tensor("banks", [P, 8, WIN], F32)),
               "ident": sb("identity", [P, P], F32), "packed": sb("packed", [P, PACKED], F32)}
        mem["weight"] = Weights(mem["packed"])
        sort_edges(nc, mem, dram)
        mem["table_index"] = sb("table_index", [P, PER], I32)
        mem["cap"] = sb("cap", [P, PER], F32)
        mem["all_through"] = sb("all_through", [P, 1], F32)
        mem["h"] = sb("h", [P, ROWS], F32)
        with ExitStack() as first:
            def early(name, shape, dt):
                mem[name] = first.enter_context(nc.sbuf_tensor(name, shape, dt))

            early("end_index", [P, PER], I32)
            early("end_row", [P, PER, 2], I32)
            early("cell_index", [P, PER], I32)
            early("cell_count", [P, PER], BF16)
            work_out_indices(nc, mem, dram)
            encode_and_scatter_counts(nc, mem, dram)
            gated_steps(nc, mem, dram)
        mem["x1"] = sb("x1", [P, TILES, FEAT], F32)
        mem["base"] = sb("self_part", [P, TILES, FEAT], F32)
        decode_and_table(nc, mem, dram)
        running_maximum(nc, mem, dram)
        finish(nc, mem, dram)


def kernel(**inputs):
    import numpy as np
    import concourse.bacc as bacc
    from concourse.bass_utils import run_bass_kernel_spmd as run

    def get(name):
        return np.asarray(inputs[name])

    def padded(values, fill):
        out = np.full(SORTED, fill, np.int32)
        out[:EDGES] = values
        return out.reshape(P, COLS)

    x = np.zeros((ROWS, FEAT), np.float32)
    x[:NODES] = get("x")
    gnn = "L0_gnn_"
    columns = [get(gnn + "enc_w1").T, get(gnn + "enc_w2").T, get(gnn + "gru_wih").T, get(gnn + "gru_whh").T,
               get(gnn + "dec_w1").T, get(gnn + "dec_w2").T,
               get(gnn + "conv_w").transpose(1, 0, 2).reshape(FEAT, -1),
               get("L1_gnn_weight").transpose(1, 0, 2).reshape(FEAT, -1),
               get(gnn + "enc_b1").reshape(1, FEAT).T, get(gnn + "enc_b2").reshape(1, FEAT).T,
               get(gnn + "gru_bih").reshape(3, FEAT).T, get(gnn + "gru_bhh").reshape(3, FEAT).T,
               get(gnn + "dec_b1").reshape(1, FEAT).T, get(gnn + "dec_b2").reshape(1, FEAT).T]
    arrays = {"x": x, "dst": padded(get("dst"), PAD_NODE), "src": padded(get("src"), 0),
              "edge_type": padded(get("edge_type_8"), 0),
              "packed": np.ascontiguousarray(np.concatenate(columns, axis=1)),
              "rel_bias": np.ascontiguousarray(get("L1_gnn_bias").reshape(1, -1))}
    nc = bacc.Bacc("TRN2", target_bir_lowering=False, num_devices=1)
    dram = {name: nc.dram_tensor(f"in_{name}", a.shape, mybir.dt.from_np(a.dtype), kind="ExternalInput").ap()
            for name, a in arrays.items()}
    dram["out"] = nc.dram_tensor("out_0", (ROWS, FEAT), F32, kind="ExternalOutput").ap()
    build(nc, dram)
    result = run(nc, [{f"in_{name}": a for name, a in arrays.items()}], core_ids=[0]).results[0]["out_0"]
    return result[:NODES]
```

```python
from contextlib import ExitStack

import concourse.bass as bass
from concourse import mybir

ALU = mybir.AluOpType
ACT = mybir.ActivationFunctionType
F32 = mybir.dt.float32
BF16 = mybir.dt.bfloat16
F16 = mybir.dt.float16
I32 = mybir.dt.int32

P = 128
NODES, FEAT, EDGES, RELS, STEPS = 6250, 128, 200000, 8, 5
TILES = -(-NODES // P)
ROWS = TILES * P
WIN = 512
FULL_WINDOWS = ROWS // WIN
WINDOWS = FULL_WINDOWS + 1
LAST = ROWS - FULL_WINDOWS * WIN

COLS = 2048
SORTED = P * COLS
COL_BITS, PART_BITS = 11, 7
SLAB = 16
SLABS = -(-EDGES // (P * SLAB))
PER = SLABS * SLAB
PAD_NODE = 8191
FLOAT_BIT = 0x20000000
SRC_SHIFT, DST_SHIFT, NODE_MASK = 3, 16, 0x1FFF
OUT_OF_BOUNDS = 27

COUNT_CELLS = WINDOWS * ROWS * WIN
NO_EDGE_ROW = P * PER
LOWEST = -3.4028234663852886e38

BLOCKS = COLS // P
assert BLOCKS == SLAB and SLABS <= P
HIGH = 64

PACK = {}
_at = 0
for _name, _width in [("enc_w1", FEAT), ("enc_w2", FEAT), ("wih", 3 * FEAT), ("whh", 3 * FEAT),
                      ("dec_w1", FEAT), ("dec_w2", FEAT), ("conv", STEPS * FEAT),
                      ("rel", (RELS + 1) * FEAT), ("enc_b1", 1), ("enc_b2", 1), ("bih", 3),
                      ("bhh", 3), ("dec_b1", 1), ("dec_b2", 1)]:
    PACK[_name] = (_at, _width)
    _at += _width
PACKED = _at


NORM_STEPS = 6
KEY_STEPS = 18
REACH_STEP, TOP_STEP, SCALE_STEPS = 4, 5, 17
THROUGH_STEP, PLACE_STEP = 4, 9


class Count:

    def __init__(self, sem):
        self.sem, self.value = sem, 0

    def add(self, by=1):
        self.value += by
        return self.sem, by


def whole_rows(keys):
    return keys.rearrange("p (g t e) -> p g t e", t=2, e=1)


class WaitHolder:

    def __init__(self, nc, ctx, engine, name):
        self.engine, self.turns = engine, ctx.enter_context(nc.semaphore(name))

    def take(self):
        self.engine.sem_inc(self.turns, 1)


def sort_edges(nc, mem, dram):
    with ExitStack() as ctx:
        def sb(name, shape, dt):
            return ctx.enter_context(nc.sbuf_tensor(name, shape, dt))

        def sem(name):
            return ctx.enter_context(nc.semaphore(name))

        raw = sb("raw_edges", [P, 3, COLS], I32)
        keys_a = sb("keys_a", [P, COLS], F32)
        keys_b = sb("keys_b", [P, COLS], F32)
        turned = sb("keys_turned", [P, COLS], F32)
        turned_b = sb("keys_turned_b", [P, COLS], F32)
        zeros = sb("zeros", [P, TILES * WIN // 2], F32)
        part = sb("partition_number", [P, 1], I32)
        bits = sb("partition_bits", [P, PART_BITS + 1], I32)
        signs = sb("partition_signs", [P, PART_BITS + 1], F32)
        flips = sb("sign_changes", [P, PART_BITS], F32)

        edges_in, packed_in = sem("edges_in"), sem("packed_in")
        zeros_set, iota_done, ident_zero, ident_done = sem("zeros_set"), sem("iota_done"), sem("ident_zero"), sem("ident_done")
        zero_filled = sem("zero_filled")
        keys_step = Count(sem("keys_step"))
        turned_psum, turned_sbuf = Count(sem("turned_psum")), Count(sem("turned_sbuf"))
        keys_out = sem("keys_out")

        psum = mem["psum"]
        ident = mem["ident"]
        psum_keys = psum[:, 0:4, :].rearrange("p b c -> p (b c)")

        handoffs = []

        block = ctx.enter_context(nc.Block())

        @block.vector
        def _(dve):
            v = nc.vector

            def done(ins):
                ins.then_inc(*keys_step.add())

            def settled():
                dve.wait_ge(keys_step.sem, keys_step.value)

            def exchange(src, dst, bit, mirrored=False):
                s = src.rearrange("p (g t e) -> p g t e", t=2, e=1 << bit)
                d = dst.rearrange("p (g t e) -> p g t e", t=2, e=1 << bit)
                turn = slice(None, None, -1) if mirrored else slice(None)
                settled()
                done(v.tensor_tensor(d[:, :, 0, :], s[:, :, 0, :], s[:, :, 1, turn], ALU.min))
                done(v.tensor_tensor(d[:, :, 1, turn], s[:, :, 0, :], s[:, :, 1, turn], ALU.max))

            dve.wait_ge(iota_done, 1)
            for b in range(PART_BITS):
                done(v.tensor_scalar(bits[:, b:b + 1], part[:], b, 1, ALU.logical_shift_right, ALU.bitwise_and))
            done(v.memset(bits[:, PART_BITS:], 0))
            settled()
            done(v.tensor_scalar(signs[:], bits[:], -2.0, 1.0, ALU.mult, ALU.add))
            settled()
            done(v.tensor_tensor(flips[:], signs[:, :PART_BITS], signs[:, 1:], ALU.mult))

            dve.wait_ge(edges_in, 48)
            key = keys_a[:].bitcast(I32)
            tmp = keys_b[:].bitcast(I32)
            done(v.scalar_tensor_tensor(out=tmp, in0=raw[:, 1, :], scalar=SRC_SHIFT, in1=raw[:, 2, :],
                                        op0=ALU.logical_shift_left, op1=ALU.bitwise_or))
            settled()
            done(v.scalar_tensor_tensor(out=key, in0=raw[:, 0, :], scalar=DST_SHIFT, in1=tmp,
                                        op0=ALU.logical_shift_left, op1=ALU.bitwise_or))
            settled()
            done(v.tensor_scalar(tmp, key, FLOAT_BIT, None, ALU.bitwise_or))
            settled()
            done(v.tensor_scalar(keys_a[:], keys_b[:], signs[:, 0:1], None, ALU.mult))

            cur, other = keys_a[:], keys_b[:]
            for phase in range(1, COL_BITS + 1):
                exchange(cur, other, phase - 1, mirrored=phase > 1)
                cur, other = other, cur
                for bit in range(phase - 2, -1, -1):
                    exchange(cur, other, bit)
                    cur, other = other, cur
            for phase in range(1, PART_BITS + 1):
                settled()
                done(v.tensor_scalar(other, cur, flips[:, phase - 1:phase], None, ALU.mult))
                cur, other = other, cur
                handoffs.append(keys_step.value)
                dve.wait_ge(turned_sbuf.sem, 4 * (2 * phase - 1))
                t_cur, t_other = turned[:], turned_b[:]
                for bit in range(phase - 1, -1, -1):
                    exchange(t_cur, t_other, bit)
                    t_cur, t_other = t_other, t_cur
                handoffs.append(keys_step.value)
                dve.wait_ge(turned_sbuf.sem, 4 * 2 * phase)
                cur, other = keys_a[:], keys_b[:]
                for bit in range(COL_BITS - 1, -1, -1):
                    exchange(cur, other, bit)
                    cur, other = other, cur
            mem["sorted_keys"] = cur
            handoffs.append(keys_step.value)

        local = COL_BITS * (COL_BITS + 1) // 2
        first = [keys_a[:], keys_b[:]]

        def keys_to_turn(phase):
            steps = local + 1 if phase == 1 else COL_BITS + 1
            return first[steps % 2]

        def turned_back(phase):
            return [turned[:], turned_b[:]][phase % 2]

        @block.tensor
        def _(pe):
            pe.wait_ge(ident_done, 1)
            for turn in range(2 * PART_BITS):
                phase = turn // 2 + 1
                src = keys_to_turn(phase) if turn % 2 == 0 else turned_back(phase)
                pe.wait_ge(keys_step.sem, handoffs[turn])
                for bank in range(4):
                    if turn:
                        pe.wait_ge(turned_sbuf.sem, 4 * (turn - 1) + bank + 1)
                    for c in range(4 * bank, 4 * bank + 4):
                        mm = nc.tensor.transpose(psum_keys[:, c * P:(c + 1) * P], src[:, c * P:(c + 1) * P], ident[:])
                    mm.then_inc(*turned_psum.add())

        @block.scalar
        def _(act):
            act.wait_ge(zeros_set, 1)
            cells = dram["counts"].rearrange("(w p c) one -> w p (c one)", w=WINDOWS, p=P)
            for w in range(WINDOWS):
                act.dma_start(cells[w], zeros[:].bitcast(BF16)).then_inc(zero_filled, 16)
            for turn in range(2 * PART_BITS):
                dst = turned if turn % 2 == 0 else keys_a
                for bank in range(4):
                    act.wait_ge(turned_psum.sem, 4 * turn + bank + 1)
                    nc.scalar.activation(dst[:, bank * 512:(bank + 1) * 512], psum_keys[:, bank * 512:(bank + 1) * 512],
                                         ACT.Copy).then_inc(*turned_sbuf.add())
            act.wait_ge(zero_filled, 16 * WINDOWS)

        @block.gpsimd
        def _(pool):
            nc.gpsimd.iota(part[:], [[0, 1]], base=0, channel_multiplier=1).then_inc(iota_done, 1)
            nc.gpsimd.memset(ident[:], 0.0).then_inc(ident_zero, 1)
            pool.wait_ge(ident_zero, 1)
            nc.gpsimd.affine_select(out=ident[:], in_=ident[:], compare_op=ALU.not_equal, fill=1.0, base=0,
                                    pattern=[[-1, P]], channel_multiplier=1).then_inc(ident_done, 1)
            nc.gpsimd.memset(zeros[:], 0.0).then_inc(zeros_set, 1)

        @block.sync
        def _(sp):
            for n, name in enumerate(("dst", "src", "edge_type")):
                sp.dma_start(raw[:, n, :], dram[name]).then_inc(edges_in, 16)
            sp.dma_start(mem["packed"][:], dram["packed"]).then_inc(packed_in, 16)
            sp.wait_ge(keys_step.sem, handoffs[-1])
            sp.dma_start(dram["keys"][1:1 + SORTED].rearrange("(p c) -> p c", p=P), mem["sorted_keys"].bitcast(I32)).then_inc(keys_out, 16)
            sp.dma_start(dram["keys"][0:1].rearrange("(a c) -> a c", a=1), zeros[0:1, 0:1].bitcast(I32)).then_inc(keys_out, 16)
            sp.dma_start(dram["keys"][1 + SORTED:2 + SORTED].rearrange("(a c) -> a c", a=1), zeros[0:1, 0:1].bitcast(I32)).then_inc(keys_out, 16)
            sp.wait_ge(keys_out, 48)
            sp.wait_ge(packed_in, 16)


def work_out_cells(nc, mem, dram):
    with ExitStack() as ctx:
        def sb(name, shape, dt):
            return ctx.enter_context(nc.sbuf_tensor(name, shape, dt))

        def sem(name):
            return ctx.enter_context(nc.semaphore(name))

        around = sb("keys_before_at_after", [P, 3, COLS], I32)
        scratch = [sb(f"scratch_{n}", [P, COLS], I32) for n in range(3)]
        before_cell = sb("before_in_cell", [P, COLS], F32)
        ones = sb("ones", [P, COLS], F32)
        rank = sb("rank_in_cell", [P, COLS], F32)
        through = sb("cell_through", [P, COLS], F32)
        count = sb("count_at_last", [P, COLS], F32)
        rows = sb("carry_rows", [1, 3, P + 1], F32)
        carry = sb("carry_column", [P, 1], F32)

        keys_in = sem("keys_in")
        step = Count(sem("cell_step"))
        rows_turned, carry_turned = sem("rows_turned"), sem("carry_turned")
        index_turned, count_turned = sem("index_turned"), sem("count_turned")
        index_lifted, count_lifted = sem("index_lifted"), sem("count_lifted")
        psum, ident = mem["psum"], mem["ident"]
        marks = {}
        index = scratch[1]

        block = ctx.enter_context(nc.Block())

        @block.vector
        def _(dve):
            v = nc.vector
            prev, key, nxt = (around[:, n, :] for n in range(3))
            a, b, c = (s[:] for s in scratch)

            def done(ins):
                ins.then_inc(*step.add())

            def settled():
                dve.wait_ge(step.sem, step.value)

            done(v.memset(ones[:], 1.0))
            done(v.memset(rows[:], 0.0))
            dve.wait_ge(keys_in, 48)
            done(v.tensor_tensor(a, prev, key, ALU.bitwise_xor))
            done(v.tensor_tensor(b, nxt, key, ALU.bitwise_xor))
            settled()
            done(v.tensor_scalar(c, a, SRC_SHIFT, None, ALU.logical_shift_right))
            settled()
            done(v.tensor_scalar(before_cell[:], c, 0.0, None, ALU.is_equal))
            settled()
            done(v.tensor_tensor_scan(rank[:], before_cell[:], ones[:], 0.0, ALU.mult, ALU.add))
            done(v.tensor_tensor_scan(through[:], before_cell[:], ones[:], 1.0, ALU.mult, ALU.mult))
            marks["scanned"] = step.value
            done(v.tensor_scalar(a, b, SRC_SHIFT, None, ALU.logical_shift_right))
            settled()
            done(v.tensor_scalar(nxt, a, 0.0, None, ALU.is_equal))
            done(v.tensor_scalar(b, key, SRC_SHIFT, NODE_MASK, ALU.logical_shift_right, ALU.bitwise_and))
            done(v.tensor_scalar(c, key, DST_SHIFT + 9, 15, ALU.logical_shift_right, ALU.bitwise_and))
            settled()
            done(v.scalar_tensor_tensor(out=prev, in0=c, scalar=float(ROWS), in1=b, op0=ALU.mult, op1=ALU.add))
            done(v.tensor_scalar(a, key, DST_SHIFT, WIN - 1, ALU.logical_shift_right, ALU.bitwise_and))
            settled()
            done(v.scalar_tensor_tensor(out=b, in0=prev, scalar=9, in1=a,
                                        op0=ALU.logical_shift_left, op1=ALU.bitwise_or))
            settled()
            done(v.scalar_tensor_tensor(out=c, in0=nxt, scalar=OUT_OF_BOUNDS, in1=b,
                                        op0=ALU.logical_shift_left, op1=ALU.bitwise_or))
            settled()
            done(v.tensor_scalar(b, c, FLOAT_BIT, None, ALU.bitwise_or))
            marks["index"] = step.value
            dve.wait_ge(rows_turned, 2)
            done(v.tensor_copy(rows[:, 0, 0:P], psum[0:1, 4, 0:P]))
            done(v.tensor_copy(rows[:, 1, 0:P], psum[0:1, 5, 0:P]))
            settled()
            done(v.tensor_tensor_scan(rows[:, 2, 1:P + 1], rows[:, 1, 0:P], rows[:, 0, 0:P], 0.0, ALU.mult, ALU.add))
            marks["carry_row"] = step.value
            dve.wait_ge(carry_turned, 1)
            done(v.tensor_copy(carry[:], psum[:, 6, 0:1]))
            settled()
            done(v.scalar_tensor_tensor(out=count[:], in0=through[:], scalar=carry[:, 0:1], in1=rank[:],
                                        op0=ALU.mult, op1=ALU.add))
            marks["count"] = step.value
            for bank in range(4):
                dve.wait_ge(index_turned, bank + 1)
                lifted = psum[:, bank, :].bitcast(I32).rearrange("q (b p) -> q p b", p=P)[:, :SLABS, :]
                v.tensor_scalar(mem["cell_index"][:, :, 4 * bank:4 * bank + 4], lifted, FLOAT_BIT - 1, None,
                                ALU.bitwise_and).then_inc(index_lifted, 1)

        @block.tensor
        def _(pe):
            pe.wait_ge(step.sem, marks["scanned"])
            nc.tensor.transpose(psum[0:1, 4, 0:P], rank[:, COLS - 1:COLS], ident[:]).then_inc(rows_turned, 1)
            nc.tensor.transpose(psum[0:1, 5, 0:P], through[:, COLS - 1:COLS], ident[:]).then_inc(rows_turned, 1)
            pe.wait_ge(step.sem, marks["index"])

            def turn(source, turned):
                for b in range(BLOCKS):
                    mm = nc.tensor.transpose(psum[:, b // 4, (b % 4) * P:(b % 4 + 1) * P],
                                             source[:, b * P:(b + 1) * P], ident[:])
                    if b % 4 == 3:
                        mm.then_inc(turned, 1)
                        yield

            for _ in turn(index[:].bitcast(F32), index_turned):
                pass
            pe.wait_ge(step.sem, marks["carry_row"])
            nc.tensor.transpose(psum[:, 6, 0:1], rows[:, 2, 0:P], ident[0:1, 0:1]).then_inc(carry_turned, 1)
            pe.wait_ge(step.sem, marks["count"])
            pe.wait_ge(index_lifted, 4)
            for _ in turn(count, count_turned):
                pass

        @block.scalar
        def _(act):
            for bank in range(4):
                act.wait_ge(count_turned, bank + 1)
                lifted = psum[:, bank, :].rearrange("q (b p) -> q p b", p=P)[:, :SLABS, :]
                nc.scalar.activation(mem["cell_count"][:, :, 4 * bank:4 * bank + 4], lifted, ACT.Copy).then_inc(count_lifted, 1)

        @block.sync
        def _(sp):
            for n in range(3):
                sp.dma_start(around[:, n, :], dram["keys"][n:n + SORTED].rearrange("(p c) -> p c", p=P)).then_inc(keys_in, 16)


def groups():
    return [list(range(g, min(g + 4, TILES))) for g in range(0, TILES, 4)]


def norm_buffers(nc, ctx, name, squares):
    def sb(what, shape):
        return ctx.enter_context(nc.sbuf_tensor(f"{name}_{what}", shape, F32))

    def sem(what):
        return ctx.enter_context(nc.semaphore(f"{name}_{what}"))

    return {"squares": squares, "mean": sb("mean", [P, TILES]),
            "var": sb("var", [P, TILES]), "std": sb("std", [P, TILES]), "scale": sb("scale", [P, TILES]),
            "eps": sb("eps", [P, 1]), "step": Count(sem("norm_step")), "rooted": sem("rooted")}


def norm_first(nc, dve, x, n):
    v, step = nc.vector, n["step"]
    AX = mybir.AxisListType.X

    def done(ins):
        ins.then_inc(*step.add())
        dve.wait_ge(step.sem, step.value)

    done(v.memset(n["eps"][:], 1e-5))
    done(v.tensor_reduce(n["mean"][:], x, AX, ALU.add))
    done(v.tensor_scalar(n["mean"][:], n["mean"][:], 1.0 / FEAT, None, ALU.mult))
    done(v.tensor_tensor(x, x, n["mean"][:].unsqueeze(2).broadcast_to([P, TILES, FEAT]), ALU.subtract))
    done(v.tensor_tensor(n["squares"], x, x, ALU.mult))
    done(v.tensor_reduce(n["var"][:], n["squares"], AX, ALU.add))
    assert step.value == NORM_STEPS


def norm_middle(nc, act, n):
    act.wait_ge(n["step"].sem, NORM_STEPS)
    nc.scalar.activation(n["std"][:], n["var"][:], ACT.Sqrt, bias=n["eps"][:, 0:1],
                         scale=1.0 / FEAT).then_inc(n["rooted"], 1)


def norm_last(nc, dve, x, n, normed):
    v, step = nc.vector, n["step"]
    dve.wait_ge(n["rooted"], 1)
    v.reciprocal(n["scale"][:], n["std"][:]).then_inc(*step.add())
    dve.wait_ge(step.sem, step.value)
    v.tensor_tensor(x, x, n["scale"][:].unsqueeze(2).broadcast_to([P, TILES, FEAT]),
                    ALU.mult).then_inc(normed, 1)


def propagate(nc, mem, dram):
    HALVES = [(0, 25), (25, TILES)]
    with ExitStack() as ctx:
        def sb(name, shape, dt):
            return ctx.enter_context(nc.sbuf_tensor(name, shape, dt))

        def sem(name):
            return ctx.enter_context(nc.semaphore(name))

        counts = sb("counts_window", [P, TILES, WIN], BF16)
        both = counts[:].rearrange("p k c -> p (k c)").bitcast(F32)
        x = both[:, :TILES * FEAT].rearrange("p (k f) -> p k f", f=FEAT)
        squares = both[:, TILES * FEAT:].rearrange("p (k f) -> p k f", f=FEAT)
        parts = [sb(f"m_parts_{n}", [P, TILES, 2, FEAT], F16) for n in range(2)]
        keys2 = parts[1][:].rearrange("p k i f -> p (k i f)").bitcast(I32)
        prev, key = keys2[:, :PER], keys2[:, PER:2 * PER]
        xor, same = keys2[:, 2 * PER:3 * PER], keys2[:, 3 * PER:4 * PER].bitcast(F32)
        ones_row = both[:, :PER]

        index_slots = sb("cell_index_slots", [P, 2, SLAB], I32)
        count_slots = sb("cell_count_slots", [P, 2, SLAB, 1], BF16)
        window = {name: sb(name, [P, WIN], F32) for name in ("sums", "gate_r", "gate_z", "candidate", "difference", "h_fresh")}
        sums, gate_r, gate_z, new, diff, fresh = (window[n] for n in ("sums", "gate_r", "gate_z", "candidate", "difference", "h_fresh"))
        gate_bias = sb("gate_bias", [P, 2], F32)
        norm = norm_buffers(nc, ctx, "encoder", squares)

        low, high = sb("dst_low", [P, PER], BF16), sb("dst_high", [P, PER], BF16)
        iota_f = sb("iota_row", [P, P], F32)
        iota_b = sb("iota_row_bf16", [P, P], BF16)
        hot_low = [sb(f"one_hot_low_{n}", [P, SLAB, P], BF16) for n in range(2)]
        hot_high = [sb(f"one_hot_high_{n}", [P, SLAB, HIGH], BF16) for n in range(2)]
        per_node = sb("edges_per_node", [HIGH, P], F32)
        through_node = sb("edges_through_node", [HIGH, P], F32)
        below = sb("strictly_below", [HIGH, HIGH], F32)
        place_f = sb("last_place", [HIGH, P], F32)
        some = sb("has_edges", [HIGH, P], F32)
        through_row = sb("edges_through_row", [1, HIGH], I32)
        slab_row = sb("slab_of_last_edge", [1, HIGH], I32)
        needed = sb("last_slab_needed", [1, HIGH], I32)
        last_col = sb("edges_through_high", [HIGH, 1], F32)
        part_base = sb("partition_first_place", [P, 1], F32)
        run_in = sb("run_in", [P, 1], F32)
        no_run = sb("no_run_in", [P, 1], F32)

        ones_mat = sb("ones_matrix", [P, P], F32)
        abs_conv = sb("abs_conv", [P, STEPS, FEAT], F32)
        reach = sb("h_reach", [P, 4], F32)
        top = sb("h_reach_row", [1, 2], F32)
        bound = sb("m_bound", [P, STEPS], F32)
        exponent = sb("m_exponent", [P, STEPS], I32)
        scale = sb("m_scale", [P, STEPS], I32)
        unscale = sb("m_unscale", [P, STEPS], I32)
        conv = sb("conv_scaled", [P, STEPS, FEAT], F32)

        copied, landed = sem("cell_copied"), [sem("cells_landed_0"), sem("cells_landed_1")]
        slabs_landed = sem("slabs_landed")
        x_in, keys_in = sem("x_in"), sem("keys_again_in")
        normed, turned, lifted = sem("x_normed"), sem("x_turned"), sem("x_lifted")
        pre1, act1, pre2, act2 = sem("enc_pre1"), sem("enc_act1"), sem("enc_pre2"), sem("enc_act2")
        iotas, consts = sem("iotas"), sem("propagate_constants")
        key_step = Count(sem("key_step"))
        hot_done, hot_used = sem("one_hots_done"), sem("one_hots_used")
        node_step, node_turned = Count(sem("node_step")), sem("node_turned")
        scale_step, scale_turned, abs_done = Count(sem("scale_step")), sem("scale_turned"), sem("abs_conv_done")
        needed_done = sem("slabs_needed_done")
        loaded = [sem("counts_loaded_0"), sem("counts_loaded_1")]
        half_done = [sem("sums_half_0"), sem("sums_half_1")]
        m_done, high_done, low_done = sem("m_product"), sem("m_high"), sem("m_low")
        sums_copied = sem("sums_copied")
        gates_done, gates_acted = sem("gates_done"), sem("gates_acted")
        cand_step, cand_pre, cand_done = sem("candidate_step"), sem("candidate_pre"), sem("candidate_done")
        h_done, h_copied = sem("h_done"), sem("h_copied")
        psum, ident, h, w = mem["psum"], mem["ident"], mem["h"], mem["weight"]
        G = len(groups())
        assert G == WINDOWS
        SUMS, M, R, Z, IN, HN, HIST, SPARE = range(8)
        marks = {}
        wins = [(n * WIN, WIN) for n in range(FULL_WINDOWS)] + [(FULL_WINDOWS * WIN, LAST)]

        def steps_of(engine, first, body):
            for t in range(STEPS):
                first(t)
                if t == 0:
                    body(0, 1, WIN)
                with engine.Fori(2 if t == 0 else 1, FULL_WINDOWS) as n:
                    body(t, n, WIN)
                body(t, FULL_WINDOWS, LAST)
            first(STEPS)

        def later(t, n):
            return t > 0 or not isinstance(n, int) or n > 0

        def at(n, width):
            return bass.ds(n * WIN, width)

        block = ctx.enter_context(nc.Block())

        @block.gpsimd
        def _(pool):
            nc.gpsimd.iota(iota_f[:], [[1, P]], base=0, channel_multiplier=0,
                           allow_small_or_imprecise_dtypes=True).then_inc(iotas, 1)
            nc.gpsimd.iota(part_base[:], [[0, 1]], base=-1, channel_multiplier=PER,
                           allow_small_or_imprecise_dtypes=True).then_inc(iotas, 1)
            nc.gpsimd.memset(below[:], 1.0).then_inc(iotas, 1)
            pool.wait_ge(iotas, 3)
            nc.gpsimd.affine_select(out=below[:], in_=below[:], compare_op=ALU.is_gt, fill=0.0, base=0,
                                    pattern=[[1, HIGH]], channel_multiplier=-1).then_inc(iotas, 1)

            def slab(pair, slot, again):
                if again:
                    pool.wait_ge(landed[slot], pair * (16 * SLAB))
                    pool.sem_inc(slabs_landed, 1)
                at_slab = bass.ds(pair * 2 + slot, 1)
                nc.gpsimd.tensor_copy(index_slots[:, slot, :].unsqueeze(1), mem["cell_index"][:, at_slab, :]).then_inc(copied, 1)
                nc.gpsimd.tensor_copy(count_slots[:, slot, :, 0].unsqueeze(1), mem["cell_count"][:, at_slab, :]).then_inc(copied, 1)
                pool.wait_ge(copied, pair * 4 + (2 * slot + 2))
                held.take()
                for j in range(SLAB):
                    nc.gpsimd.indirect_dma_start(
                        out=dram["counts"], out_offset=bass.IndirectOffsetOnAxis(ap=index_slots[:, slot, j:j + 1], axis=0),
                        in_=count_slots[:, slot, j], in_offset=None,
                        bounds_check=COUNT_CELLS - 1, oob_is_err=False).then_inc(landed[slot], 16)

            held = WaitHolder(nc, ctx, pool, "slab_turns")
            for slot in range(2):
                slab(0, slot, False)
            with pool.Fori(1, SLABS // 2) as pair:
                for slot in range(2):
                    slab(pair, slot, True)
            for slot in range(2):
                pool.wait_ge(landed[slot], 16 * SLAB * (SLABS // 2))
                pool.sem_inc(slabs_landed, 1)

        @block.sync
        def _(sp):
            sp.dma_start(x, dram["x"].rearrange("(k p) f -> p k f", p=P)).then_inc(x_in, 16)
            for n, to in enumerate((prev, key)):
                sp.dma_start(to, dram["keys"][n:n + P * PER].rearrange("(p c) -> p c", p=P)).then_inc(keys_in, 16)
            cells = dram["counts"].rearrange("(w k p c) one -> w p k (c one)", w=WINDOWS, p=P, c=WIN)

            def load(t, n, width):
                for half, (a, b) in enumerate(HALVES):
                    if later(t, n):
                        sp.wait_ge(half_done[half], n + t * WINDOWS)
                    src = cells[n] if isinstance(n, int) else cells[bass.ds(n, 1)].rearrange("w p k c -> (w p) k c")
                    sp.dma_start(counts[:, a:b, :width], src[:, a:b, :width]).then_inc(loaded[half], 16)

            sp.wait_ge(lifted, G)
            sp.wait_ge(key_step.sem, KEY_STEPS)
            sp.wait_ge(needed_done, 1)
            for n, (_, width) in enumerate(wins):
                sp.wait_ge(slabs_landed, sp.value_load(needed[0:1, 4 * n + 3:4 * n + 4], min_val=0, max_val=SLABS - 1) + 1)
                load(0, n, width)
            for t in range(1, STEPS):
                with sp.Fori(0, FULL_WINDOWS) as n:
                    load(t, n, WIN)
                load(t, FULL_WINDOWS, LAST)

        @block.tensor
        def _(pe):
            mm = nc.tensor.matmul
            pe.wait_ge(normed, 1)
            for g, tiles in enumerate(groups()):
                if g >= 2:
                    pe.wait_ge(lifted, g - 1)
                for i, k in enumerate(tiles):
                    last = nc.tensor.transpose(psum[:, g % 2, i * P:(i + 1) * P], x[:, k, :], ident[:])
                last.then_inc(turned, 1)
            pe.wait_ge(lifted, G)
            for n, (a, width) in enumerate(wins):
                if n:
                    pe.wait_ge(act1, n)
                mm(psum[:, 2, :width], w("enc_w1"), h[:, a:a + width], start=True, stop=True).then_inc(pre1, 1)
                pe.wait_ge(act1, n + 1)
                if n:
                    pe.wait_ge(act2, n)
                mm(psum[:, 3, :width], w("enc_w2"), diff[:, :width], start=True, stop=True).then_inc(pre2, 1)
            pe.wait_ge(act1, WINDOWS)
            pe.wait_ge(act2, WINDOWS)
            pe.wait_ge(abs_done, 1)
            pe.wait_ge(consts, 2)
            mm(psum[:, R, :4 * FEAT], ones_mat[:], abs_conv[:, :4, :], start=True, stop=True).then_inc(scale_turned, 1)
            mm(psum[:, Z, :FEAT], ones_mat[:], abs_conv[:, 4, :], start=True, stop=True).then_inc(scale_turned, 1)
            pe.wait_ge(scale_step.sem, REACH_STEP)
            nc.tensor.transpose(psum[0:1, SPARE, 0:P], reach[:, 3:4], ident[:]).then_inc(scale_turned, 1)
            pe.wait_ge(scale_step.sem, TOP_STEP)
            mm(psum[:, SPARE, 0:1], ones_mat[0:1, :], top[:, 0:1], start=True, stop=True).then_inc(scale_turned, 1)
            pe.wait_ge(scale_step.sem, SCALE_STEPS)
            for g, tiles in enumerate(groups()):
                if g:
                    pe.wait_ge(low_done, g)
                for i, k in enumerate(tiles):
                    last = mm(psum[:, M, i * P:(i + 1) * P], h[:, k * P:(k + 1) * P], conv[:, 0, :], start=True, stop=True)
                last.then_inc(m_done, 1)
            for s in range(2):
                pe.wait_ge(hot_done, 2 * s + 2)
                for j in range(SLAB):
                    last = mm(psum[0:HIGH, HIST, 0:P], hot_high[s][:, j, :], hot_low[s][:, j, :],
                              start=(s == 0 and j == 0), stop=False, skip_group_check=True)
                last.then_inc(hot_used, 1)
            with pe.Fori(1, SLABS // 2) as pair:
                for s in range(2):
                    pe.wait_ge(hot_done, pair * 4 + (2 * s + 2))
                    for j in range(SLAB):
                        last = mm(psum[0:HIGH, HIST, 0:P], hot_high[s][:, j, :], hot_low[s][:, j, :],
                                  start=False, stop=False, skip_group_check=True)
                    last.then_inc(hot_used, 1)
            pe.wait_ge(node_step.sem, THROUGH_STEP)
            mm(psum[0:HIGH, SPARE, 0:1], below[:], last_col[:], start=True, stop=True).then_inc(node_turned, 1)
            pe.wait_ge(node_step.sem, PLACE_STEP)
            nc.tensor.transpose(psum[:, SPARE, 0:HIGH], place_f[:], ident[0:HIGH, 0:HIGH]).then_inc(node_turned, 1)
            pe.wait_ge(node_step.sem, PLACE_STEP + 1)
            nc.tensor.transpose(psum[0:1, HIST, 0:HIGH], last_col[:], ident[0:HIGH, 0:HIGH]).then_inc(node_turned, 1)

            def half(t, n, width, which):
                g = n + t * WINDOWS
                if which == 0 and later(t, n):
                    pe.wait_ge(sums_copied, g)
                if isinstance(n, int) and n == 0:
                    pe.wait_ge(low_done, t * G + (7 if which == 0 else G))
                pe.wait_ge(loaded[which], g * 16 + 16)
                a, b = HALVES[which]
                for k in range(a, b):
                    for i in range(2):
                        last = mm(psum[:, SUMS, :width], parts[t % 2][:, k, i, :], counts[:, k, :width],
                                  start=(k == 0 and i == 0), stop=(k == TILES - 1 and i == 1))
                last.then_inc(half_done[which], 1)

            def gates(t, n, width):
                g = n + t * WINDOWS
                pe.wait_ge(sums_copied, g + 1)
                if later(t, n):
                    pe.wait_ge(h_done, g)
                if t:
                    pe.wait_ge(h_copied, g - (WINDOWS - 1))
                hw = h[:, at(n, width)]
                for bank, gate in ((R, 0), (Z, 1)):
                    mm(psum[:, bank, :width], w("wih", gate), sums[:, :width], start=True, stop=False)
                    mm(psum[:, bank, :width], w("whh", gate), hw, start=False, stop=True)
                mm(psum[:, IN, :width], w("wih", 2), sums[:, :width], start=True, stop=True)
                mm(psum[:, HN, :width], w("whh", 2), hw, start=True, stop=True).then_inc(gates_done, 1)

            def next_m(t, n, width):
                if t == STEPS - 1:
                    return
                g = n + t * WINDOWS
                pe.wait_ge(h_done, g + 1)
                pe.wait_ge(low_done, g + G)
                for i in range(width // P):
                    last = mm(psum[:, M, i * P:(i + 1) * P], fresh[:, i * P:(i + 1) * P], conv[:, t + 1, :], start=True, stop=True)
                last.then_inc(m_done, 1)

            def first(t):
                if t < STEPS:
                    half(t, 0, WIN, 0)
                if t:
                    gates(t - 1, FULL_WINDOWS, LAST)
                    next_m(t - 1, FULL_WINDOWS, LAST)
                if t < STEPS:
                    half(t, 0, WIN, 1)

            def body(t, n, width):
                half(t, n, width, 0)
                gates(t, n - 1, WIN)
                half(t, n, width, 1)
                next_m(t, n - 1, WIN)

            steps_of(pe, first, body)

        @block.scalar
        def _(act):
            A = nc.scalar.activation
            A(abs_conv[:].rearrange("p t f -> p (t f)"), w.wide("conv", 0, STEPS * FEAT), ACT.Abs).then_inc(abs_done, 1)
            norm_middle(nc, act, norm)
            for g, tiles in enumerate(groups()):
                act.wait_ge(turned, g + 1)
                A(h[:, tiles[0] * P:(tiles[-1] + 1) * P], psum[:, g % 2, :len(tiles) * P], ACT.Relu).then_inc(lifted, 1)
            for n, (a, width) in enumerate(wins):
                act.wait_ge(pre1, n + 1)
                if n:
                    act.wait_ge(pre2, n)
                A(diff[:, :width], psum[:, 2, :width], ACT.Relu, bias=w("enc_b1")).then_inc(act1, 1)
                act.wait_ge(pre2, n + 1)
                A(h[:, a:a + width], psum[:, 3, :width], ACT.Identity, bias=w("enc_b2")).then_inc(act2, 1)

            def m_high(to, tile, n, g):
                act.wait_ge(m_done, g + 1)
                A(to[:, tile, 0, :], psum[:, M, :n * P].rearrange("p (k f) -> p k f", f=FEAT), ACT.Copy).then_inc(high_done, 1)

            for g, tiles in enumerate(groups()):
                m_high(parts[0], slice(tiles[0], tiles[-1] + 1), len(tiles), g)
            act.wait_ge(consts, 2)
            act.wait_ge(scale_step.sem, SCALE_STEPS)

            def lift_sums(t, n, width):
                g = n + t * WINDOWS
                act.wait_ge(half_done[1], g + 1)
                if later(t, n):
                    act.wait_ge(gates_done, g)
                A(sums[:, :width], psum[:, SUMS, :width], ACT.Copy, scale=unscale[:, t:t + 1].bitcast(F32)).then_inc(sums_copied, 1)

            def cell(t, n, width):
                g = n + t * WINDOWS
                act.wait_ge(gates_done, g + 1)
                if later(t, n):
                    act.wait_ge(h_done, g)
                A(gate_r[:, :width], psum[:, R, :width], ACT.Sigmoid, bias=gate_bias[:, 0:1]).then_inc(gates_acted, 1)
                A(gate_z[:, :width], psum[:, Z, :width], ACT.Sigmoid, bias=gate_bias[:, 1:2]).then_inc(gates_acted, 1)
                act.wait_ge(cand_pre, g + 1)
                A(new[:, :width], diff[:, :width], ACT.Tanh, bias=w("bih", 2)).then_inc(cand_done, 1)
                act.wait_ge(h_done, g + 1)
                A(h[:, at(n, width)], fresh[:, :width], ACT.Copy).then_inc(h_copied, 1)

            def high(t, n, width):
                if t < STEPS - 1:
                    m_high(parts[(t + 1) % 2], bass.ds(n * 4, width // P), width // P, n + (t + 1) * WINDOWS)

            def first(t):
                if t:
                    cell(t - 1, FULL_WINDOWS, LAST)
                    high(t - 1, FULL_WINDOWS, LAST)
                if t < STEPS:
                    lift_sums(t, 0, WIN)

            def body(t, n, width):
                cell(t, n - 1, WIN)
                lift_sums(t, n, width)
                high(t, n - 1, WIN)

            steps_of(act, first, body)

        @block.vector
        def _(dve):
            v = nc.vector
            AX = mybir.AxisListType.X
            v.memset(ones_mat[:], 1.0).then_inc(consts, 1)
            v.tensor_tensor(gate_bias[:], w.wide("bih", 0, 2), w.wide("bhh", 0, 2), ALU.add).then_inc(consts, 1)
            dve.wait_ge(x_in, 16)
            norm_first(nc, dve, x, norm)
            norm_last(nc, dve, x, norm, normed)

            def done(ins, count=key_step):
                ins.then_inc(*count.add())

            def settled(count=key_step):
                dve.wait_ge(count.sem, count.value)

            dve.wait_ge(iotas, 4)
            done(v.tensor_copy(iota_b[:], iota_f[:]))
            dve.wait_ge(keys_in, 32)
            done(v.tensor_tensor(xor, prev, key, ALU.bitwise_xor))
            settled()
            done(v.tensor_scalar(prev, xor, DST_SHIFT, None, ALU.logical_shift_right))
            settled()
            done(v.tensor_scalar(same, prev, 0.0, None, ALU.is_equal))
            dve.wait_ge(turned, G)
            done(v.memset(ones_row, 1.0))
            settled()
            done(v.tensor_tensor_scan(xor.bitcast(F32), same, ones_row, 1.0, ALU.mult, ALU.mult))
            done(v.tensor_scalar(mem["cap"][:], same, -2.0, 1.0, ALU.mult, ALU.add))
            settled()
            done(v.tensor_scalar(mem["cap"][:], mem["cap"][:], LOWEST, None, ALU.mult))
            done(v.tensor_copy(mem["all_through"][:], xor.bitcast(F32)[:, PER - 1:PER]))
            done(v.tensor_reduce(run_in[:], xor.bitcast(F32), AX, ALU.add))
            settled()
            done(v.tensor_scalar(no_run[:], run_in[:], 0.0, float(1 << 25), ALU.is_equal, ALU.mult))
            done(v.tensor_scalar(run_in[:], run_in[:], part_base[:, 0:1], None, ALU.add))
            settled()
            done(v.tensor_tensor(mem["run_in_end"][:], run_in[:], no_run[:], ALU.add))
            done(v.tensor_scalar(mem["table_index"][:], key, (1 << DST_SHIFT) - 1, None, ALU.bitwise_and))
            done(v.tensor_scalar(prev, key, DST_SHIFT, P - 1, ALU.logical_shift_right, ALU.bitwise_and))
            done(v.tensor_scalar(xor, key, DST_SHIFT + 7, HIGH - 1, ALU.logical_shift_right, ALU.bitwise_and))
            settled()
            done(v.tensor_copy(low[:], prev))
            done(v.tensor_copy(high[:], xor))
            settled()
            assert key_step.value == KEY_STEPS

            def sdone(ins):
                done(ins, scale_step)

            def ssettled():
                settled(scale_step)

            dve.wait_ge(act2, WINDOWS)
            sdone(v.tensor_reduce(reach[:, 0:1], h[:], AX, ALU.max))
            sdone(v.tensor_reduce(reach[:, 1:2], h[:], AX, ALU.min))
            ssettled()
            sdone(v.tensor_scalar(reach[:, 2:3], reach[:, 1:2], -1.0, 1.0, ALU.mult, ALU.max))
            ssettled()
            sdone(v.tensor_tensor(reach[:, 3:4], reach[:, 0:1], reach[:, 2:3], ALU.max))
            assert scale_step.value == REACH_STEP
            dve.wait_ge(scale_turned, 3)
            sdone(v.tensor_reduce(top[:, 0:1], psum[0:1, SPARE, 0:P], AX, ALU.max))
            assert scale_step.value == TOP_STEP
            sdone(v.tensor_reduce(bound[:, 0:4], psum[:, R, :].rearrange("p (t f) -> p t f", f=FEAT), AX, ALU.max))
            sdone(v.tensor_reduce(bound[:, 4:5], psum[:, Z, :FEAT], AX, ALU.max))
            ssettled()
            dve.wait_ge(scale_turned, 4)
            sdone(v.tensor_scalar(bound[:], bound[:], psum[:, SPARE, 0:1], None, ALU.mult))
            ssettled()
            sdone(v.tensor_scalar(bound[:], bound[:], 1e-30, 1e36, ALU.max, ALU.min))
            ssettled()
            sdone(v.tensor_scalar(exponent[:], bound[:].bitcast(I32), 0x7F800000, None, ALU.bitwise_and))
            ssettled()
            sdone(v.tensor_scalar(scale[:], exponent[:], -1.0, float(266 << 23), ALU.mult, ALU.add))
            sdone(v.tensor_scalar(unscale[:], exponent[:], float(12 << 23), None, ALU.subtract))
            ssettled()
            for t in range(STEPS):
                sdone(v.tensor_scalar(conv[:, t, :], w("conv", t), scale[:, t:t + 1].bitcast(F32), None, ALU.mult))
            assert scale_step.value == SCALE_STEPS

            def m_low(to, tile, n, g):
                dve.wait_ge(high_done, g + 1)
                v.tensor_tensor(to[:, tile, 1, :], psum[:, M, :n * P].rearrange("p (k f) -> p k f", f=FEAT),
                                to[:, tile, 0, :], ALU.subtract).then_inc(low_done, 1)

            for g, tiles in enumerate(groups()):
                m_low(parts[0], slice(tiles[0], tiles[-1] + 1), len(tiles), g)

            def hot(s, columns):
                v.tensor_tensor(hot_low[s][:], iota_b[:].unsqueeze(1).broadcast_to([P, SLAB, P]),
                                low[:, columns].unsqueeze(2).broadcast_to([P, SLAB, P]), ALU.is_equal).then_inc(hot_done, 1)
                v.tensor_tensor(hot_high[s][:], iota_b[:, :HIGH].unsqueeze(1).broadcast_to([P, SLAB, HIGH]),
                                high[:, columns].unsqueeze(2).broadcast_to([P, SLAB, HIGH]), ALU.is_equal).then_inc(hot_done, 1)

            for s in range(2):
                hot(s, slice(s * SLAB, (s + 1) * SLAB))
            with dve.Fori(1, SLABS // 2) as pair:
                for s in range(2):
                    dve.wait_ge(hot_used, pair * 2 + (s - 1))
                    hot(s, bass.ds(pair * (2 * SLAB) + s * SLAB, SLAB))

            def ndone(ins):
                done(ins, node_step)

            def nsettled():
                settled(node_step)

            dve.wait_ge(hot_used, SLABS)
            ndone(v.tensor_copy(per_node[:], psum[0:HIGH, HIST, 0:P]))
            nsettled()
            ndone(v.memset(place_f[:], 1.0))
            nsettled()
            ndone(v.tensor_tensor_scan(through_node[:], place_f[:], per_node[:], 0.0, ALU.mult, ALU.add))
            nsettled()
            ndone(v.tensor_copy(last_col[:], through_node[:, P - 1:P]))
            assert node_step.value == THROUGH_STEP
            ndone(v.tensor_scalar(some[:], per_node[:], 0.0, None, ALU.is_gt))
            dve.wait_ge(node_turned, 1)
            ndone(v.tensor_copy(no_run[0:HIGH], psum[0:HIGH, SPARE, 0:1]))
            nsettled()
            ndone(v.tensor_scalar(place_f[:], through_node[:], no_run[0:HIGH, 0:1], float(-1 - NO_EDGE_ROW), ALU.add, ALU.add))
            nsettled()
            ndone(v.tensor_tensor(place_f[:], place_f[:], some[:], ALU.mult))
            nsettled()
            ndone(v.tensor_scalar(place_f[:], place_f[:], float(NO_EDGE_ROW), None, ALU.add))
            assert node_step.value == PLACE_STEP
            ndone(v.tensor_tensor(last_col[:], last_col[:], no_run[0:HIGH], ALU.add))
            dve.wait_ge(node_turned, 2)
            ndone(v.tensor_copy(mem["node_place"][:], psum[:, SPARE, 0:TILES]))
            dve.wait_ge(node_turned, 3)
            ndone(v.tensor_copy(through_row[:], psum[0:1, HIST, 0:HIGH]))
            nsettled()
            ndone(v.tensor_scalar(slab_row[:], through_row[:], COL_BITS, None, ALU.logical_shift_right))
            nsettled()
            v.tensor_scalar(needed[:], slab_row[:], float(SLABS - 1), None, ALU.min).then_inc(needed_done, 1)

            def cell(t, n, width):
                g = n + t * WINDOWS
                hw = h[:, at(n, width)]
                dve.wait_ge(gates_acted, g * 2 + 2)
                v.scalar_tensor_tensor(out=diff[:, :width], in0=psum[:, HN, :width], scalar=w("bhh", 2),
                                       in1=gate_r[:, :width], op0=ALU.add, op1=ALU.mult).then_inc(cand_step, 1)
                dve.wait_ge(cand_step, g * 3 + 1)
                v.tensor_tensor(diff[:, :width], diff[:, :width], psum[:, IN, :width], ALU.add).then_inc(cand_pre, 1)
                dve.wait_ge(cand_done, g + 1)
                v.tensor_tensor(diff[:, :width], hw, new[:, :width], ALU.subtract).then_inc(cand_step, 1)
                dve.wait_ge(cand_step, g * 3 + 2)
                v.tensor_tensor(diff[:, :width], diff[:, :width], gate_z[:, :width], ALU.mult).then_inc(cand_step, 1)
                dve.wait_ge(cand_step, g * 3 + 3)
                if later(t, n):
                    dve.wait_ge(h_copied, g)
                    dve.wait_ge(m_done, g + G if t < STEPS - 1 else STEPS * G)
                v.tensor_tensor(fresh[:, :width], diff[:, :width], new[:, :width], ALU.add).then_inc(h_done, 1)

            def low_part(t, n, width):
                if t < STEPS - 1:
                    m_low(parts[(t + 1) % 2], bass.ds(n * 4, width // P), width // P, n + (t + 1) * WINDOWS)

            def first(t):
                if t:
                    cell(t - 1, FULL_WINDOWS, LAST)
                    low_part(t - 1, FULL_WINDOWS, LAST)

            def body(t, n, width):
                cell(t, n - 1, WIN)
                low_part(t, n - 1, WIN)

            steps_of(dve, first, body)


def decode_and_table(nc, mem, dram):
    with ExitStack() as ctx:
        def sb(name, shape, dt):
            return ctx.enter_context(nc.sbuf_tensor(name, shape, dt))

        def sem(name):
            return ctx.enter_context(nc.semaphore(name))

        hidden = sb("decoder_hidden", [P, WIN], F32)
        decoded = sb("decoded", [P, 2, WIN], F32)
        y = sb("second_norm", [P, TILES, FEAT], F32)
        squares = sb("second_squares", [P, TILES, FEAT], F32)
        norm = norm_buffers(nc, ctx, "second", squares[:])
        table = sb("table_rows", [P, 2, RELS * FEAT], F32)
        rel_bias = sb("relation_bias", [P, (RELS + 1) * FEAT], F32)
        x_in, bias_in = sem("x_again_in"), sem("relation_bias_in")
        h_relu = sem("h_relu")
        pre1, act1, pre2, act2 = sem("dec_pre1"), sem("dec_act1"), sem("dec_pre2"), sem("dec_act2")
        back, added = sem("turned_back"), sem("residual_added")
        y_copied, normed, turned, lifted = sem("y_copied"), sem("y_normed"), sem("y_turned"), sem("y_lifted")
        rows_done, rows_biased, rows_out = sem("rows_done"), sem("rows_biased"), [sem("rows_out_0"), sem("rows_out_1")]
        psum, ident, h, w = mem["psum"], mem["ident"], mem["h"], mem["weight"]
        x1, base = mem["x1"], mem["base"]
        wins = [(n * WIN, WIN) for n in range(FULL_WINDOWS)] + [(FULL_WINDOWS * WIN, LAST)]
        HALF = RELS * FEAT // 2

        block = ctx.enter_context(nc.Block())

        @block.sync
        def _(sp):
            sp.dma_start(x1[:], dram["x"].rearrange("(k p) f -> p k f", p=P)).then_inc(x_in, 16)
            sp.dma_start(rel_bias[:], dram["rel_bias"].broadcast_to([P, (RELS + 1) * FEAT])).then_inc(bias_in, 16)
            rows = dram["table"].rearrange("(k p r) f -> k p (r f)", p=P, r=RELS)
            for k in range(TILES):
                sp.wait_ge(rows_biased, 3 * k + 2)
                sp.dma_start(rows[k], table[:, k % 2, :]).then_inc(rows_out[k % 2], 16)
            sp.wait_ge(rows_out[0], 16 * (TILES - TILES // 2))
            sp.wait_ge(rows_out[1], 16 * (TILES // 2))

        @block.tensor
        def _(pe):
            for n, (at, width) in enumerate(wins):
                pe.wait_ge(h_relu, n + 1)
                if n:
                    pe.wait_ge(act1, n)
                nc.tensor.matmul(psum[:, 0, :width], w("dec_w1"), h[:, at:at + width], start=True, stop=True).then_inc(pre1, 1)
                pe.wait_ge(act1, n + 1)
                if n:
                    pe.wait_ge(act2, n)
                nc.tensor.matmul(psum[:, 1, :width], w("dec_w2"), hidden[:, :width], start=True, stop=True).then_inc(pre2, 1)
                pe.wait_ge(act2, n + 1)
                if n >= 2:
                    pe.wait_ge(added, n - 1)
                for i in range(width // P):
                    mm = nc.tensor.transpose(psum[:, 2 + n % 2, i * P:(i + 1) * P], decoded[:, n % 2, i * P:(i + 1) * P], ident[:])
                mm.then_inc(back, 1)
            pe.wait_ge(normed, 1)
            for g, tiles in enumerate(groups()):
                if g >= 2:
                    pe.wait_ge(lifted, g - 1)
                for i, k in enumerate(tiles):
                    mm = nc.tensor.transpose(psum[:, g % 2, i * P:(i + 1) * P], y[:, k, :], ident[:])
                mm.then_inc(turned, 1)
            pe.wait_ge(added, len(wins))
            for k in range(TILES):
                if k % 4 == 0:
                    pe.wait_ge(lifted, k // 4 + 1)
                banks = (2, 3, 4) if k % 2 == 0 else (5, 6, 7)
                if k >= 2:
                    pe.wait_ge(rows_biased, 3 * (k - 1))
                lhs = h[:, k * P:(k + 1) * P]
                nc.tensor.matmul(psum[:, banks[0], :], lhs, w.wide("rel", 0, HALF), start=True, stop=True)
                nc.tensor.matmul(psum[:, banks[1], :], lhs, w.wide("rel", HALF, HALF), start=True, stop=True)
                nc.tensor.matmul(psum[:, banks[2], :FEAT], lhs, w.wide("rel", 2 * HALF, FEAT), start=True, stop=True).then_inc(rows_done, 1)

        @block.scalar
        def _(act):
            for n, (at, width) in enumerate(wins):
                nc.scalar.activation(h[:, at:at + width], h[:, at:at + width], ACT.Relu).then_inc(h_relu, 1)
            for n, (at, width) in enumerate(wins):
                act.wait_ge(pre1, n + 1)
                if n:
                    act.wait_ge(pre2, n)
                nc.scalar.activation(hidden[:, :width], psum[:, 0, :width], ACT.Relu, bias=w("dec_b1")).then_inc(act1, 1)
                act.wait_ge(pre2, n + 1)
                if n >= 2:
                    act.wait_ge(back, n - 1)
                nc.scalar.activation(decoded[:, n % 2, :width], psum[:, 1, :width], ACT.Sigmoid, bias=w("dec_b2")).then_inc(act2, 1)
            norm_middle(nc, act, norm)
            for g, tiles in enumerate(groups()):
                act.wait_ge(turned, g + 1)
                nc.scalar.activation(h[:, tiles[0] * P:(tiles[-1] + 1) * P], psum[:, g % 2, :len(tiles) * P],
                                     ACT.Relu).then_inc(lifted, 1)

        @block.vector
        def _(dve):
            v = nc.vector
            dve.wait_ge(x_in, 16)
            for n, (at, width) in enumerate(wins):
                dve.wait_ge(back, n + 1)
                tiles = x1[:, 4 * n:4 * n + width // P, :]
                v.tensor_tensor(tiles, tiles, psum[:, 2 + n % 2, :width].rearrange("p (k f) -> p k f", f=FEAT), ALU.add).then_inc(added, 1)
            dve.wait_ge(added, len(wins))
            v.tensor_copy(y[:], x1[:]).then_inc(y_copied, 1)
            dve.wait_ge(y_copied, 1)
            norm_first(nc, dve, y[:], norm)
            norm_last(nc, dve, y[:], norm, normed)
            dve.wait_ge(bias_in, 16)
            for k in range(TILES):
                banks = (2, 3, 4) if k % 2 == 0 else (5, 6, 7)
                dve.wait_ge(rows_done, k + 1)
                if k >= 2:
                    dve.wait_ge(rows_out[k % 2], 16 * (k // 2))
                for half in range(2):
                    v.tensor_tensor(table[:, k % 2, half * HALF:(half + 1) * HALF], psum[:, banks[half], :],
                                    rel_bias[:, half * HALF:(half + 1) * HALF], ALU.add).then_inc(rows_biased, 1)
                v.tensor_tensor(base[:, k, :], psum[:, banks[2], :FEAT], rel_bias[:, 2 * HALF:], ALU.add).then_inc(rows_biased, 1)


def running_maximum(nc, mem, dram):
    with ExitStack() as ctx:
        def sb(name, shape, dt):
            return ctx.enter_context(nc.sbuf_tensor(name, shape, dt))

        def sem(name):
            return ctx.enter_context(nc.semaphore(name))

        index_slots = sb("table_index_slots", [P, 2, SLAB], I32)
        cap_slots = sb("cap_slots", [P, 2, SLAB], F32)
        rows = sb("gathered", [P, 2, SLAB, FEAT], F32)
        best = sb("best", [P, 2, SLAB, FEAT], F32)
        zero_row = sb("zero_row", [1, FEAT], F32)
        spread = sb("all_through_spread", [P, P], F32)
        keep = sb("keep", [P, P], F32)
        last = sb("last_turned", [P, P], F32)
        joined = sb("joined", [P, P + 1], F32)
        fixed = sb("run_in_maxima", [P, FEAT], F32)
        copied = sem("table_index_copied")
        slot_read = [sem("gathered_read_0"), sem("gathered_read_1")]
        gathered = [sem("gathered_0"), sem("gathered_1")]
        consts = sem("max_constants")
        masks, step = sem("cap_copied"), sem("max_step")
        written = [sem("best_written_0"), sem("best_written_1")]
        zero_out = sem("zero_row_out")
        fix_read, fix_written = sem("run_in_read"), sem("run_in_written")
        join_step, join_turned = sem("join_step"), sem("join_turned")
        psum, ident = mem["psum"], mem["ident"]
        CONSTS, JOINED = 5, 6

        block = ctx.enter_context(nc.Block())

        @block.gpsimd
        def _(pool):
            held = WaitHolder(nc, ctx, pool, "gather_turns")

            def gather(pair, slot, again):
                if again:
                    pool.wait_ge(slot_read[slot], pair)
                nc.gpsimd.tensor_copy(index_slots[:, slot, :],
                                      mem["table_index"][:, bass.ds(pair * (2 * SLAB) + slot * SLAB, SLAB)]).then_inc(copied, 1)
                pool.wait_ge(copied, pair * 2 + (slot + 1))
                held.take()
                for j in range(SLAB):
                    nc.gpsimd.indirect_dma_start(
                        out=rows[:, slot, j, :], out_offset=None, in_=dram["table"],
                        in_offset=bass.IndirectOffsetOnAxis(ap=index_slots[:, slot, j:j + 1], axis=0)).then_inc(gathered[slot], 16)

            for slot in range(2):
                gather(0, slot, False)
            with pool.Fori(1, SLABS // 2) as pair:
                for slot in range(2):
                    gather(pair, slot, True)
            for slot in range(2):
                pool.wait_ge(written[slot], 16 * (SLABS // 2))
            pool.wait_ge(consts, CONSTS)
            where = bass.IndirectOffsetOnAxis(ap=mem["run_in_end"][:, 0:1], axis=0)
            nc.gpsimd.indirect_dma_start(out=fixed[:], out_offset=None, in_=dram["maxima"], in_offset=where,
                                         bounds_check=NO_EDGE_ROW, oob_is_err=False).then_inc(fix_read, 16)
            pool.wait_ge(join_step, JOINED)
            nc.gpsimd.indirect_dma_start(out=dram["maxima"], out_offset=where, in_=fixed[:], in_offset=None,
                                         bounds_check=NO_EDGE_ROW, oob_is_err=False).then_inc(fix_written, 16)
            pool.wait_ge(fix_written, 16)

        @block.vector
        def _(dve):
            v = nc.vector
            v.memset(best[:, 1, SLAB - 1, :], LOWEST).then_inc(consts, 1)
            v.memset(joined[:, 0:1], LOWEST).then_inc(consts, 1)
            v.memset(zero_row[:], 0.0).then_inc(consts, 1)
            v.memset(spread[:], 1.0).then_inc(consts, 1)
            v.memset(fixed[:], 0.0).then_inc(consts, 1)
            dve.wait_ge(consts, CONSTS)

            def maxima(pair, slot, again):
                first = pair * (2 * SLAB) + slot * SLAB
                v.tensor_copy(cap_slots[:, slot, :], mem["cap"][:, bass.ds(first, SLAB)]).then_inc(masks, 1)
                dve.wait_ge(masks, pair * 2 + (slot + 1))
                dve.wait_ge(gathered[slot], pair * (16 * SLAB) + 16 * SLAB)
                if again:
                    dve.wait_ge(written[slot], pair * 16)
                for j in range(SLAB):
                    before = best[:, slot, j - 1, :] if j else best[:, 1 - slot, SLAB - 1, :]
                    if again or slot or j:
                        dve.wait_ge(step, first + j)
                    v.scalar_tensor_tensor(out=best[:, slot, j, :], in0=before, scalar=cap_slots[:, slot, j:j + 1],
                                           in1=rows[:, slot, j, :], op0=ALU.min, op1=ALU.max).then_inc(step, 1)
                dve.wait_ge(step, first + SLAB)
                dve.sem_inc(slot_read[slot], 1)

            for slot in range(2):
                maxima(0, slot, False)
            with dve.Fori(1, SLABS // 2) as pair:
                for slot in range(2):
                    maxima(pair, slot, True)
            v.tensor_scalar(spread[:], spread[:], mem["all_through"][:, 0:1], None, ALU.mult).then_inc(join_step, 1)
            dve.wait_ge(join_turned, 2)
            v.tensor_scalar(keep[:], psum[:, 0, 0:P], -2.0, 1.0, ALU.mult, ALU.add).then_inc(join_step, 1)
            v.tensor_copy(last[:], psum[:, 1, 0:P]).then_inc(join_step, 1)
            dve.wait_ge(join_step, 3)
            v.tensor_scalar(keep[:], keep[:], LOWEST, None, ALU.mult).then_inc(join_step, 1)
            dve.wait_ge(join_step, 4)
            v.tensor_tensor_scan(joined[:, 1:P + 1], keep[:], last[:], LOWEST, ALU.min, ALU.max).then_inc(join_step, 1)
            dve.wait_ge(join_turned, 3)
            dve.wait_ge(fix_read, 16)
            v.tensor_tensor(fixed[:], fixed[:], psum[:, 2, 0:FEAT], ALU.max).then_inc(join_step, 1)

        @block.tensor
        def _(pe):
            pe.wait_ge(join_step, 1)
            pe.wait_ge(step, PER)
            nc.tensor.transpose(psum[:, 0, 0:P], spread[:], ident[:]).then_inc(join_turned, 1)
            nc.tensor.transpose(psum[:, 1, 0:P], best[:, 1, SLAB - 1, :], ident[:]).then_inc(join_turned, 1)
            pe.wait_ge(join_step, 5)
            nc.tensor.transpose(psum[:, 2, 0:FEAT], joined[:, 0:P], ident[:]).then_inc(join_turned, 1)

        @block.sync
        def _(sp):
            sp.wait_ge(consts, CONSTS)
            sp.dma_start(dram["maxima"][NO_EDGE_ROW:NO_EDGE_ROW + 1, :], zero_row[:]).then_inc(zero_out, 16)
            maxima = dram["maxima"][0:P * PER, :].rearrange("(p s c) f -> p s (c f)", p=P, s=SLABS)
            with sp.Fori(0, SLABS // 2) as pair:
                for slot in range(2):
                    sp.wait_ge(step, pair * (2 * SLAB) + (slot + 1) * SLAB)
                    sp.dma_start(maxima[:, bass.ds(pair * 2 + slot, 1), :].rearrange("p s c -> p (s c)"),
                                 best[:, slot].rearrange("p c f -> p (c f)")).then_inc(written[slot], 16)
            sp.wait_ge(zero_out, 16)
            for slot in range(2):
                sp.wait_ge(written[slot], 16 * (SLABS // 2))


def finish(nc, mem, dram):
    BATCH = 7
    BATCHES = TILES // BATCH
    with ExitStack() as ctx:
        def sb(name, shape, dt):
            return ctx.enter_context(nc.sbuf_tensor(name, shape, dt))

        def sem(name):
            return ctx.enter_context(nc.semaphore(name))

        maxima = sb("node_maxima", [P, TILES, FEAT], F32)
        gathered = [sem(f"maxima_gathered_{n}") for n in range(BATCHES)]
        step, out_done = Count(sem("finish_step")), sem("out_done")
        x1, base = mem["x1"], mem["base"]

        block = ctx.enter_context(nc.Block())

        @block.gpsimd
        def _(pool):
            for k in range(TILES):
                nc.gpsimd.indirect_dma_start(
                    out=maxima[:, k, :], out_offset=None, in_=dram["maxima"],
                    in_offset=bass.IndirectOffsetOnAxis(ap=mem["node_place"][:, k:k + 1], axis=0)).then_inc(gathered[k // BATCH], 16)

        @block.vector
        def _(dve):
            v = nc.vector
            for b in range(BATCHES):
                tiles = slice(b * BATCH, (b + 1) * BATCH)
                dve.wait_ge(gathered[b], 16 * BATCH)
                for ins in (lambda m: v.tensor_tensor(m, m, base[:, tiles, :], ALU.add),
                            lambda m: v.tensor_scalar(m, m, 0.0, None, ALU.max),
                            lambda m: v.tensor_tensor(m, m, x1[:, tiles, :], ALU.add)):
                    ins(maxima[:, tiles, :]).then_inc(*step.add())
                    dve.wait_ge(step.sem, step.value)

        @block.sync
        def _(sp):
            out = dram["out"].rearrange("(k p) f -> p k f", p=P)
            for b in range(BATCHES):
                tiles = slice(b * BATCH, (b + 1) * BATCH)
                sp.wait_ge(step.sem, 3 * (b + 1))
                sp.dma_start(out[:, tiles, :], maxima[:, tiles, :]).then_inc(out_done, 16)
            sp.wait_ge(out_done, 16 * BATCHES)


class Weights:

    def __init__(self, packed):
        self.packed = packed

    def __call__(self, name, n=0):
        at, width = PACK[name]
        one = 1 if name in ("enc_b1", "enc_b2", "bih", "bhh", "dec_b1", "dec_b2") else FEAT
        return self.packed[:, at + n * one:at + (n + 1) * one]

    def wide(self, name, first, width):
        at = PACK[name][0] + first
        return self.packed[:, at:at + width]


def build(nc, dram):
    def scratch(name, shape, dt):
        dram[name] = nc.dram_tensor(f"scratch_{name}", shape, dt, kind="Internal").ap()

    scratch("keys", (2 + SORTED,), I32)
    scratch("counts", (COUNT_CELLS, 1), BF16)
    scratch("table", (ROWS * RELS, FEAT), F32)
    scratch("maxima", (NO_EDGE_ROW + 1, FEAT), F32)
    with ExitStack() as ctx:
        def sb(name, shape, dt):
            return ctx.enter_context(nc.sbuf_tensor(name, shape, dt))

        mem = {"psum": ctx.enter_context(nc.psum_tensor("banks", [P, 8, WIN], F32)),
               "ident": sb("identity", [P, P], F32), "packed": sb("packed", [P, PACKED], F32)}
        mem["weight"] = Weights(mem["packed"])
        sort_edges(nc, mem, dram)
        mem["table_index"] = sb("table_index", [P, PER], I32)
        mem["cap"] = sb("cap", [P, PER], F32)
        mem["all_through"] = sb("all_through", [P, 1], F32)
        mem["h"] = sb("h", [P, ROWS], F32)
        mem["run_in_end"] = sb("run_in_end", [P, 1], I32)
        mem["node_place"] = sb("node_place", [P, TILES], I32)
        with ExitStack() as cells:
            mem["cell_index"] = cells.enter_context(nc.sbuf_tensor("cell_index", [P, SLABS, SLAB], I32))
            mem["cell_count"] = cells.enter_context(nc.sbuf_tensor("cell_count", [P, SLABS, SLAB], BF16))
            work_out_cells(nc, mem, dram)
            propagate(nc, mem, dram)
        mem["x1"] = sb("x1", [P, TILES, FEAT], F32)
        mem["base"] = sb("self_part", [P, TILES, FEAT], F32)
        decode_and_table(nc, mem, dram)
        running_maximum(nc, mem, dram)
        finish(nc, mem, dram)


def kernel(**inputs):
    import numpy as np
    import concourse.bacc as bacc
    from concourse.bass_utils import run_bass_kernel_spmd as run

    def get(name):
        return np.asarray(inputs[name])

    def padded(values, fill):
        out = np.full(SORTED, fill, np.int32)
        out[:EDGES] = values
        return out.reshape(P, COLS)

    x = np.zeros((ROWS, FEAT), np.float32)
    x[:NODES] = get("x")
    gnn = "L0_gnn_"
    columns = [get(gnn + "enc_w1").T, get(gnn + "enc_w2").T, get(gnn + "gru_wih").T, get(gnn + "gru_whh").T,
               get(gnn + "dec_w1").T, get(gnn + "dec_w2").T,
               get(gnn + "conv_w").transpose(1, 0, 2).reshape(FEAT, -1),
               get("L1_gnn_weight").transpose(1, 0, 2).reshape(FEAT, -1),
               get(gnn + "enc_b1").reshape(1, FEAT).T, get(gnn + "enc_b2").reshape(1, FEAT).T,
               get(gnn + "gru_bih").reshape(3, FEAT).T, get(gnn + "gru_bhh").reshape(3, FEAT).T,
               get(gnn + "dec_b1").reshape(1, FEAT).T, get(gnn + "dec_b2").reshape(1, FEAT).T]
    arrays = {"x": x, "dst": padded(get("dst"), PAD_NODE), "src": padded(get("src"), 0),
              "edge_type": padded(get("edge_type_8"), 0),
              "packed": np.ascontiguousarray(np.concatenate(columns, axis=1)),
              "rel_bias": np.ascontiguousarray(get("L1_gnn_bias").reshape(1, -1))}
    nc = bacc.Bacc("TRN2", target_bir_lowering=False, num_devices=1)
    dram = {name: nc.dram_tensor(f"in_{name}", a.shape, mybir.dt.from_np(a.dtype), kind="ExternalInput").ap()
            for name, a in arrays.items()}
    dram["out"] = nc.dram_tensor("out_0", (ROWS, FEAT), F32, kind="ExternalOutput").ap()
    build(nc, dram)
    result = run(nc, [{f"in_{name}": a for name, a in arrays.items()}], core_ids=[0]).results[0]["out_0"]
    return result[:NODES]
```

```python
from contextlib import ExitStack

import numpy as np

import concourse.bass as bass
from concourse import mybir

ALU = mybir.AluOpType
ACT = mybir.ActivationFunctionType
F32 = mybir.dt.float32
BF16 = mybir.dt.bfloat16
F16 = mybir.dt.float16
I32 = mybir.dt.int32

P = 128
NODES, FEAT, EDGES, RELS, STEPS = 6250, 128, 200000, 8, 5
TILES = -(-NODES // P)
ROWS = TILES * P
WIN = 512
FULL_WINDOWS = ROWS // WIN
WINDOWS = FULL_WINDOWS + 1
LAST = ROWS - FULL_WINDOWS * WIN

HALVES = 2
COLS = 1024
SORTED = P * COLS
COL_BITS, PART_BITS = 10, 7
HALF_EDGES = EDGES // HALVES
HOLDING = -(-HALF_EDGES // COLS)
BLOCKS = COLS // P
BANKS = COLS // 512
SLAB = 16
BLOCK_WORDS = BLOCKS + BLOCKS // 2
HALF_SLABS = HOLDING * BLOCKS // SLAB
SLAB_EDGE_BITS = 11
SLABS = HALVES * HALF_SLABS
PER = SLABS * SLAB
FLOAT_BIT = 0x20000000
SRC_SHIFT, DST_SHIFT, NODE_MASK = 3, 16, 0x1FFF

COUNT_CELLS = WINDOWS * ROWS * WIN
PAD_NODE = WINDOWS * WIN + WIN - 1
SPARE_CELLS = 2 * SORTED
COUNT_UNIT = 1 / 8
COUNT_UNIT_BITS = 3
NO_EDGE_ROW = P * PER
LOWEST = -3.4028234663852886e38

assert HALVES * HALF_EDGES == EDGES and HOLDING * BLOCKS % SLAB == 0 and HOLDING <= P
assert 1 << SLAB_EDGE_BITS == SLAB * P and PAD_NODE >> 9 == WINDOWS and PAD_NODE >> 7 < 64
HIGH = 64

PACK = {}
_at = 0
for _name, _width in [("enc_w1", FEAT), ("enc_w2", FEAT), ("wih", 3 * FEAT), ("whh", 3 * FEAT),
                      ("dec_w1", FEAT), ("dec_w2", FEAT), ("conv", STEPS * FEAT),
                      ("rel", (RELS + 1) * FEAT), ("enc_b1", 1), ("enc_b2", 1), ("bih", 3),
                      ("bhh", 3), ("dec_b1", 1), ("dec_b2", 1)]:
    PACK[_name] = (_at, _width)
    _at += _width
PACKED = _at


NORM_STEPS = 6
KEY_STEPS = 18
REACH_STEP, TOP_STEP, SCALE_STEPS = 4, 5, 17
THROUGH_STEP, PLACE_STEP = 4, 9


class Count:

    def __init__(self, sem):
        self.sem, self.value = sem, 0

    def add(self, by=1):
        self.value += by
        return self.sem, by


class WaitHolder:

    def __init__(self, nc, ctx, engine, name):
        self.engine, self.turns = engine, ctx.enter_context(nc.semaphore(name))

    def take(self):
        self.engine.sem_inc(self.turns, 1)


def indices_of(cells):
    return cells[..., :BLOCKS]


def counts_of(cells):
    return cells[..., BLOCKS:].bitcast(F16)


def scatter_slabs(nc, ctx, pool, mem, dram, half, first, count, landed=None):
    slots = ctx.enter_context(nc.sbuf_tensor(f"cell_slots_{half}_{first}", [P, 2, SLAB // BLOCKS, BLOCK_WORDS], I32))
    copied = ctx.enter_context(nc.semaphore(f"cells_copied_{half}_{first}"))
    if landed is None:
        landed = [ctx.enter_context(nc.semaphore(f"cells_landed_{half}_{first}_{slot}")) for slot in range(2)]
    held = WaitHolder(nc, ctx, pool, f"slab_turns_{half}_{first}")
    compute = {"compute_op": ALU.add} if half else {}

    def slab(pair, slot, again):
        if again:
            pool.wait_ge(landed[slot], pair * (16 * SLAB))
            held.take()
        blocks = bass.ds(pair * (2 * SLAB // BLOCKS) + (slot + first) * (SLAB // BLOCKS), SLAB // BLOCKS)
        nc.gpsimd.tensor_copy(slots[:, slot], mem["cells"][half][:, blocks, :]).then_inc(copied, 1)
        pool.wait_ge(copied, pair * 2 + (slot + 1))
        held.take()
        for j in range(SLAB):
            block, at = j // BLOCKS, j % BLOCKS
            nc.gpsimd.indirect_dma_start(
                out=dram["counts"],
                out_offset=bass.IndirectOffsetOnAxis(ap=indices_of(slots[:, slot, block])[:, at:at + 1], axis=0),
                in_=counts_of(slots[:, slot, block])[:, at:at + 1], in_offset=None, **compute).then_inc(landed[slot], 16)

    for slot in range(2):
        slab(0, slot, False)
    if count > 3:
        with pool.Fori(1, count // 2) as pair:
            for slot in range(2):
                slab(pair, slot, True)
    if count % 2:
        slab(count // 2, 0, True)
    for slot in range(2):
        pool.wait_ge(landed[slot], 16 * SLAB * ((count + 1 - slot) // 2))


def sort_half(nc, mem, dram, half, scatter=None):
    with ExitStack() as ctx:
        def sb(name, shape, dt):
            return ctx.enter_context(nc.sbuf_tensor(f"{name}_{half}", shape, dt))

        def sem(name):
            return ctx.enter_context(nc.semaphore(f"{name}_{half}"))

        raw = sb("raw_edges", [P, 3, COLS], I32)
        keys_a = sb("keys_a", [P, COLS], F32)
        keys_b = sb("keys_b", [P, COLS], F32)
        turned = sb("keys_turned", [P, COLS], F32)
        turned_b = sb("keys_turned_b", [P, COLS], F32)
        zeros = mem["zeros"]
        part = sb("partition_number", [P, 1], I32)
        bits = sb("partition_bits", [P, PART_BITS + 1], I32)
        signs = sb("partition_signs", [P, PART_BITS + 1], F32)
        flips = sb("sign_changes", [P, PART_BITS], F32)

        edges_in, packed_in = sem("edges_in"), sem("packed_in")
        zeros_set, iota_done, ident_zero, ident_done = sem("zeros_set"), sem("iota_done"), sem("ident_zero"), sem("ident_done")
        zero_filled = mem["zero_filled"]
        keys_step = Count(sem("keys_step"))
        turned_psum, turned_sbuf = Count(sem("turned_psum")), Count(sem("turned_sbuf"))
        keys_out = sem("keys_out")

        psum = mem["psum"]
        ident = mem["ident"]
        psum_keys = psum[:, 0:BANKS, :].rearrange("p b c -> p (b c)")

        handoffs = []

        block = ctx.enter_context(nc.Block())

        @block.vector
        def _(dve):
            v = nc.vector

            def done(ins):
                ins.then_inc(*keys_step.add())

            def settled():
                dve.wait_ge(keys_step.sem, keys_step.value)

            PART = COLS // BANKS
            whole, parts = slice(0, COLS), [slice(b * PART, (b + 1) * PART) for b in range(BANKS)]
            ready = [0] * BANKS

            def exchange(src, dst, bit, mirrored=False):
                s = src.rearrange("p (g t e) -> p g t e", t=2, e=1 << bit)
                d = dst.rearrange("p (g t e) -> p g t e", t=2, e=1 << bit)
                turn = slice(None, None, -1) if mirrored else slice(None)
                done(v.tensor_tensor(d[:, :, 0, :], s[:, :, 0, :], s[:, :, 1, turn], ALU.min))
                done(v.tensor_tensor(d[:, :, 1, turn], s[:, :, 0, :], s[:, :, 1, turn], ALU.max))

            def over_top(buffers, mirrored=False):
                dve.wait_ge(keys_step.sem, max(ready))
                exchange(buffers[0], buffers[1], COL_BITS - 1, mirrored)
                ready[:] = [keys_step.value] * BANKS

            def within(buffers, stages, turns=None):
                order = [(b, at) for n in range(len(stages) + BANKS - 1) for b, at in enumerate(range(n, n - BANKS, -1))
                         if 0 <= at < len(stages)]
                for b, n in order:
                    if n == 0 and turns is not None:
                        dve.wait_ge(turned_sbuf.sem, BANKS * turns + b + 1)
                    if n or turns is None:
                        dve.wait_ge(keys_step.sem, ready[b])
                    stages[n](buffers[n % 2][:, parts[b]], buffers[(n + 1) % 2][:, parts[b]])
                    ready[b] = keys_step.value

            def by_bit(bit, mirrored=False):
                return lambda src, dst: exchange(src, dst, bit, mirrored)

            def change_signs(phase):
                return lambda src, dst: done(v.tensor_scalar(dst, src, flips[:, phase - 1:phase], None, ALU.mult))

            dve.wait_ge(iota_done, 1)
            for b in range(PART_BITS):
                done(v.tensor_scalar(bits[:, b:b + 1], part[:], b, 1, ALU.logical_shift_right, ALU.bitwise_and))
            done(v.memset(bits[:, PART_BITS:], 0))
            settled()
            done(v.tensor_scalar(signs[:], bits[:], -2.0, 1.0, ALU.mult, ALU.add))
            settled()
            done(v.tensor_tensor(flips[:], signs[:, :PART_BITS], signs[:, 1:], ALU.mult))

            dve.wait_ge(edges_in, 48)
            key = keys_a[:].bitcast(I32)
            tmp = keys_b[:].bitcast(I32)
            done(v.scalar_tensor_tensor(out=tmp, in0=raw[:, 1, :], scalar=SRC_SHIFT, in1=raw[:, 2, :],
                                        op0=ALU.logical_shift_left, op1=ALU.bitwise_or))
            settled()
            done(v.scalar_tensor_tensor(out=key, in0=raw[:, 0, :], scalar=DST_SHIFT, in1=tmp,
                                        op0=ALU.logical_shift_left, op1=ALU.bitwise_or))
            settled()
            done(v.tensor_scalar(tmp, key, FLOAT_BIT, None, ALU.bitwise_or))
            settled()
            done(v.tensor_scalar(keys_a[:], keys_b[:], signs[:, 0:1], None, ALU.mult))
            ready[:] = [keys_step.value] * BANKS

            buffers, turned_buffers = [keys_a[:], keys_b[:]], [turned[:], turned_b[:]]
            first = []
            for phase in range(1, COL_BITS):
                first += [by_bit(phase - 1, mirrored=phase > 1)] + [by_bit(bit) for bit in range(phase - 2, -1, -1)]
            within(buffers, first)
            if len(first) % 2:
                buffers.reverse()
            over_top(buffers, mirrored=True)
            buffers.reverse()
            for phase in range(1, PART_BITS + 1):
                within(buffers, [by_bit(bit) for bit in range(COL_BITS - 2, -1, -1)] + [change_signs(phase)])
                handoffs.append(list(ready))
                within(turned_buffers, [by_bit(bit) for bit in range(phase - 1, -1, -1)], turns=2 * phase - 2)
                handoffs.append(list(ready))
                dve.wait_ge(turned_sbuf.sem, BANKS * 2 * phase)
                buffers = [keys_a[:], keys_b[:]]
                over_top(buffers)
                buffers.reverse()
            within(buffers, [by_bit(bit) for bit in range(COL_BITS - 2, -1, -1)])
            mem["sorted_keys"] = buffers[1]
            handoffs.append(list(ready))

        local = COL_BITS * (COL_BITS + 1) // 2
        first = [keys_a[:], keys_b[:]]

        def keys_to_turn(phase):
            steps = local + 1 if phase == 1 else COL_BITS + 1
            return first[steps % 2]

        def turned_back(phase):
            return [turned[:], turned_b[:]][phase % 2]

        @block.tensor
        def _(pe):
            if half == 0:
                pe.wait_ge(ident_done, 1)
            for turn in range(2 * PART_BITS):
                phase = turn // 2 + 1
                src = keys_to_turn(phase) if turn % 2 == 0 else turned_back(phase)
                for bank in range(BANKS):
                    pe.wait_ge(keys_step.sem, handoffs[turn][bank])
                    if turn:
                        pe.wait_ge(turned_sbuf.sem, BANKS * (turn - 1) + bank + 1)
                    for c in range(4 * bank, 4 * bank + 4):
                        mm = nc.tensor.transpose(psum_keys[:, c * P:(c + 1) * P], src[:, c * P:(c + 1) * P], ident[:])
                    mm.then_inc(*turned_psum.add())

        @block.scalar
        def _(act):
            if half == 0:
                act.wait_ge(zeros_set, 1)
                cells = dram["counts"][:COUNT_CELLS].rearrange("(w p c) one -> w p (c one)", w=WINDOWS, p=P)
                for w in range(WINDOWS):
                    act.dma_start(cells[w], zeros[:].bitcast(F16)).then_inc(zero_filled, 16)
                act.dma_start(dram["counts"][COUNT_CELLS:].rearrange("(p c) one -> p (c one)", p=P),
                              zeros[:, :SPARE_CELLS // P // 2].bitcast(F16)).then_inc(zero_filled, 16)
            for turn in range(2 * PART_BITS):
                dst = turned if turn % 2 == 0 else keys_a
                for bank in range(BANKS):
                    act.wait_ge(turned_psum.sem, BANKS * turn + bank + 1)
                    nc.scalar.activation(dst[:, bank * 512:(bank + 1) * 512], psum_keys[:, bank * 512:(bank + 1) * 512],
                                         ACT.Copy).then_inc(*turned_sbuf.add())

        @block.gpsimd
        def _(pool):
            nc.gpsimd.iota(part[:], [[0, 1]], base=0, channel_multiplier=1).then_inc(iota_done, 1)
            if half == 0:
                nc.gpsimd.memset(ident[:], 0.0).then_inc(ident_zero, 1)
                nc.gpsimd.memset(mem["guard"][:], 0).then_inc(ident_zero, 1)
                pool.wait_ge(ident_zero, 2)
                nc.gpsimd.affine_select(out=ident[:], in_=ident[:], compare_op=ALU.not_equal, fill=1.0, base=0,
                                        pattern=[[-1, P]], channel_multiplier=1).then_inc(ident_done, 1)
                nc.gpsimd.memset(zeros[:], 0.0).then_inc(zeros_set, 1)
            else:
                scatter(ctx, pool)

        @block.sync
        def _(sp):
            for n, name in enumerate(("dst", "src", "edge_type")):
                sp.dma_start(raw[:, n, :], dram[name][half]).then_inc(edges_in, 16)
            if half == 0:
                sp.dma_start(mem["packed"][:], dram["packed"]).then_inc(packed_in, 16)
                sp.wait_ge(ident_zero, 2)
            sp.wait_ge(keys_step.sem, max(handoffs[-1]))
            put_keys(sp, dram[f"keys_{half}"], mem["sorted_keys"].unsqueeze(1), mem["guard"], keys_out)
            sp.wait_ge(keys_out, 48)
            if half == 0:
                sp.wait_ge(packed_in, 16)


def put_keys(sp, to, keys, guard, out):
    end = to.shape[0] - 1
    sp.dma_start(to[1:end].rearrange("(h p c) -> p h c", p=P, c=COLS), keys.bitcast(I32)).then_inc(out, 16)
    for at in (0, end):
        sp.dma_start(to[at:at + 1].rearrange("(a c) -> a c", a=1), guard[:]).then_inc(out, 16)




def work_out_cells(nc, mem, dram, half, scatter=None):
    with ExitStack() as ctx:
        def sb(name, shape, dt):
            return ctx.enter_context(nc.sbuf_tensor(f"{name}_{half}", shape, dt))

        def sem(name):
            return ctx.enter_context(nc.semaphore(f"{name}_{half}"))

        around = sb("keys_before_at_after", [P, 3, COLS], I32)
        scratch = [sb(f"scratch_{n}", [P, COLS], I32) for n in range(3)]
        before_cell = sb("before_in_cell", [P, COLS], F32)
        ones = sb("ones", [P, COLS], F32)
        rank = sb("rank_in_cell", [P, COLS], F32)
        through = sb("cell_through", [P, COLS], F32)
        count = sb("count_at_last", [P, COLS], F32)
        rows = sb("carry_rows", [1, 3, P + 1], F32)
        carry = sb("carry_column", [P, 1], F32)
        spare = sb("spare_cells", [P, COLS], I32)

        keys_in, spare_done = sem("keys_in"), sem("spare_cells_done")
        step = Count(sem("cell_step"))
        rows_turned, carry_turned = sem("rows_turned"), sem("carry_turned")
        index_turned, count_turned = sem("index_turned"), sem("count_turned")
        index_lifted, count_lifted = sem("index_lifted"), sem("count_lifted")
        psum, ident = mem["psum"], mem["ident"]
        marks = {}
        index = scratch[2]

        block = ctx.enter_context(nc.Block())

        @block.vector
        def _(dve):
            v = nc.vector
            prev, key, nxt = (around[:, n, :] for n in range(3))
            a, b, c = (s[:] for s in scratch)

            def done(ins):
                ins.then_inc(*step.add())

            def settled():
                dve.wait_ge(step.sem, step.value)

            done(v.memset(ones[:], 1.0))
            done(v.memset(rows[:], 0.0))
            dve.wait_ge(keys_in, 48)
            done(v.tensor_tensor(a, prev, key, ALU.bitwise_xor))
            done(v.tensor_tensor(b, nxt, key, ALU.bitwise_xor))
            settled()
            done(v.tensor_scalar(before_cell[:], a, float(1 << SRC_SHIFT), None, ALU.is_lt))
            settled()
            done(v.tensor_tensor_scan(rank[:], before_cell[:], ones[:], 0.0, ALU.mult, ALU.add))
            done(v.tensor_tensor_scan(through[:], before_cell[:], ones[:], 1.0, ALU.mult, ALU.mult))
            marks["scanned"] = step.value
            done(v.tensor_scalar(nxt, b, float(1 << SRC_SHIFT), None, ALU.is_lt))
            settled()
            done(v.tensor_scalar(b, key, SRC_SHIFT, NODE_MASK, ALU.logical_shift_right, ALU.bitwise_and))
            done(v.tensor_scalar(c, key, DST_SHIFT + 9, 15, ALU.logical_shift_right, ALU.bitwise_and))
            settled()
            done(v.scalar_tensor_tensor(out=prev, in0=c, scalar=float(ROWS), in1=b, op0=ALU.mult, op1=ALU.add))
            done(v.tensor_scalar(a, key, DST_SHIFT, WIN - 1, ALU.logical_shift_right, ALU.bitwise_and))
            settled()
            done(v.scalar_tensor_tensor(out=b, in0=prev, scalar=9, in1=a,
                                        op0=ALU.logical_shift_left, op1=ALU.bitwise_or))
            settled()
            dve.wait_ge(spare_done, 1)
            done(v.copy_predicated(b, nxt, spare[:]))
            settled()
            done(v.tensor_scalar(c, b, FLOAT_BIT, None, ALU.bitwise_or))
            marks["index"] = step.value
            dve.wait_ge(rows_turned, 2)
            done(v.tensor_copy(rows[:, 0, 0:P], psum[0:1, 4, 0:P]))
            done(v.tensor_copy(rows[:, 1, 0:P], psum[0:1, 5, 0:P]))
            settled()
            done(v.tensor_tensor_scan(rows[:, 2, 1:P + 1], rows[:, 1, 0:P], rows[:, 0, 0:P], 0.0, ALU.mult, ALU.add))
            marks["carry_row"] = step.value
            dve.wait_ge(carry_turned, 1)
            done(v.tensor_copy(carry[:], psum[:, 6, 0:1]))
            settled()
            done(v.scalar_tensor_tensor(out=count[:], in0=through[:], scalar=carry[:, 0:1], in1=rank[:],
                                        op0=ALU.mult, op1=ALU.add))
            marks["count"] = step.value
            for bank in range(BANKS):
                dve.wait_ge(index_turned, bank + 1)
                lifted = psum[:, bank, :].bitcast(I32).rearrange("q (b p) -> q p b", p=P)[:, :HOLDING, :]
                v.tensor_scalar(indices_of(mem["cells"][half])[:, :, 4 * bank:4 * bank + 4], lifted, FLOAT_BIT - 1, None,
                                ALU.bitwise_and).then_inc(index_lifted, 1)

        @block.tensor
        def _(pe):
            pe.wait_ge(step.sem, marks["scanned"])
            nc.tensor.transpose(psum[0:1, 4, 0:P], rank[:, COLS - 1:COLS], ident[:]).then_inc(rows_turned, 1)
            nc.tensor.transpose(psum[0:1, 5, 0:P], through[:, COLS - 1:COLS], ident[:]).then_inc(rows_turned, 1)
            pe.wait_ge(step.sem, marks["index"])

            def turn(source, turned):
                for b in range(BLOCKS):
                    mm = nc.tensor.transpose(psum[:, b // 4, (b % 4) * P:(b % 4 + 1) * P],
                                             source[:, b * P:(b + 1) * P], ident[:])
                    if b % 4 == 3:
                        mm.then_inc(turned, 1)

            turn(index[:].bitcast(F32), index_turned)
            pe.wait_ge(step.sem, marks["carry_row"])
            nc.tensor.transpose(psum[:, 6, 0:1], rows[:, 2, 0:P], ident[0:1, 0:1]).then_inc(carry_turned, 1)
            pe.wait_ge(step.sem, marks["count"])
            pe.wait_ge(index_lifted, BANKS)
            turn(count, count_turned)

        @block.scalar
        def _(act):
            for bank in range(BANKS):
                act.wait_ge(count_turned, bank + 1)
                lifted = psum[:, bank, :].rearrange("q (b p) -> q p b", p=P)[:, :HOLDING, :]
                nc.scalar.activation(counts_of(mem["cells"][half])[:, :, 4 * bank:4 * bank + 4], lifted, ACT.Copy,
                                     scale=COUNT_UNIT).then_inc(count_lifted, 1)
            if half == 0:
                act.wait_ge(mem["zero_filled"], 16 * (WINDOWS + 1))

        @block.gpsimd
        def _(pool):
            nc.gpsimd.iota(spare[:], [[1, COLS]], base=COUNT_CELLS + WIN, channel_multiplier=COLS).then_inc(spare_done, 1)
            if scatter is not None:
                scatter(ctx, pool)

        @block.sync
        def _(sp):
            for n in range(3):
                sp.dma_start(around[:, n, :], dram[f"keys_{half}"][n:n + SORTED].rearrange("(p c) -> p c", p=P)).then_inc(keys_in, 16)


def join_halves(nc, mem, dram, scatter):
    with ExitStack() as ctx:
        def sb(name, shape, dt):
            return ctx.enter_context(nc.sbuf_tensor(name, shape, dt))

        def sem(name):
            return ctx.enter_context(nc.semaphore(name))

        halves = sb("halves", [P, HALVES, COLS], F32)
        mirrored = sb("second_half_mirrored", [P, COLS], F32)
        turned = [sb(f"joined_turned_{n}", [P, HALVES * COLS], F32) for n in range(2)]
        keys = [sb(f"joined_{n}", [P, HALVES * COLS], F32) for n in range(2)]
        is_below = sb("is_below", [P, COLS], F32)
        below = sb("below_window_end", [P, WINDOWS], F32)
        ones = sb("ones_column", [P, 1], F32)
        slab_row = sb("slab_of_last_edge", [1, WINDOWS], I32)

        halves_in, keys_out = sem("halves_in"), sem("joined_out")
        step = Count(sem("join_keys_step"))
        counted = Count(sem("windows_counted"))
        turned_psum, turned_sbuf, summed = sem("joined_turned_psum"), sem("joined_turned_sbuf"), sem("windows_summed")
        psum, ident = mem["psum"], mem["ident"]
        marks = {}

        block = ctx.enter_context(nc.Block())

        @block.vector
        def _(dve):
            v = nc.vector

            def done(ins, count=step):
                ins.then_inc(*count.add())

            def settled(count=step):
                dve.wait_ge(count.sem, count.value)

            dve.wait_ge(halves_in, 32)
            done(v.tensor_copy(mirrored[:], halves[:, 1, ::-1]))
            marks["mirrored"] = step.value

            done(v.memset(ones[:], 1.0), counted)
            for n in range(WINDOWS):
                bits = np.array([FLOAT_BIT | ((n + 1) * WIN) << DST_SHIFT], np.int32)
                if n:
                    settled(counted)
                done(v.tensor_scalar(is_below[:], halves[:, 1, :], float(bits.view(np.float32)[0]), None, ALU.is_lt), counted)
                settled(counted)
                done(v.tensor_reduce(below[:, n:n + 1], is_below[:], mybir.AxisListType.X, ALU.add), counted)
            marks["below"] = counted.value

            def exchange(src, dst, bit):
                s = src.rearrange("p (g t e) -> p g t e", t=2, e=1 << bit)
                d = dst.rearrange("p (g t e) -> p g t e", t=2, e=1 << bit)
                settled()
                done(v.tensor_tensor(d[:, :, 0, :], s[:, :, 0, :], s[:, :, 1, :], ALU.min))
                done(v.tensor_tensor(d[:, :, 1, :], s[:, :, 0, :], s[:, :, 1, :], ALU.max))

            dve.wait_ge(turned_sbuf, 2 * BANKS)
            s = turned[0][:].rearrange("q (h b p) -> q h b p", h=HALVES, p=P)
            d = turned[1][:].rearrange("q (h b p) -> q h b p", h=HALVES, p=P)
            done(v.tensor_tensor(d[:, 0], s[:, 0], s[:, 1, :, ::-1], ALU.min))
            done(v.tensor_tensor(d[:, 1], s[:, 0], s[:, 1, :, ::-1], ALU.max))
            cur, other = turned[1][:], turned[0][:]
            for bit in range(PART_BITS - 1, -1, -1):
                exchange(cur, other, bit)
                cur, other = other, cur
            marks["turn_back"] = step.value
            mem["joined_turned"] = cur
            dve.wait_ge(summed, 1)
            done(v.tensor_copy(slab_row[:], psum[0:1, 5, 0:WINDOWS]), counted)
            settled(counted)
            done(v.tensor_scalar(slab_row[:], slab_row[:], SLAB_EDGE_BITS, None, ALU.logical_shift_right), counted)
            settled(counted)
            done(v.tensor_scalar(slab_row[:], slab_row[:], 1.0, float(HALF_SLABS - 1), ALU.max, ALU.min), counted)
            settled(counted)
            for slot in range(2):
                needed = mem["needed"][:, slot, :]
                done(v.tensor_scalar(needed, slab_row[:], float(2 - slot), None, ALU.add), counted)
                settled(counted)
                done(v.tensor_scalar(needed, needed, 1, None, ALU.logical_shift_right), counted)
                settled(counted)
                done(v.tensor_scalar(needed, needed, float(16 * SLAB), -1.0, ALU.mult, ALU.add), counted)
            dve.wait_ge(turned_sbuf, 4 * BANKS)
            cur, other = keys[0][:], keys[1][:]
            for bit in range(COL_BITS - 1, -1, -1):
                exchange(cur, other, bit)
                cur, other = other, cur
            marks["joined"] = step.value
            mem["joined_keys"] = cur

        @block.tensor
        def _(pe):
            def turn(source, bank, col):
                for c in range(4):
                    mm = nc.tensor.transpose(psum[:, bank, c * P:(c + 1) * P], source[:, col + c * P:col + (c + 1) * P], ident[:])
                mm.then_inc(turned_psum, 1)

            pe.wait_ge(halves_in, 32)
            for bank in range(BANKS):
                turn(halves[:, 0, :], bank, bank * 512)
            pe.wait_ge(step.sem, marks["mirrored"])
            for bank in range(BANKS):
                turn(mirrored, BANKS + bank, bank * 512)
            pe.wait_ge(counted.sem, marks["below"])
            nc.tensor.matmul(psum[0:1, 5, 0:WINDOWS], ones[:], below[:], start=True, stop=True).then_inc(summed, 1)
            pe.wait_ge(step.sem, marks["turn_back"])
            pe.wait_ge(turned_sbuf, 2 * BANKS)
            for bank in range(2 * BANKS):
                turn(mem["joined_turned"], bank, bank * 512)

        @block.scalar
        def _(act):
            for n, dst in enumerate((turned[0], keys[0])):
                for bank in range(2 * BANKS):
                    act.wait_ge(turned_psum, 2 * BANKS * n + bank + 1)
                    nc.scalar.activation(dst[:, bank * 512:(bank + 1) * 512], psum[:, bank, :],
                                         ACT.Copy).then_inc(turned_sbuf, 1)

        @block.gpsimd
        def _(pool):
            scatter(ctx, pool)

        @block.sync
        def _(sp):
            for h in range(HALVES):
                sp.dma_start(halves[:, h, :].bitcast(I32), dram[f"keys_{h}"][1:1 + SORTED].rearrange("(p c) -> p c", p=P)).then_inc(halves_in, 16)
            sp.wait_ge(step.sem, marks["joined"])
            put_keys(sp, dram["keys"], mem["joined_keys"].rearrange("p (h c) -> p h c", c=COLS), mem["guard"], keys_out)
            sp.wait_ge(keys_out, 48)


def groups():
    return [list(range(g, min(g + 4, TILES))) for g in range(0, TILES, 4)]


def norm_buffers(nc, ctx, name, squares):
    def sb(what, shape):
        return ctx.enter_context(nc.sbuf_tensor(f"{name}_{what}", shape, F32))

    def sem(what):
        return ctx.enter_context(nc.semaphore(f"{name}_{what}"))

    return {"squares": squares, "mean": sb("mean", [P, TILES]),
            "var": sb("var", [P, TILES]), "std": sb("std", [P, TILES]), "scale": sb("scale", [P, TILES]),
            "eps": sb("eps", [P, 1]), "step": Count(sem("norm_step")), "rooted": sem("rooted")}


def norm_first(nc, dve, given, x, n):
    v, step = nc.vector, n["step"]
    AX = mybir.AxisListType.X

    def done(ins):
        ins.then_inc(*step.add())
        dve.wait_ge(step.sem, step.value)

    done(v.memset(n["eps"][:], 1e-5))
    done(v.tensor_reduce(n["mean"][:], given, AX, ALU.add))
    done(v.tensor_scalar(n["mean"][:], n["mean"][:], 1.0 / FEAT, None, ALU.mult))
    done(v.tensor_tensor(x, given, n["mean"][:].unsqueeze(2).broadcast_to([P, TILES, FEAT]), ALU.subtract))
    done(v.tensor_tensor(n["squares"], x, x, ALU.mult))
    done(v.tensor_reduce(n["var"][:], n["squares"], AX, ALU.add))
    assert step.value == NORM_STEPS


def norm_middle(nc, act, n):
    act.wait_ge(n["step"].sem, NORM_STEPS)
    nc.scalar.activation(n["std"][:], n["var"][:], ACT.Sqrt, bias=n["eps"][:, 0:1],
                         scale=1.0 / FEAT).then_inc(n["rooted"], 1)


def norm_last(nc, dve, x, n, normed):
    v, step = nc.vector, n["step"]
    dve.wait_ge(n["rooted"], 1)
    v.reciprocal(n["scale"][:], n["std"][:]).then_inc(*step.add())
    dve.wait_ge(step.sem, step.value)
    v.tensor_tensor(x, x, n["scale"][:].unsqueeze(2).broadcast_to([P, TILES, FEAT]),
                    ALU.mult).then_inc(normed, 1)


def describe_edges(nc, mem, dram, scatter):
    with ExitStack() as ctx:
        def sb(name, shape, dt):
            return ctx.enter_context(nc.sbuf_tensor(name, shape, dt))

        def sem(name):
            return ctx.enter_context(nc.semaphore(name))

        prev, key, xor = (sb(name, [P, PER], I32)[:] for name in ("key_before", "key", "key_changes"))
        same, ones_row = sb("same_dst", [P, PER], F32)[:], sb("ones_row", [P, PER], F32)

        low, high = sb("dst_low", [P, PER], BF16), sb("dst_high", [P, PER], BF16)
        iota_f = sb("iota_row", [P, P], F32)
        iota_b = sb("iota_row_bf16", [P, P], BF16)
        hot_low = [sb(f"one_hot_low_{n}", [P, SLAB, P], BF16) for n in range(2)]
        hot_high = [sb(f"one_hot_high_{n}", [P, SLAB, HIGH], BF16) for n in range(2)]
        per_node = sb("edges_per_node", [HIGH, P], F32)
        through_node = sb("edges_through_node", [HIGH, P], F32)
        below = sb("strictly_below", [HIGH, HIGH], F32)
        place_f = sb("last_place", [HIGH, P], F32)
        some = sb("has_edges", [HIGH, P], F32)
        last_col = sb("edges_through_high", [HIGH, 1], F32)
        part_base = sb("partition_first_place", [P, 1], F32)
        run_in = sb("run_in", [P, 1], F32)
        no_run = sb("no_run_in", [P, 1], F32)

        keys_in, iotas = sem("keys_again_in"), sem("iotas")
        key_step = Count(sem("key_step"))
        hot_done, hot_used = sem("one_hots_done"), sem("one_hots_used")
        node_step, node_turned = Count(sem("node_step")), sem("node_turned")
        psum, ident = mem["psum"], mem["ident"]
        HIST, SPARE = range(2)

        block = ctx.enter_context(nc.Block())

        @block.gpsimd
        def _(pool):
            nc.gpsimd.iota(iota_f[:], [[1, P]], base=0, channel_multiplier=0,
                           allow_small_or_imprecise_dtypes=True).then_inc(iotas, 1)
            nc.gpsimd.iota(part_base[:], [[0, 1]], base=-1, channel_multiplier=PER,
                           allow_small_or_imprecise_dtypes=True).then_inc(iotas, 1)
            nc.gpsimd.memset(below[:], 1.0).then_inc(iotas, 1)
            pool.wait_ge(iotas, 3)
            nc.gpsimd.affine_select(out=below[:], in_=below[:], compare_op=ALU.is_gt, fill=0.0, base=0,
                                    pattern=[[1, HIGH]], channel_multiplier=-1).then_inc(iotas, 1)
            scatter(ctx, pool)

        @block.sync
        def _(sp):
            for n, to in enumerate((prev, key)):
                sp.dma_start(to, dram["keys"][n:n + P * PER].rearrange("(p c) -> p c", p=P)).then_inc(keys_in, 16)

        @block.vector
        def _(dve):
            v = nc.vector
            AX = mybir.AxisListType.X

            def done(ins, count=key_step):
                ins.then_inc(*count.add())

            def settled(count=key_step):
                dve.wait_ge(count.sem, count.value)

            dve.wait_ge(iotas, 4)
            done(v.tensor_copy(iota_b[:], iota_f[:]))
            dve.wait_ge(keys_in, 32)
            done(v.tensor_tensor(xor, prev, key, ALU.bitwise_xor))
            settled()
            done(v.tensor_scalar(prev, xor, DST_SHIFT, None, ALU.logical_shift_right))
            settled()
            done(v.tensor_scalar(same, prev, 0.0, None, ALU.is_equal))
            done(v.memset(ones_row[:], 1.0))
            settled()
            done(v.tensor_tensor_scan(xor.bitcast(F32), same, ones_row[:], 1.0, ALU.mult, ALU.mult))
            done(v.tensor_scalar(mem["cap"][:], same, -2.0, 1.0, ALU.mult, ALU.add))
            settled()
            done(v.tensor_scalar(mem["cap"][:], mem["cap"][:], LOWEST, None, ALU.mult))
            done(v.tensor_copy(mem["all_through"][:], xor.bitcast(F32)[:, PER - 1:PER]))
            done(v.tensor_reduce(run_in[:], xor.bitcast(F32), AX, ALU.add))
            settled()
            done(v.tensor_scalar(no_run[:], run_in[:], 0.0, float(1 << 25), ALU.is_equal, ALU.mult))
            done(v.tensor_scalar(run_in[:], run_in[:], part_base[:, 0:1], None, ALU.add))
            settled()
            done(v.tensor_tensor(mem["run_in_end"][:], run_in[:], no_run[:], ALU.add))
            done(v.tensor_scalar(mem["table_index"][:], key, (1 << DST_SHIFT) - 1, None, ALU.bitwise_and))
            done(v.tensor_scalar(prev, key, DST_SHIFT, P - 1, ALU.logical_shift_right, ALU.bitwise_and))
            done(v.tensor_scalar(xor, key, DST_SHIFT + 7, HIGH - 1, ALU.logical_shift_right, ALU.bitwise_and))
            settled()
            done(v.tensor_copy(low[:], prev))
            done(v.tensor_copy(high[:], xor))
            settled()
            assert key_step.value == KEY_STEPS

            def hot(s, columns):
                v.tensor_tensor(hot_low[s][:], iota_b[:].unsqueeze(1).broadcast_to([P, SLAB, P]),
                                low[:, columns].unsqueeze(2).broadcast_to([P, SLAB, P]), ALU.is_equal).then_inc(hot_done, 1)
                v.tensor_tensor(hot_high[s][:], iota_b[:, :HIGH].unsqueeze(1).broadcast_to([P, SLAB, HIGH]),
                                high[:, columns].unsqueeze(2).broadcast_to([P, SLAB, HIGH]), ALU.is_equal).then_inc(hot_done, 1)

            for s in range(2):
                hot(s, slice(s * SLAB, (s + 1) * SLAB))
            with dve.Fori(1, SLABS // 2) as pair:
                for s in range(2):
                    dve.wait_ge(hot_used, pair * 2 + (s - 1))
                    hot(s, bass.ds(pair * (2 * SLAB) + s * SLAB, SLAB))

            def ndone(ins):
                done(ins, node_step)

            def nsettled():
                settled(node_step)

            dve.wait_ge(hot_used, SLABS)
            ndone(v.tensor_copy(per_node[:], psum[0:HIGH, HIST, 0:P]))
            nsettled()
            ndone(v.memset(place_f[:], 1.0))
            nsettled()
            ndone(v.tensor_tensor_scan(through_node[:], place_f[:], per_node[:], 0.0, ALU.mult, ALU.add))
            nsettled()
            ndone(v.tensor_copy(last_col[:], through_node[:, P - 1:P]))
            assert node_step.value == THROUGH_STEP
            ndone(v.tensor_scalar(some[:], per_node[:], 0.0, None, ALU.is_gt))
            dve.wait_ge(node_turned, 1)
            ndone(v.tensor_copy(no_run[0:HIGH], psum[0:HIGH, SPARE, 0:1]))
            nsettled()
            ndone(v.tensor_scalar(place_f[:], through_node[:], no_run[0:HIGH, 0:1], float(-1 - NO_EDGE_ROW), ALU.add, ALU.add))
            nsettled()
            ndone(v.tensor_tensor(place_f[:], place_f[:], some[:], ALU.mult))
            nsettled()
            ndone(v.tensor_scalar(place_f[:], place_f[:], float(NO_EDGE_ROW), None, ALU.add))
            assert node_step.value == PLACE_STEP
            dve.wait_ge(node_turned, 2)
            ndone(v.tensor_copy(mem["node_place"][:], psum[:, SPARE, 0:TILES]))

        @block.tensor
        def _(pe):
            mm = nc.tensor.matmul
            for s in range(2):
                pe.wait_ge(hot_done, 2 * s + 2)
                for j in range(SLAB):
                    last = mm(psum[0:HIGH, HIST, 0:P], hot_high[s][:, j, :], hot_low[s][:, j, :],
                              start=(s == 0 and j == 0), stop=False, skip_group_check=True)
                last.then_inc(hot_used, 1)
            with pe.Fori(1, SLABS // 2) as pair:
                for s in range(2):
                    pe.wait_ge(hot_done, pair * 4 + (2 * s + 2))
                    for j in range(SLAB):
                        last = mm(psum[0:HIGH, HIST, 0:P], hot_high[s][:, j, :], hot_low[s][:, j, :],
                                  start=False, stop=False, skip_group_check=True)
                    last.then_inc(hot_used, 1)
            pe.wait_ge(node_step.sem, THROUGH_STEP)
            mm(psum[0:HIGH, SPARE, 0:1], below[:], last_col[:], start=True, stop=True).then_inc(node_turned, 1)
            pe.wait_ge(node_step.sem, PLACE_STEP)
            nc.tensor.transpose(psum[:, SPARE, 0:HIGH], place_f[:], ident[0:HIGH, 0:HIGH]).then_inc(node_turned, 1)


def propagate(nc, mem, dram):
    LOADS = [(0, 25), (25, TILES)]
    with ExitStack() as ctx:
        def sb(name, shape, dt):
            return ctx.enter_context(nc.sbuf_tensor(name, shape, dt))

        def sem(name):
            return ctx.enter_context(nc.semaphore(name))

        counts = sb("counts_window", [P, TILES, WIN], F16)
        both = counts[:].rearrange("p k c -> p (k c)").bitcast(F32)
        x = both[:, :TILES * FEAT].rearrange("p (k f) -> p k f", f=FEAT)
        squares = both[:, TILES * FEAT:].rearrange("p (k f) -> p k f", f=FEAT)
        parts = [sb(f"m_parts_{n}", [P, TILES, 2, FEAT], F16) for n in range(2)]
        window = {name: sb(name, [P, WIN], F32) for name in ("sums", "gate_r", "gate_z", "candidate", "difference", "h_fresh")}
        sums, gate_r, gate_z, new, diff, fresh = (window[n] for n in ("sums", "gate_r", "gate_z", "candidate", "difference", "h_fresh"))
        gate_bias = sb("gate_bias", [P, 2], F32)
        norm = norm_buffers(nc, ctx, "encoder", squares)

        ones_mat = sb("ones_matrix", [P, P], F32)
        abs_conv = sb("abs_conv", [P, STEPS, FEAT], F32)
        reach = sb("h_reach", [P, 4], F32)
        top = sb("h_reach_row", [1, 2], F32)
        bound = sb("m_bound", [P, STEPS], F32)
        exponent = sb("m_exponent", [P, STEPS], I32)
        scale = sb("m_scale", [P, STEPS], I32)
        unscale = sb("m_unscale", [P, STEPS], I32)
        conv = sb("conv_scaled", [P, STEPS, FEAT], F32)

        landed = [sem(f"second_cells_landed_{slot}") for slot in range(2)]
        x_in = sem("x_in")
        normed, turned, lifted = sem("x_normed"), sem("x_turned"), sem("x_lifted")
        pre1, act1, pre2, act2 = sem("enc_pre1"), sem("enc_act1"), sem("enc_pre2"), sem("enc_act2")
        consts = sem("propagate_constants")
        scale_step, scale_turned, abs_done = Count(sem("scale_step")), sem("scale_turned"), sem("abs_conv_done")
        loaded = [sem("counts_loaded_0"), sem("counts_loaded_1")]
        half_done = [sem("sums_half_0"), sem("sums_half_1")]
        m_done, high_done, low_done = sem("m_product"), sem("m_high"), sem("m_low")
        sums_copied = sem("sums_copied")
        gates_done, gates_acted = sem("gates_done"), sem("gates_acted")
        cand_step, cand_pre, cand_done = sem("candidate_step"), sem("candidate_pre"), sem("candidate_done")
        h_done, h_copied = sem("h_done"), sem("h_copied")
        psum, ident, h, w = mem["psum"], mem["ident"], mem["h"], mem["weight"]
        G = len(groups())
        assert G == WINDOWS
        SUMS, M, R, Z, IN, HN, SPARE = range(7)
        marks = {}
        wins = [(n * WIN, WIN) for n in range(FULL_WINDOWS)] + [(FULL_WINDOWS * WIN, LAST)]

        def steps_of(engine, first, body):
            for t in range(STEPS):
                first(t)
                if t == 0:
                    body(0, 1, WIN)
                with engine.Fori(2 if t == 0 else 1, FULL_WINDOWS) as n:
                    body(t, n, WIN)
                body(t, FULL_WINDOWS, LAST)
            first(STEPS)

        def later(t, n):
            return t > 0 or not isinstance(n, int) or n > 0

        def at(n, width):
            return bass.ds(n * WIN, width)

        block = ctx.enter_context(nc.Block())

        @block.gpsimd
        def _(pool):
            scatter_slabs(nc, ctx, pool, mem, dram, 1, 0, HALF_SLABS, landed)

        @block.sync
        def _(sp):
            sp.dma_start(mem["x1"][:], dram["x"].rearrange("(k p) f -> p k f", p=P)).then_inc(x_in, 16)
            cells = dram["counts"][:COUNT_CELLS].rearrange("(w k p c) one -> w p k (c one)", w=WINDOWS, p=P, c=WIN)

            def load(t, n, width):
                for half, (a, b) in enumerate(LOADS):
                    if later(t, n):
                        sp.wait_ge(half_done[half], n + t * WINDOWS)
                    src = cells[n] if isinstance(n, int) else cells[bass.ds(n, 1)].rearrange("w p k c -> (w p) k c")
                    sp.dma_start(counts[:, a:b, :width], src[:, a:b, :width]).then_inc(loaded[half], 16)

            sp.wait_ge(lifted, G)
            held = WaitHolder(nc, ctx, sp, "windows_turns")
            for n, (_, width) in enumerate(wins):
                needed = [sp.value_load(mem["needed"][0:1, slot, n:n + 1], min_val=16 * SLAB - 1,
                                        max_val=16 * SLAB * ((HALF_SLABS + 1 - slot) // 2) - 1) for slot in range(2)]
                for slot in range(2):
                    sp.wait_ge(landed[slot], needed[slot] + 1)
                    held.take()
                load(0, n, width)
            for t in range(1, STEPS):
                with sp.Fori(0, FULL_WINDOWS) as n:
                    load(t, n, WIN)
                load(t, FULL_WINDOWS, LAST)

        @block.tensor
        def _(pe):
            mm = nc.tensor.matmul
            pe.wait_ge(normed, 1)
            for g, tiles in enumerate(groups()):
                if g >= 2:
                    pe.wait_ge(lifted, g - 1)
                for i, k in enumerate(tiles):
                    last = nc.tensor.transpose(psum[:, g % 2, i * P:(i + 1) * P], x[:, k, :], ident[:])
                last.then_inc(turned, 1)
            pe.wait_ge(lifted, G)
            for n, (a, width) in enumerate(wins):
                if n:
                    pe.wait_ge(act1, n)
                mm(psum[:, 2, :width], w("enc_w1"), h[:, a:a + width], start=True, stop=True).then_inc(pre1, 1)
                pe.wait_ge(act1, n + 1)
                if n:
                    pe.wait_ge(act2, n)
                mm(psum[:, 3, :width], w("enc_w2"), diff[:, :width], start=True, stop=True).then_inc(pre2, 1)
            pe.wait_ge(act1, WINDOWS)
            pe.wait_ge(act2, WINDOWS)
            pe.wait_ge(abs_done, 1)
            pe.wait_ge(consts, 2)
            mm(psum[:, R, :4 * FEAT], ones_mat[:], abs_conv[:, :4, :], start=True, stop=True).then_inc(scale_turned, 1)
            mm(psum[:, Z, :FEAT], ones_mat[:], abs_conv[:, 4, :], start=True, stop=True).then_inc(scale_turned, 1)
            pe.wait_ge(scale_step.sem, REACH_STEP)
            nc.tensor.transpose(psum[0:1, SPARE, 0:P], reach[:, 3:4], ident[:]).then_inc(scale_turned, 1)
            pe.wait_ge(scale_step.sem, TOP_STEP)
            mm(psum[:, SPARE, 0:1], ones_mat[0:1, :], top[:, 0:1], start=True, stop=True).then_inc(scale_turned, 1)
            pe.wait_ge(scale_step.sem, SCALE_STEPS)
            for g, tiles in enumerate(groups()):
                if g:
                    pe.wait_ge(low_done, g)
                for i, k in enumerate(tiles):
                    last = mm(psum[:, M, i * P:(i + 1) * P], h[:, k * P:(k + 1) * P], conv[:, 0, :], start=True, stop=True)
                last.then_inc(m_done, 1)
            def half(t, n, width, which):
                g = n + t * WINDOWS
                if which == 0 and later(t, n):
                    pe.wait_ge(sums_copied, g)
                if isinstance(n, int) and n == 0:
                    pe.wait_ge(low_done, t * G + (7 if which == 0 else G))
                pe.wait_ge(loaded[which], g * 16 + 16)
                a, b = LOADS[which]
                for k in range(a, b):
                    for i in range(2):
                        last = mm(psum[:, SUMS, :width], parts[t % 2][:, k, i, :], counts[:, k, :width],
                                  start=(k == 0 and i == 0), stop=(k == TILES - 1 and i == 1))
                last.then_inc(half_done[which], 1)

            def gates(t, n, width):
                g = n + t * WINDOWS
                pe.wait_ge(sums_copied, g + 1)
                if later(t, n):
                    pe.wait_ge(h_done, g)
                if t:
                    pe.wait_ge(h_copied, g - (WINDOWS - 1))
                hw = h[:, at(n, width)]
                for bank, gate in ((R, 0), (Z, 1)):
                    mm(psum[:, bank, :width], w("wih", gate), sums[:, :width], start=True, stop=False)
                    mm(psum[:, bank, :width], w("whh", gate), hw, start=False, stop=True)
                mm(psum[:, IN, :width], w("wih", 2), sums[:, :width], start=True, stop=True)
                mm(psum[:, HN, :width], w("whh", 2), hw, start=True, stop=True).then_inc(gates_done, 1)

            def next_m(t, n, width):
                if t == STEPS - 1:
                    return
                g = n + t * WINDOWS
                pe.wait_ge(h_done, g + 1)
                pe.wait_ge(low_done, g + G)
                for i in range(width // P):
                    last = mm(psum[:, M, i * P:(i + 1) * P], fresh[:, i * P:(i + 1) * P], conv[:, t + 1, :], start=True, stop=True)
                last.then_inc(m_done, 1)

            def first(t):
                if t:
                    gates(t - 1, FULL_WINDOWS, LAST)
                if t < STEPS:
                    half(t, 0, WIN, 0)
                if t:
                    next_m(t - 1, FULL_WINDOWS, LAST)
                if t < STEPS:
                    half(t, 0, WIN, 1)

            def body(t, n, width):
                half(t, n, width, 0)
                gates(t, n - 1, WIN)
                half(t, n, width, 1)
                next_m(t, n - 1, WIN)

            steps_of(pe, first, body)

        @block.scalar
        def _(act):
            A = nc.scalar.activation
            A(abs_conv[:].rearrange("p t f -> p (t f)"), w.wide("conv", 0, STEPS * FEAT), ACT.Abs).then_inc(abs_done, 1)
            norm_middle(nc, act, norm)
            for g, tiles in enumerate(groups()):
                act.wait_ge(turned, g + 1)
                A(h[:, tiles[0] * P:(tiles[-1] + 1) * P], psum[:, g % 2, :len(tiles) * P], ACT.Relu).then_inc(lifted, 1)
            for n, (a, width) in enumerate(wins):
                act.wait_ge(pre1, n + 1)
                if n:
                    act.wait_ge(pre2, n)
                A(diff[:, :width], psum[:, 2, :width], ACT.Relu, bias=w("enc_b1")).then_inc(act1, 1)
                act.wait_ge(pre2, n + 1)
                A(h[:, a:a + width], psum[:, 3, :width], ACT.Identity, bias=w("enc_b2")).then_inc(act2, 1)

            def m_high(to, tile, n, g):
                act.wait_ge(m_done, g + 1)
                A(to[:, tile, 0, :], psum[:, M, :n * P].rearrange("p (k f) -> p k f", f=FEAT), ACT.Copy).then_inc(high_done, 1)

            for g, tiles in enumerate(groups()):
                m_high(parts[0], slice(tiles[0], tiles[-1] + 1), len(tiles), g)
            act.wait_ge(consts, 2)
            act.wait_ge(scale_step.sem, SCALE_STEPS)

            def lift_sums(t, n, width):
                g = n + t * WINDOWS
                act.wait_ge(half_done[1], g + 1)
                if later(t, n):
                    act.wait_ge(gates_done, g)
                A(sums[:, :width], psum[:, SUMS, :width], ACT.Copy, scale=unscale[:, t:t + 1].bitcast(F32)).then_inc(sums_copied, 1)

            def cell(t, n, width):
                g = n + t * WINDOWS
                act.wait_ge(gates_done, g + 1)
                if later(t, n):
                    act.wait_ge(h_done, g)
                A(gate_r[:, :width], psum[:, R, :width], ACT.Sigmoid, bias=gate_bias[:, 0:1]).then_inc(gates_acted, 1)
                A(gate_z[:, :width], psum[:, Z, :width], ACT.Sigmoid, bias=gate_bias[:, 1:2]).then_inc(gates_acted, 1)
                act.wait_ge(cand_pre, g + 1)
                A(new[:, :width], diff[:, :width], ACT.Tanh, bias=w("bih", 2)).then_inc(cand_done, 1)
                act.wait_ge(h_done, g + 1)
                A(h[:, at(n, width)], fresh[:, :width], ACT.Copy).then_inc(h_copied, 1)

            def high(t, n, width):
                if t < STEPS - 1:
                    m_high(parts[(t + 1) % 2], bass.ds(n * 4, width // P), width // P, n + (t + 1) * WINDOWS)

            def first(t):
                if t:
                    cell(t - 1, FULL_WINDOWS, LAST)
                    high(t - 1, FULL_WINDOWS, LAST)
                if t < STEPS:
                    lift_sums(t, 0, WIN)

            def body(t, n, width):
                cell(t, n - 1, WIN)
                lift_sums(t, n, width)
                high(t, n - 1, WIN)

            steps_of(act, first, body)

        @block.vector
        def _(dve):
            v = nc.vector
            AX = mybir.AxisListType.X
            v.memset(ones_mat[:], 1.0).then_inc(consts, 1)
            v.tensor_tensor(gate_bias[:], w.wide("bih", 0, 2), w.wide("bhh", 0, 2), ALU.add).then_inc(consts, 1)
            dve.wait_ge(x_in, 16)
            norm_first(nc, dve, mem["x1"][:], x, norm)
            norm_last(nc, dve, x, norm, normed)

            def sdone(ins):
                ins.then_inc(*scale_step.add())

            def ssettled():
                dve.wait_ge(scale_step.sem, scale_step.value)

            dve.wait_ge(act2, WINDOWS)
            sdone(v.tensor_reduce(reach[:, 0:1], h[:], AX, ALU.max))
            sdone(v.tensor_reduce(reach[:, 1:2], h[:], AX, ALU.min))
            ssettled()
            sdone(v.tensor_scalar(reach[:, 2:3], reach[:, 1:2], -1.0, 1.0, ALU.mult, ALU.max))
            ssettled()
            sdone(v.tensor_tensor(reach[:, 3:4], reach[:, 0:1], reach[:, 2:3], ALU.max))
            assert scale_step.value == REACH_STEP
            dve.wait_ge(scale_turned, 3)
            sdone(v.tensor_reduce(top[:, 0:1], psum[0:1, SPARE, 0:P], AX, ALU.max))
            assert scale_step.value == TOP_STEP
            sdone(v.tensor_reduce(bound[:, 0:4], psum[:, R, :].rearrange("p (t f) -> p t f", f=FEAT), AX, ALU.max))
            sdone(v.tensor_reduce(bound[:, 4:5], psum[:, Z, :FEAT], AX, ALU.max))
            ssettled()
            dve.wait_ge(scale_turned, 4)
            sdone(v.tensor_scalar(bound[:], bound[:], psum[:, SPARE, 0:1], None, ALU.mult))
            ssettled()
            sdone(v.tensor_scalar(bound[:], bound[:], 1e-30, 1e36, ALU.max, ALU.min))
            ssettled()
            sdone(v.tensor_scalar(exponent[:], bound[:].bitcast(I32), 0x7F800000, None, ALU.bitwise_and))
            ssettled()
            sdone(v.tensor_scalar(scale[:], exponent[:], -1.0, float(266 << 23), ALU.mult, ALU.add))
            sdone(v.tensor_scalar(unscale[:], exponent[:], float((12 - COUNT_UNIT_BITS) << 23), None, ALU.subtract))
            ssettled()
            for t in range(STEPS):
                sdone(v.tensor_scalar(conv[:, t, :], w("conv", t), scale[:, t:t + 1].bitcast(F32), None, ALU.mult))
            assert scale_step.value == SCALE_STEPS

            def m_low(to, tile, n, g):
                dve.wait_ge(high_done, g + 1)
                v.tensor_tensor(to[:, tile, 1, :], psum[:, M, :n * P].rearrange("p (k f) -> p k f", f=FEAT),
                                to[:, tile, 0, :], ALU.subtract).then_inc(low_done, 1)

            for g, tiles in enumerate(groups()):
                m_low(parts[0], slice(tiles[0], tiles[-1] + 1), len(tiles), g)

            def cell(t, n, width):
                g = n + t * WINDOWS
                hw = h[:, at(n, width)]
                dve.wait_ge(gates_acted, g * 2 + 2)
                v.scalar_tensor_tensor(out=diff[:, :width], in0=psum[:, HN, :width], scalar=w("bhh", 2),
                                       in1=gate_r[:, :width], op0=ALU.add, op1=ALU.mult).then_inc(cand_step, 1)
                dve.wait_ge(cand_step, g * 3 + 1)
                v.tensor_tensor(diff[:, :width], diff[:, :width], psum[:, IN, :width], ALU.add).then_inc(cand_pre, 1)
                dve.wait_ge(cand_done, g + 1)
                v.tensor_tensor(diff[:, :width], hw, new[:, :width], ALU.subtract).then_inc(cand_step, 1)
                dve.wait_ge(cand_step, g * 3 + 2)
                v.tensor_tensor(diff[:, :width], diff[:, :width], gate_z[:, :width], ALU.mult).then_inc(cand_step, 1)
                dve.wait_ge(cand_step, g * 3 + 3)
                if later(t, n):
                    dve.wait_ge(h_copied, g)
                    dve.wait_ge(m_done, g + G if t < STEPS - 1 else STEPS * G)
                v.tensor_tensor(fresh[:, :width], diff[:, :width], new[:, :width], ALU.add).then_inc(h_done, 1)

            def low_part(t, n, width):
                if t < STEPS - 1:
                    m_low(parts[(t + 1) % 2], bass.ds(n * 4, width // P), width // P, n + (t + 1) * WINDOWS)

            def first(t):
                if t:
                    cell(t - 1, FULL_WINDOWS, LAST)
                    low_part(t - 1, FULL_WINDOWS, LAST)

            def body(t, n, width):
                cell(t, n - 1, WIN)
                low_part(t, n - 1, WIN)

            steps_of(dve, first, body)


def decode_and_table(nc, mem, dram):
    SLOTS = 4
    with ExitStack() as ctx:
        def sb(name, shape, dt):
            return ctx.enter_context(nc.sbuf_tensor(name, shape, dt))

        def sem(name):
            return ctx.enter_context(nc.semaphore(name))

        hidden = sb("decoder_hidden", [P, WIN], F32)
        decoded = sb("decoded", [P, 2, WIN], F32)
        y = sb("second_norm", [P, 2, 4, FEAT], F32)
        stats = sb("row_stats", [P, 2, 4, 6], F32)
        moments = sb("row_moments", [P, 2, 4, 2], F32)
        std = sb("row_std", [P, 2, 4], F32)
        rstd = sb("row_rstd", [P, 2, 4], F32)
        eps = sb("second_eps", [P, 1], F32)
        table = sb("table_rows", [P, SLOTS, RELS * FEAT], F32)
        rel_bias = sb("relation_bias", [P, (RELS + 1) * FEAT], F32)
        bias_in, eps_set = sem("relation_bias_in"), sem("second_eps_set")
        h_relu = sem("h_relu")
        pre1, act1, pre2, act2 = sem("dec_pre1"), sem("dec_act1"), sem("dec_pre2"), sem("dec_act2")
        back, added = sem("turned_back"), sem("residual_added")
        norm_step = Count(sem("second_norm_step"))
        rooted, normed, turned, lifted = sem("second_rooted"), sem("y_normed"), sem("y_turned"), sem("y_lifted")
        rows_done, rows_biased, self_biased = sem("rows_done"), sem("rows_biased"), sem("self_biased")
        rows_out = [sem(f"rows_out_{n}") for n in range(SLOTS)]
        psum, ident, h, w = mem["psum"], mem["ident"], mem["h"], mem["weight"]
        x1, base = mem["x1"], mem["base"]
        wins = [(n * WIN, WIN) for n in range(FULL_WINDOWS)] + [(FULL_WINDOWS * WIN, LAST)]
        HALF = RELS * FEAT // 2
        DEC, TURN, BACK, SELF = range(4)
        varied = {}

        def tiles_of(n):
            return wins[n][1] // P if 0 <= n < WINDOWS else 0

        block = ctx.enter_context(nc.Block())

        @block.vector
        def _(dve):
            v = nc.vector

            def done(ins):
                ins.then_inc(*norm_step.add())

            def settled():
                dve.wait_ge(norm_step.sem, norm_step.value)

            def bias_tile(n, q):
                if q >= tiles_of(n):
                    return
                k = 4 * n + q
                dve.wait_ge(rows_done, k + 1)
                if k >= SLOTS:
                    dve.wait_ge(rows_out[k % SLOTS], 16 * (k // SLOTS))
                for half in range(2):
                    v.tensor_tensor(table[:, k % SLOTS, half * HALF:(half + 1) * HALF], psum[:, 4 + 2 * (k % 2) + half, :],
                                    rel_bias[:, half * HALF:(half + 1) * HALF], ALU.add).then_inc(rows_biased, 1)

            v.memset(eps[:], 1e-5).then_inc(eps_set, 1)
            dve.wait_ge(bias_in, 16)
            for n in range(WINDOWS + 2):
                for q in range(3):
                    bias_tile(n - 2, q)
                T, slot = tiles_of(n), n % 2
                if T:
                    rows = x1[:, 4 * n:4 * n + T, :]
                    dve.wait_ge(back, n + 1)
                    v.tensor_tensor(rows, rows, psum[:, BACK, :T * P].rearrange("p (k f) -> p k f", f=FEAT), ALU.add).then_inc(added, 1)
                    dve.wait_ge(added, n + 1)
                    for i in range(T):
                        done(v.bn_stats(stats[:, slot, i, :], rows[:, i, :]))
                    settled()
                    for i in range(T):
                        done(v.bn_aggr(moments[:, slot, i, :], stats[:, slot, i, :]))
                    varied[n] = norm_step.value
                bias_tile(n - 2, 3)
                S = tiles_of(n - 2)
                if S:
                    k = 4 * (n - 2)
                    dve.wait_ge(rows_done, k + S)
                    v.tensor_tensor(base[:, k:k + S, :], psum[:, SELF, :S * P].rearrange("p (k f) -> p k f", f=FEAT),
                                    rel_bias[:, 2 * HALF:].unsqueeze(1).broadcast_to([P, S, FEAT]), ALU.add).then_inc(self_biased, 1)
                if T:
                    dve.wait_ge(rooted, n + 1)
                    done(v.reciprocal(rstd[:, slot, :T], std[:, slot, :T]))
                    settled()
                    if n >= 2:
                        dve.wait_ge(turned, n - 1)
                    for i in range(T):
                        last = v.tensor_scalar(y[:, slot, i, :], rows[:, i, :], moments[:, slot, i, 0:1], rstd[:, slot, i:i + 1],
                                               ALU.subtract, ALU.mult)
                        last.then_inc(normed, 1)

        @block.sync
        def _(sp):
            sp.dma_start(rel_bias[:], dram["rel_bias"].broadcast_to([P, (RELS + 1) * FEAT])).then_inc(bias_in, 16)
            rows = dram["table"].rearrange("(k p r) f -> k p (r f)", p=P, r=RELS)
            for k in range(TILES):
                sp.wait_ge(rows_biased, 2 * k + 2)
                sp.dma_start(rows[k], table[:, k % SLOTS, :]).then_inc(rows_out[k % SLOTS], 16)
            for slot in range(SLOTS):
                sp.wait_ge(rows_out[slot], 16 * len(range(slot, TILES, SLOTS)))

        @block.tensor
        def _(pe):
            mm = nc.tensor.matmul

            def table_tile(n, q):
                if q >= tiles_of(n):
                    return
                k = 4 * n + q
                lhs = h[:, k * P:(k + 1) * P]
                pe.wait_ge(lifted, n + 1)
                if k >= 2:
                    pe.wait_ge(rows_biased, 2 * (k - 1))
                if q == 0 and n:
                    pe.wait_ge(self_biased, n)
                for half in range(2):
                    mm(psum[:, 4 + 2 * (k % 2) + half, :], lhs, w.wide("rel", half * HALF, HALF), start=True, stop=True)
                mm(psum[:, SELF, q * P:(q + 1) * P], lhs, w.wide("rel", 2 * HALF, FEAT), start=True, stop=True).then_inc(rows_done, 1)

            for n in range(WINDOWS + 2):
                at, width = wins[n] if n < WINDOWS else (0, 0)
                if n < WINDOWS:
                    pe.wait_ge(h_relu, n + 1)
                    if n:
                        pe.wait_ge(act2, n)
                    mm(psum[:, DEC, :width], w("dec_w1"), h[:, at:at + width], start=True, stop=True).then_inc(pre1, 1)
                table_tile(n - 2, 0)
                table_tile(n - 2, 1)
                if n < WINDOWS:
                    pe.wait_ge(act1, n + 1)
                    mm(psum[:, DEC, :width], w("dec_w2"), hidden[:, :width], start=True, stop=True).then_inc(pre2, 1)
                table_tile(n - 2, 2)
                if n < WINDOWS:
                    pe.wait_ge(act2, n + 1)
                    if n:
                        pe.wait_ge(added, n)
                    for i in range(width // P):
                        last = nc.tensor.transpose(psum[:, BACK, i * P:(i + 1) * P], decoded[:, n % 2, i * P:(i + 1) * P], ident[:])
                    last.then_inc(back, 1)
                table_tile(n - 2, 3)
                if tiles_of(n - 1):
                    pe.wait_ge(normed, min(4 * n, TILES))
                    if n >= 2:
                        pe.wait_ge(lifted, n - 1)
                    for i in range(tiles_of(n - 1)):
                        last = nc.tensor.transpose(psum[:, TURN, i * P:(i + 1) * P], y[:, (n - 1) % 2, i, :], ident[:])
                    last.then_inc(turned, 1)

        @block.scalar
        def _(act):
            A = nc.scalar.activation
            act.wait_ge(eps_set, 1)
            for n in range(WINDOWS + 2):
                at, width = wins[n] if n < WINDOWS else (0, 0)
                if n < WINDOWS:
                    A(h[:, at:at + width], h[:, at:at + width], ACT.Relu).then_inc(h_relu, 1)
                if n >= 2:
                    at2, width2 = wins[n - 2]
                    act.wait_ge(turned, n - 1)
                    A(h[:, at2:at2 + width2], psum[:, TURN, :width2], ACT.Relu).then_inc(lifted, 1)
                if n < WINDOWS:
                    act.wait_ge(pre1, n + 1)
                    A(hidden[:, :width], psum[:, DEC, :width], ACT.Relu, bias=w("dec_b1")).then_inc(act1, 1)
                    act.wait_ge(pre2, n + 1)
                    if n >= 2:
                        act.wait_ge(back, n - 1)
                    A(decoded[:, n % 2, :width], psum[:, DEC, :width], ACT.Sigmoid, bias=w("dec_b2")).then_inc(act2, 1)
                    act.wait_ge(norm_step.sem, varied[n])
                    A(std[:, n % 2, :width // P], moments[:, n % 2, :width // P, 1], ACT.Sqrt, bias=eps[:, 0:1]).then_inc(rooted, 1)


def running_maximum(nc, mem, dram):
    with ExitStack() as ctx:
        def sb(name, shape, dt):
            return ctx.enter_context(nc.sbuf_tensor(name, shape, dt))

        def sem(name):
            return ctx.enter_context(nc.semaphore(name))

        index_slots = sb("table_index_slots", [P, 2, SLAB], I32)
        cap_slots = sb("cap_slots", [P, 2, SLAB], F32)
        rows = sb("gathered", [P, 2, SLAB, FEAT], F32)
        best = sb("best", [P, 2, SLAB, FEAT], F32)
        zero_row = sb("zero_row", [1, FEAT], F32)
        spread = sb("all_through_spread", [P, P], F32)
        keep = sb("keep", [P, P], F32)
        last = sb("last_turned", [P, P], F32)
        joined = sb("joined", [P, P + 1], F32)
        fixed = sb("run_in_maxima", [P, FEAT], F32)
        copied = sem("table_index_copied")
        slot_read = [sem("gathered_read_0"), sem("gathered_read_1")]
        gathered = [sem("gathered_0"), sem("gathered_1")]
        consts = sem("max_constants")
        masks, step = sem("cap_copied"), sem("max_step")
        written = [sem("best_written_0"), sem("best_written_1")]
        zero_out = sem("zero_row_out")
        fix_read, fix_written = sem("run_in_read"), sem("run_in_written")
        join_step, join_turned = sem("join_step"), sem("join_turned")
        psum, ident = mem["psum"], mem["ident"]
        CONSTS, JOINED = 5, 6

        block = ctx.enter_context(nc.Block())

        @block.gpsimd
        def _(pool):
            held = WaitHolder(nc, ctx, pool, "gather_turns")

            def gather(pair, slot, again):
                if again:
                    pool.wait_ge(slot_read[slot], pair)
                nc.gpsimd.tensor_copy(index_slots[:, slot, :],
                                      mem["table_index"][:, bass.ds(pair * (2 * SLAB) + slot * SLAB, SLAB)]).then_inc(copied, 1)
                pool.wait_ge(copied, pair * 2 + (slot + 1))
                held.take()
                for j in range(SLAB):
                    nc.gpsimd.indirect_dma_start(
                        out=rows[:, slot, j, :], out_offset=None, in_=dram["table"],
                        in_offset=bass.IndirectOffsetOnAxis(ap=index_slots[:, slot, j:j + 1], axis=0)).then_inc(gathered[slot], 16)

            for slot in range(2):
                gather(0, slot, False)
            with pool.Fori(1, SLABS // 2) as pair:
                for slot in range(2):
                    gather(pair, slot, True)
            for slot in range(2):
                pool.wait_ge(written[slot], 16 * (SLABS // 2))
            pool.wait_ge(consts, CONSTS)
            where = bass.IndirectOffsetOnAxis(ap=mem["run_in_end"][:, 0:1], axis=0)
            nc.gpsimd.indirect_dma_start(out=fixed[:], out_offset=None, in_=dram["maxima"], in_offset=where,
                                         bounds_check=NO_EDGE_ROW, oob_is_err=False).then_inc(fix_read, 16)
            pool.wait_ge(join_step, JOINED)
            nc.gpsimd.indirect_dma_start(out=dram["maxima"], out_offset=where, in_=fixed[:], in_offset=None,
                                         bounds_check=NO_EDGE_ROW, oob_is_err=False).then_inc(fix_written, 16)
            pool.wait_ge(fix_written, 16)

        @block.vector
        def _(dve):
            v = nc.vector
            v.memset(best[:, 1, SLAB - 1, :], LOWEST).then_inc(consts, 1)
            v.memset(joined[:, 0:1], LOWEST).then_inc(consts, 1)
            v.memset(zero_row[:], 0.0).then_inc(consts, 1)
            v.memset(spread[:], 1.0).then_inc(consts, 1)
            v.memset(fixed[:], 0.0).then_inc(consts, 1)
            dve.wait_ge(consts, CONSTS)

            def maxima(pair, slot, again):
                first = pair * (2 * SLAB) + slot * SLAB
                v.tensor_copy(cap_slots[:, slot, :], mem["cap"][:, bass.ds(first, SLAB)]).then_inc(masks, 1)
                dve.wait_ge(masks, pair * 2 + (slot + 1))
                dve.wait_ge(gathered[slot], pair * (16 * SLAB) + 16 * SLAB)
                if again:
                    dve.wait_ge(written[slot], pair * 16)
                for j in range(SLAB):
                    before = best[:, slot, j - 1, :] if j else best[:, 1 - slot, SLAB - 1, :]
                    if again or slot or j:
                        dve.wait_ge(step, first + j)
                    v.scalar_tensor_tensor(out=best[:, slot, j, :], in0=before, scalar=cap_slots[:, slot, j:j + 1],
                                           in1=rows[:, slot, j, :], op0=ALU.min, op1=ALU.max).then_inc(step, 1)
                dve.wait_ge(step, first + SLAB)
                dve.sem_inc(slot_read[slot], 1)

            for slot in range(2):
                maxima(0, slot, False)
            with dve.Fori(1, SLABS // 2) as pair:
                for slot in range(2):
                    maxima(pair, slot, True)
            v.tensor_scalar(spread[:], spread[:], mem["all_through"][:, 0:1], None, ALU.mult).then_inc(join_step, 1)
            dve.wait_ge(join_turned, 2)
            v.tensor_scalar(keep[:], psum[:, 0, 0:P], -2.0, 1.0, ALU.mult, ALU.add).then_inc(join_step, 1)
            v.tensor_copy(last[:], psum[:, 1, 0:P]).then_inc(join_step, 1)
            dve.wait_ge(join_step, 3)
            v.tensor_scalar(keep[:], keep[:], LOWEST, None, ALU.mult).then_inc(join_step, 1)
            dve.wait_ge(join_step, 4)
            v.tensor_tensor_scan(joined[:, 1:P + 1], keep[:], last[:], LOWEST, ALU.min, ALU.max).then_inc(join_step, 1)
            dve.wait_ge(join_turned, 3)
            dve.wait_ge(fix_read, 16)
            v.tensor_tensor(fixed[:], fixed[:], psum[:, 2, 0:FEAT], ALU.max).then_inc(join_step, 1)

        @block.tensor
        def _(pe):
            pe.wait_ge(join_step, 1)
            pe.wait_ge(step, PER)
            nc.tensor.transpose(psum[:, 0, 0:P], spread[:], ident[:]).then_inc(join_turned, 1)
            nc.tensor.transpose(psum[:, 1, 0:P], best[:, 1, SLAB - 1, :], ident[:]).then_inc(join_turned, 1)
            pe.wait_ge(join_step, 5)
            nc.tensor.transpose(psum[:, 2, 0:FEAT], joined[:, 0:P], ident[:]).then_inc(join_turned, 1)

        @block.sync
        def _(sp):
            sp.wait_ge(consts, CONSTS)
            sp.dma_start(dram["maxima"][NO_EDGE_ROW:NO_EDGE_ROW + 1, :], zero_row[:]).then_inc(zero_out, 16)
            maxima = dram["maxima"][0:P * PER, :].rearrange("(p s c) f -> p s (c f)", p=P, s=SLABS)
            with sp.Fori(0, SLABS // 2) as pair:
                for slot in range(2):
                    sp.wait_ge(step, pair * (2 * SLAB) + (slot + 1) * SLAB)
                    sp.dma_start(maxima[:, bass.ds(pair * 2 + slot, 1), :].rearrange("p s c -> p (s c)"),
                                 best[:, slot].rearrange("p c f -> p (c f)")).then_inc(written[slot], 16)
            sp.wait_ge(zero_out, 16)
            for slot in range(2):
                sp.wait_ge(written[slot], 16 * (SLABS // 2))


def finish(nc, mem, dram):
    BATCH = 7
    BATCHES = TILES // BATCH
    with ExitStack() as ctx:
        def sb(name, shape, dt):
            return ctx.enter_context(nc.sbuf_tensor(name, shape, dt))

        def sem(name):
            return ctx.enter_context(nc.semaphore(name))

        maxima = sb("node_maxima", [P, TILES, FEAT], F32)
        gathered = [sem(f"maxima_gathered_{n}") for n in range(BATCHES)]
        step, out_done = Count(sem("finish_step")), sem("out_done")
        x1, base = mem["x1"], mem["base"]

        block = ctx.enter_context(nc.Block())

        @block.gpsimd
        def _(pool):
            for k in range(TILES):
                nc.gpsimd.indirect_dma_start(
                    out=maxima[:, k, :], out_offset=None, in_=dram["maxima"],
                    in_offset=bass.IndirectOffsetOnAxis(ap=mem["node_place"][:, k:k + 1], axis=0)).then_inc(gathered[k // BATCH], 16)

        @block.vector
        def _(dve):
            v = nc.vector
            for b in range(BATCHES):
                tiles = slice(b * BATCH, (b + 1) * BATCH)
                dve.wait_ge(gathered[b], 16 * BATCH)
                for ins in (lambda m: v.tensor_tensor(m, m, base[:, tiles, :], ALU.add),
                            lambda m: v.tensor_scalar(m, m, 0.0, None, ALU.max),
                            lambda m: v.tensor_tensor(m, m, x1[:, tiles, :], ALU.add)):
                    ins(maxima[:, tiles, :]).then_inc(*step.add())
                    dve.wait_ge(step.sem, step.value)

        @block.sync
        def _(sp):
            out = dram["out"].rearrange("(k p) f -> p k f", p=P)
            for b in range(BATCHES):
                tiles = slice(b * BATCH, (b + 1) * BATCH)
                sp.wait_ge(step.sem, 3 * (b + 1))
                sp.dma_start(out[:, tiles, :], maxima[:, tiles, :]).then_inc(out_done, 16)
            sp.wait_ge(out_done, 16 * BATCHES)


class Weights:

    def __init__(self, packed):
        self.packed = packed

    def __call__(self, name, n=0):
        at, width = PACK[name]
        one = 1 if name in ("enc_b1", "enc_b2", "bih", "bhh", "dec_b1", "dec_b2") else FEAT
        return self.packed[:, at + n * one:at + (n + 1) * one]

    def wide(self, name, first, width):
        at = PACK[name][0] + first
        return self.packed[:, at:at + width]


def build(nc, dram):
    def scratch(name, shape, dt):
        dram[name] = nc.dram_tensor(f"scratch_{name}", shape, dt, kind="Internal").ap()

    for half in range(HALVES):
        scratch(f"keys_{half}", (2 + SORTED,), I32)
    scratch("keys", (2 + HALVES * SORTED,), I32)
    scratch("counts", (COUNT_CELLS + SPARE_CELLS, 1), F16)
    scratch("table", (ROWS * RELS, FEAT), F32)
    scratch("maxima", (NO_EDGE_ROW + 1, FEAT), F32)
    with ExitStack() as ctx:
        def sb(name, shape, dt):
            return ctx.enter_context(nc.sbuf_tensor(name, shape, dt))

        mem = {"psum": ctx.enter_context(nc.psum_tensor("banks", [P, 8, WIN], F32)),
               "ident": sb("identity", [P, P], F32), "packed": sb("packed", [P, PACKED], F32)}
        mem["weight"] = Weights(mem["packed"])
        mem["guard"], mem["needed"] = sb("guard", [1, 1], I32), sb("landed_needed", [1, 2, WINDOWS], I32)
        mem["table_index"] = sb("table_index", [P, PER], I32)
        mem["cap"] = sb("cap", [P, PER], F32)
        mem["all_through"] = sb("all_through", [P, 1], F32)
        mem["h"] = sb("h", [P, ROWS], F32)
        mem["run_in_end"] = sb("run_in_end", [P, 1], I32)
        mem["node_place"] = sb("node_place", [P, TILES], I32)

        shares = (15, 4, 6, HALF_SLABS - 25)

        def share(n):
            def scatter(ctx, pool):
                scatter_slabs(nc, ctx, pool, mem, dram, 0, sum(shares[:n]), shares[n])
            return scatter

        mem["x1"] = sb("x1", [P, TILES, FEAT], F32)
        with ExitStack() as cells:
            first_cells = cells.enter_context(ExitStack())
            mem["cells"] = [None, cells.enter_context(nc.sbuf_tensor("cells_1", [P, HOLDING, BLOCK_WORDS], I32))]
            mem["cells"][0] = first_cells.enter_context(nc.sbuf_tensor("cells_0", [P, HOLDING, BLOCK_WORDS], I32))
            with ExitStack() as fill:
                mem["zeros"] = fill.enter_context(nc.sbuf_tensor("zeros", [P, TILES * WIN // 2], F32))
                mem["zero_filled"] = fill.enter_context(nc.semaphore("zero_filled"))
                sort_half(nc, mem, dram, 0)
                work_out_cells(nc, mem, dram, 0)
            mem["zeros"] = mem["zero_filled"] = None
            sort_half(nc, mem, dram, 1, share(0))
            work_out_cells(nc, mem, dram, 1, share(1))
            join_halves(nc, mem, dram, share(2))
            describe_edges(nc, mem, dram, share(3))
            first_cells.close()
            propagate(nc, mem, dram)
        mem["base"] = sb("self_part", [P, TILES, FEAT], F32)
        decode_and_table(nc, mem, dram)
        running_maximum(nc, mem, dram)
        finish(nc, mem, dram)


def kernel(**inputs):
    import concourse.bacc as bacc
    from concourse.bass_utils import run_bass_kernel_spmd as run

    def get(name):
        return np.asarray(inputs[name])

    def padded(values, fill):
        out = np.full((HALVES, SORTED), fill, np.int32)
        out[:, :HALF_EDGES] = values.reshape(HALVES, HALF_EDGES)
        return out.reshape(HALVES, P, COLS)

    x = np.zeros((ROWS, FEAT), np.float32)
    x[:NODES] = get("x")
    gnn = "L0_gnn_"
    columns = [get(gnn + "enc_w1").T, get(gnn + "enc_w2").T, get(gnn + "gru_wih").T, get(gnn + "gru_whh").T,
               get(gnn + "dec_w1").T, get(gnn + "dec_w2").T,
               get(gnn + "conv_w").transpose(1, 0, 2).reshape(FEAT, -1),
               get("L1_gnn_weight").transpose(1, 0, 2).reshape(FEAT, -1),
               get(gnn + "enc_b1").reshape(1, FEAT).T, get(gnn + "enc_b2").reshape(1, FEAT).T,
               get(gnn + "gru_bih").reshape(3, FEAT).T, get(gnn + "gru_bhh").reshape(3, FEAT).T,
               get(gnn + "dec_b1").reshape(1, FEAT).T, get(gnn + "dec_b2").reshape(1, FEAT).T]
    arrays = {"x": x, "dst": padded(get("dst"), PAD_NODE), "src": padded(get("src"), 0),
              "edge_type": padded(get("edge_type_8"), 0),
              "packed": np.ascontiguousarray(np.concatenate(columns, axis=1)),
              "rel_bias": np.ascontiguousarray(get("L1_gnn_bias").reshape(1, -1))}
    nc = bacc.Bacc("TRN2", target_bir_lowering=False, num_devices=1)
    dram = {name: nc.dram_tensor(f"in_{name}", a.shape, mybir.dt.from_np(a.dtype), kind="ExternalInput").ap()
            for name, a in arrays.items()}
    dram["out"] = nc.dram_tensor("out_0", (ROWS, FEAT), F32, kind="ExternalOutput").ap()
    build(nc, dram)
    result = run(nc, [{f"in_{name}": a for name, a in arrays.items()}], core_ids=[0]).results[0]["out_0"]
    return result[:NODES]
```
